# Optimizing a Trainium2 kernel written in Bass

```python
import numpy as np
import jax
import jax.numpy as jnp

def _softmax(x, axis=-1):
    return jax.nn.softmax(x, axis=axis)

def _gelu(x):
    return jax.nn.gelu(x, approximate=True)

def _silu(x):
    return jax.nn.silu(x)

def _sigmoid(x):
    return jax.nn.sigmoid(x)

def _layernorm(x, axis=-1, eps=1e-05):
    m = jnp.mean(x, axis=axis, keepdims=True)
    v = jnp.var(x, axis=axis, keepdims=True)
    return (x - m) / jnp.sqrt(v + eps)

def _scatter_add(tgt, idx, src, axis=0):
    return tgt.at[idx].add(src)

def _segment_sum(src, seg, n):
    return jax.ops.segment_sum(src, seg, n)
kernel_name = 'mk_decoder_preln_d1_seqx_r4_0d1588'

def setup_inputs(seed: int=0):
    np.random.seed(seed)
    _w = jnp.asarray

    def _rec_inputs():
        import jax
        import jax.numpy as jnp
        _rk = jax.random.key(seed)
        x = -0.0002928 + 1 * jax.random.normal(jax.random.fold_in(_rk, 1), (4, 512, 256), jnp.float32)
        _lenS = 512 - jax.random.randint(jax.random.fold_in(_rk, 7), (4,), 0, max(1, 512 // 4) + 1, jnp.int32)
        _lenS2 = 512 - jax.random.randint(jax.random.fold_in(_rk, 8), (4,), 0, max(1, 512 // 4) + 1, jnp.int32)
        _ctx_1024P = jax.random.normal(jax.random.fold_in(_rk, 11), (4, 16, 256), jnp.float32)
        _ctx_1024c = jax.random.dirichlet(jax.random.fold_in(_rk, 511), 0.3 * jnp.ones((16,), jnp.float32), (4, 512))
        _ctx_1024t = jnp.einsum('bsk,bkd->bsd', _ctx_1024c, _ctx_1024P)
        _ctx_1024t = _ctx_1024t * jax.lax.rsqrt(jnp.mean(jnp.square(_ctx_1024t)) + 1e-12) * 0.953939
        ctx_1024 = -1.39393e-06 + 0.999914 * (_ctx_1024t + 0.3 * jax.random.normal(jax.random.fold_in(_rk, 611), (4, 512, 256), jnp.float32))
        fside_Bx1xSxS2_0 = -4.48278e-06 + 1.00019 * jax.random.normal(jax.random.fold_in(_rk, 12), (4, 1, 512, 512), jnp.float32)
        return (x, ctx_1024, fside_Bx1xSxS2_0)
    x, ctx_1024, fside_Bx1xSxS2_0 = _rec_inputs()

    def _L0_attn_setup():
        import math
        import jax, jax.numpy as jnp
        import numpy as np
        DIM = 256
        N_HEADS = 16
        HEAD_DIM = DIM // N_HEADS
        SEQ_LEN = 512
        BASE = 10000.0
        EPS = 1e-05

        def rope_cache(seq_len, dim):
            pos = jnp.arange(seq_len, dtype=jnp.float32)[:, None]
            di = jnp.arange(0, dim, 2, dtype=jnp.float32) / dim
            theta = pos * jnp.exp(-di * math.log(BASE))
            cos = jnp.repeat(jnp.cos(theta), 2, axis=1)
            sin = jnp.repeat(jnp.sin(theta), 2, axis=1)
            return (cos, sin)

        def rotate_half(x):
            x1 = x[..., ::2]
            x2 = x[..., 1::2]
            return jnp.concatenate((-x2, x1), axis=-1)

        def layernorm(x, gamma, beta):
            mu = jnp.mean(x, axis=-1, keepdims=True)
            var = jnp.var(x, axis=-1, keepdims=True)
            return (x - mu) * jax.lax.rsqrt(var + EPS) * gamma + beta
        key = jax.random.key(seed)
        ks = jax.random.split(key, 7)
        s = 1.0 / math.sqrt(DIM)
        return {'x': jax.random.normal(ks[0], (2, SEQ_LEN, DIM), dtype=jnp.float32), 'Wq': jax.random.normal(ks[1], (DIM, DIM), dtype=jnp.float32) * s, 'Wk': jax.random.normal(ks[2], (DIM, DIM), dtype=jnp.float32) * s, 'Wv': jax.random.normal(ks[3], (DIM, DIM), dtype=jnp.float32) * s, 'q_gamma': jnp.ones((HEAD_DIM,), jnp.float32), 'q_beta': jnp.zeros((HEAD_DIM,), jnp.float32), 'k_gamma': jnp.ones((HEAD_DIM,), jnp.float32), 'k_beta': jnp.zeros((HEAD_DIM,), jnp.float32), 'Wo': jax.random.normal(ks[4], (DIM, DIM), dtype=jnp.float32) * s, 'bo': jnp.zeros((DIM,), jnp.float32)}
    _L0_attn_all = _L0_attn_setup()
    _L0_attn_in = {k: v for k, v in _L0_attn_all.items() if k in ('Wq', 'Wk', 'Wv', 'q_gamma', 'q_beta', 'k_gamma', 'k_beta', 'Wo', 'bo')}
    del _L0_attn_all

    def _L0_xattn_setup():
        import jax, jax.numpy as jnp
        import numpy as np
        B, S, D_FF = (2, 512, 256)
        NUM_HEADS, D_KV = (16, 64)
        INNER = NUM_HEADS * D_KV
        key = jax.random.key(seed)
        ks = jax.random.split(key, 8)
        scale = 1.0 / np.sqrt(D_FF)
        return {'q': jax.random.normal(ks[0], (B, S, D_FF), jnp.float32), 'k': jax.random.normal(ks[1], (B, S, D_FF), jnp.float32), 'v': jax.random.normal(ks[2], (B, S, D_FF), jnp.float32), 'attn_mask': jax.random.normal(ks[3], (B, 1, S, S), jnp.float32), 'Wq': jax.random.normal(ks[4], (INNER, D_FF), jnp.float32) * scale, 'Wk': jax.random.normal(ks[5], (INNER, D_FF), jnp.float32) * scale, 'Wv': jax.random.normal(ks[6], (INNER, D_FF), jnp.float32) * scale, 'Wo': jax.random.normal(ks[7], (D_FF, INNER), jnp.float32) * scale, 'num_heads': NUM_HEADS}
    _L0_xattn_all = _L0_xattn_setup()
    _L0_xattn_in = {k: v for k, v in _L0_xattn_all.items() if k in ('Wq', 'Wk', 'Wv', 'Wo')}
    del _L0_xattn_all

    def _L0_ffn_setup():
        import jax, jax.numpy as jnp
        import numpy as np
        FF_DIM = 512
        TOP_K = 2
        key = jax.random.key(seed)
        k1, k2, k3, k4 = jax.random.split(key, 4)
        B, S, D, E, F = (2, 512, 256, 8, FF_DIM)
        std = 0.006
        return {'x': jax.random.normal(k1, (B, S, D), dtype=jnp.float32), 'gate_w': jax.random.normal(k2, (D, E), dtype=jnp.float32) * 0.02, 'gate_up_w': jax.random.normal(k3, (E, D, 2 * F), dtype=jnp.float32) * std, 'down_w': jax.random.normal(k4, (E, F, D), dtype=jnp.float32) * std}
    _L0_ffn_all = _L0_ffn_setup()
    _L0_ffn_in = {k: v for k, v in _L0_ffn_all.items() if k in ('gate_w', 'gate_up_w', 'down_w')}
    del _L0_ffn_all
    return {'x': x, 'ctx_1024': ctx_1024, 'fside_Bx1xSxS2_0': fside_Bx1xSxS2_0, 'L0_attn_Wq': _L0_attn_in['Wq'], 'L0_attn_Wk': _L0_attn_in['Wk'], 'L0_attn_Wv': _L0_attn_in['Wv'], 'L0_attn_q_gamma': _L0_attn_in['q_gamma'], 'L0_attn_q_beta': _L0_attn_in['q_beta'], 'L0_attn_k_gamma': _L0_attn_in['k_gamma'], 'L0_attn_k_beta': _L0_attn_in['k_beta'], 'L0_attn_Wo': _L0_attn_in['Wo'], 'L0_attn_bo': _L0_attn_in['bo'], 'L0_xattn_Wq': _L0_xattn_in['Wq'], 'L0_xattn_Wk': _L0_xattn_in['Wk'], 'L0_xattn_Wv': _L0_xattn_in['Wv'], 'L0_xattn_Wo': _L0_xattn_in['Wo'], 'L0_ffn_gate_w': _L0_ffn_in['gate_w'], 'L0_ffn_gate_up_w': _L0_ffn_in['gate_up_w'], 'L0_ffn_down_w': _L0_ffn_in['down_w']}

def reference(x, ctx_1024, fside_Bx1xSxS2_0, L0_attn_Wq, L0_attn_Wk, L0_attn_Wv, L0_attn_q_gamma, L0_attn_q_beta, L0_attn_k_gamma, L0_attn_k_beta, L0_attn_Wo, L0_attn_bo, L0_xattn_Wq, L0_xattn_Wk, L0_xattn_Wv, L0_xattn_Wo, L0_ffn_gate_w, L0_ffn_gate_up_w, L0_ffn_down_w):
    import jax
    import jax.numpy as jnp

    def _L0_attn_ref(x, Wq, Wk, Wv, q_gamma, q_beta, k_gamma, k_beta, Wo, bo):
        import math
        import jax, jax.numpy as jnp
        import numpy as np
        DIM = 256
        N_HEADS = 16
        HEAD_DIM = DIM // N_HEADS
        SEQ_LEN = 512
        BASE = 10000.0
        EPS = 1e-05

        def rope_cache(seq_len, dim):
            pos = jnp.arange(seq_len, dtype=jnp.float32)[:, None]
            di = jnp.arange(0, dim, 2, dtype=jnp.float32) / dim
            theta = pos * jnp.exp(-di * math.log(BASE))
            cos = jnp.repeat(jnp.cos(theta), 2, axis=1)
            sin = jnp.repeat(jnp.sin(theta), 2, axis=1)
            return (cos, sin)

        def rotate_half(x):
            x1 = x[..., ::2]
            x2 = x[..., 1::2]
            return jnp.concatenate((-x2, x1), axis=-1)

        def layernorm(x, gamma, beta):
            mu = jnp.mean(x, axis=-1, keepdims=True)
            var = jnp.var(x, axis=-1, keepdims=True)
            return (x - mu) * jax.lax.rsqrt(var + EPS) * gamma + beta
        B, S, D = x.shape
        H, hd = (N_HEADS, HEAD_DIM)
        q = (x @ Wq.T).reshape(B, S, H, hd).transpose(0, 2, 1, 3)
        k = (x @ Wk.T).reshape(B, S, H, hd).transpose(0, 2, 1, 3)
        v = (x @ Wv.T).reshape(B, S, H, hd).transpose(0, 2, 1, 3)
        q = layernorm(q, q_gamma, q_beta)
        k = layernorm(k, k_gamma, k_beta)
        cos, sin = rope_cache(S, hd)
        cos = cos[None, None]
        sin = sin[None, None]
        q = q * cos + rotate_half(q) * sin
        k = k * cos + rotate_half(k) * sin
        scale = 1.0 / math.sqrt(hd)
        scores = scale * jnp.einsum('bhqd,bhkd->bhqk', q, k)
        mask = jnp.tril(jnp.ones((S, S), dtype=bool))
        scores = jnp.where(mask, scores, -jnp.inf)
        attn = jax.nn.softmax(scores, axis=-1)
        out = jnp.einsum('bhqk,bhkd->bhqd', attn, v)
        out = out.transpose(0, 2, 1, 3).reshape(B, S, D)
        return out @ Wo.T + bo

    def _L0_xattn_ref(q, k, v, attn_mask, Wq, Wk, Wv, Wo, num_heads):
        import jax, jax.numpy as jnp
        import numpy as np
        B, S, D_FF = (2, 512, 256)
        NUM_HEADS, D_KV = (16, 64)
        INNER = NUM_HEADS * D_KV
        b, s, _ = q.shape

        def proj_heads(x, W):
            y = jnp.einsum('bsd,ed->bse', x, W)
            return y.reshape(b, s, num_heads, -1).transpose(0, 2, 1, 3)
        qh = proj_heads(q, Wq)
        kh = proj_heads(k, Wk)
        vh = proj_heads(v, Wv)
        scores = jnp.einsum('bhqd,bhkd->bhqk', qh, kh) + attn_mask
        probs = jax.nn.softmax(scores, axis=-1)
        ctx = jnp.einsum('bhqk,bhkd->bhqd', probs, vh)
        ctx = ctx.transpose(0, 2, 1, 3).reshape(b, s, -1)
        return jnp.einsum('bse,de->bsd', ctx, Wo)

    def _L0_ffn_ref(x, gate_w, gate_up_w, down_w):
        import jax, jax.numpy as jnp
        import numpy as np
        FF_DIM = 512
        TOP_K = 2
        B, S, D = x.shape
        E = gate_up_w.shape[0]
        F = down_w.shape[1]
        x_flat = x.reshape(B * S, D)
        router_logits = x_flat @ gate_w
        router_probs = jax.nn.softmax(router_logits, axis=-1)
        top_k_probs, top_k_idx = jax.lax.top_k(router_probs, TOP_K)
        top_k_probs = top_k_probs / jnp.sum(top_k_probs, axis=-1, keepdims=True)
        gate_up = jnp.einsum('nd,edh->enh', x_flat, gate_up_w)
        gate_out = gate_up[..., :F]
        up_out = gate_up[..., F:]
        hidden = jax.nn.silu(gate_out) * up_out
        expert_out = jnp.einsum('enf,efd->end', hidden, down_w)
        out_t = jnp.transpose(expert_out, (1, 0, 2))
        sel = jnp.take_along_axis(out_t, top_k_idx[:, :, None], axis=1)
        output = jnp.sum(sel * top_k_probs[:, :, None], axis=1)
        return output.reshape(B, S, D)
    x = x + _L0_attn_ref(_layernorm(x, axis=-1), L0_attn_Wq, L0_attn_Wk, L0_attn_Wv, L0_attn_q_gamma, L0_attn_q_beta, L0_attn_k_gamma, L0_attn_k_beta, L0_attn_Wo, L0_attn_bo)
    x = x + _L0_xattn_ref(_layernorm(x, axis=-1), ctx_1024, ctx_1024, fside_Bx1xSxS2_0, L0_xattn_Wq, L0_xattn_Wk, L0_xattn_Wv, L0_xattn_Wo, 16)
    x = x + _L0_ffn_ref(_layernorm(x, axis=-1), L0_ffn_gate_w, L0_ffn_gate_up_w, L0_ffn_down_w)
    return x

_drawn_inputs = setup_inputs


def setup_inputs(seed=0):
    import zlib

    import numpy as np

    out = dict(_drawn_inputs(seed))
    spreads = {'L0_attn_q_gamma': (1.0, 0.2),
     'L0_attn_q_beta': (0.0, 0.291),
     'L0_attn_k_gamma': (1.0, 0.2),
     'L0_attn_k_beta': (0.0, 0.385),
     'L0_attn_bo': (0.0, 0.1)}
    factors = {'L0_ffn_gate_w': 8.0, 'L0_ffn_gate_up_w': 8.0, 'L0_ffn_down_w': 8.0}
    for name, (base, spread) in spreads.items():
        noise = np.random.default_rng([zlib.crc32(name.encode()), seed]).standard_normal(out[name].shape)
        drawn = base * np.exp(spread * noise) if base else spread * noise
        out[name] = jnp.asarray(drawn.astype(out[name].dtype))
    for name, factor in factors.items():
        out[name] = (out[name] * factor).astype(out[name].dtype)
    return out
```

```python
import math
from contextlib import ExitStack

import concourse.bass as bass
from concourse import mybir

F32 = mybir.dt.float32
U32 = mybir.dt.uint32
ALU = mybir.AluOpType
ACT = mybir.ActivationFunctionType
AX = mybir.AxisListType

P = 128
EPS = 1e-5
BIG = 3.0e38
MASKED = -1.0e30
TOP = 2


def build(nc, x, ctx_in, fside, wqkv, head_affine, rope, wo1, bo, wq2, wk2, wv2, wo2, gate_w, gate_up_w, down_w, out):
    B, S, D = x.shape
    H = 16
    HD = D // H
    E2 = wq2.shape[1]
    HD2 = E2 // H
    T = S // P
    KD = D // P
    SLOT = 32
    GH = P // SLOT
    G1 = H // GH
    GH2 = P // HD2
    G2 = H // GH2
    NE, _, F2 = gate_up_w.shape
    F = F2 // 2
    FT = F // P
    NT = B * T
    SCALE1 = 1.0 / math.sqrt(HD)

    x_v = x.rearrange("b (t p) d -> b p t d", p=P)
    c_v = ctx_in.rearrange("b (t p) d -> b p t d", p=P)
    m_v = fside.rearrange("b o (t p) k -> b p (o t) k", p=P)
    out_b = out.rearrange("b (t p) d -> b p t d", p=P)
    out_v = out.rearrange("b (t p) d -> p (b t) d", p=P)
    xT_dram = nc.dram_tensor("xT_dram", [B, P, KD, S], F32, kind="Internal").ap()

    with ExitStack() as ctx:
        def sb(name, shape, dt=F32):
            return ctx.enter_context(nc.sbuf_tensor(name, shape, dt))

        bank = ctx.enter_context(nc.psum_tensor("bank", [P, 8, 512], F32))

        comb = sb("comb", [P, NT, NE])
        ident = sb("ident", [P, P])
        half_neg = sb("half_neg", [P, 64 * 2 * 2])
        expert_no = sb("expert_no", [P, NE])

        with ExitStack() as att:
            def sa(name, shape, dt=F32):
                return att.enter_context(nc.sbuf_tensor(name, shape, dt))

            w_qkv = sa("w_qkv", [P, KD, 3 * D])
            w_o1 = sa("w_o1", [P, G1, D])
            w_q2 = sa("w_q2", [P, KD, E2])
            w_k2 = sa("w_k2", [P, KD, E2])
            w_v2 = sa("w_v2", [P, KD, E2])
            w_o2 = sa("w_o2", [P, G2, D])
            w_g = sa("w_g", [P, KD, NE])
            b_o = sa("b_o", [P, D])
            affine = sa("affine", [P, 4, HD])
            cs = sa("cs", [P, T, 2, HD])
            gcos = sa("gcos", [P, T, 2, HD])
            gsin = sa("gsin", [P, T, 2, HD])
            bsum = sa("bsum", [P, T, 2, HD])
            btmp = sa("btmp", [P, T, 2, HD])
            causal = sa("causal", [P, 2 * S])

            xb = sa("xb", [P, T, D])
            cb = sa("cb", [P, T, D])
            mb = sa("mb", [P, T, S])
            xn = sa("xn", [P, T, D])
            xT = sa("xT", [P, KD, S])
            cT = sa("cT", [P, KD, S])
            qkv = sa("qkv", [P, T, 3 * D])
            stat = sa("stat", [P, T, 6])
            mv = sa("mv", [P, T, 2])
            rstd = sa("rstd", [P, T])
            hsum = sa("hsum", [P, T, 2 * H])
            hvar = sa("hvar", [P, T, 2 * H])
            hstd = sa("hstd", [P, T, 2 * H])
            qk_pad = sa("qk_pad", [P, T, 2 * H, SLOT])
            v_pad = sa("v_pad", [P, T, H, SLOT])
            k2T = sa("k2T", [P, G2, S])
            qT = sa("qT", [P, G2, S])
            qk1T = qT[:].rearrange("p (a g) s -> p a g s", a=2)
            o1T, q2T, o2T = qT[:, 0:G1, :], qT, qT
            v2 = sa("v2", [P, T, E2])
            s_sb = sa("s_sb", [P, 3, S])
            p_sb = sa("p_sb", [P, 3, S])
            pT = sa("pT", [P, 2, T, S])
            negmax = sa("negmax", [P, H * T])
            psum_row = sa("psum_row", [P, H * T])
            pinv = sa("pinv", [P, H * T])
            logit = sa("logit", [P, T, NE])
            top = sa("top", [P, T, 8])
            topi = sa("topi", [P, T, 8], U32)
            topf = sa("topf", [P, T, 8])
            ntop = sa("ntop", [P, T])
            ew = sa("ew", [P, T, TOP])
            esum = sa("esum", [P, T])
            pick = sa("pick", [P, T, NE])

            with nc.semaphore("loaded") as loaded, nc.semaphore("pool_set") as pool_set, \
                    nc.semaphore("tab") as tab, nc.Block() as block:
                LOADS = 12

                @block.sync
                def _(sp):
                    sp.dma_start(w_qkv[:], wqkv.rearrange("(k p) n -> p k n", p=P)).then_inc(loaded, 16)
                    sp.dma_start(w_k2[:], wk2.rearrange("(k p) n -> p k n", p=P)).then_inc(loaded, 16)
                    sp.dma_start(w_v2[:], wv2.rearrange("(k p) n -> p k n", p=P)).then_inc(loaded, 16)
                    sp.dma_start(w_q2[:], wq2.rearrange("(k p) n -> p k n", p=P)).then_inc(loaded, 16)
                    sp.dma_start(w_o1[:], wo1.rearrange("(g p) n -> p g n", p=P)).then_inc(loaded, 16)
                    sp.dma_start(w_o2[:], wo2.rearrange("(g p) n -> p g n", p=P)).then_inc(loaded, 16)
                    sp.dma_start(w_g[:], gate_w.rearrange("(k p) n -> p k n", p=P)).then_inc(loaded, 16)
                    sp.dma_start(b_o[:], bo.partition_broadcast(P)).then_inc(loaded, 16)
                    for i in range(2):
                        sp.dma_start(affine[:, 2 * i:2 * i + 2, :].rearrange("p a d -> p (a d)"),
                                     head_affine[2 * i:2 * i + 2, :].rearrange("a d -> (a d)").partition_broadcast(P)
                                     ).then_inc(loaded, 16)
                    for i in range(2):
                        sp.dma_start(cs[:, :, i, :], rope[i].rearrange("(t p) d -> p t d", p=P)).then_inc(loaded, 16)
                    sp.wait_ge(loaded, 16 * LOADS)

                @block.gpsimd
                def _(pool):
                    pool.memset(ident[:], 0.0).then_inc(pool_set, 1)
                    pool.memset(causal[:], 0.0).then_inc(pool_set, 1)
                    pool.memset(half_neg[:], -0.5).then_inc(pool_set, 1)
                    pool.memset(qk_pad[:], 0.0).then_inc(pool_set, 1)
                    pool.memset(v_pad[:], 0.0).then_inc(pool_set, 1)
                    pool.iota(expert_no[:], [[1, NE]], base=0, channel_multiplier=0,
                              allow_small_or_imprecise_dtypes=True).then_inc(pool_set, 1)
                    pool.wait_ge(pool_set, 6)
                    pool.affine_select(out=ident[:], in_=ident[:], compare_op=ALU.not_equal, fill=1.0, base=0,
                                       pattern=[[-1, P]], channel_multiplier=1).then_inc(pool_set, 1)
                    pool.affine_select(out=causal[:], in_=causal[:], compare_op=ALU.is_ge, fill=MASKED, base=S,
                                       pattern=[[-1, 2 * S]], channel_multiplier=1).then_inc(pool_set, 1)
                    pool.wait_ge(pool_set, 8)

                @block.vector
                def _(dve):
                    dve.wait_ge(loaded, 16 * LOADS)
                    HH = HD // 2
                    n = 0
                    for i in range(2):
                        for (dst, src, rotated) in ((gcos, i, False), (gsin, i, True), (bsum, 2 + i, False),
                                                    (btmp, 2 + i, True)):
                            if not rotated:
                                nc.vector.tensor_tensor(dst[:, :, i, :], cs[:, :, 0, :],
                                                        affine[:, src:src + 1, :].to_broadcast([P, T, HD]),
                                                        ALU.mult).then_inc(tab, 1)
                                n += 1
                                continue
                            for half in range(2):
                                nc.vector.tensor_tensor(
                                    dst[:, :, i, half * HH:(half + 1) * HH], cs[:, :, 1, half * HH:(half + 1) * HH],
                                    affine[:, src:src + 1, 1 - half:HD:2].to_broadcast([P, T, HH]),
                                    ALU.mult).then_inc(tab, 1)
                                n += 1
                    dve.wait_ge(tab, n)
                    nc.vector.tensor_tensor(bsum[:], bsum[:], btmp[:], ALU.add).then_inc(tab, 1)
                    dve.wait_ge(tab, n + 1)
            nc.all_engine_barrier(sems_to_clear=range(loaded.num, tab.num + 1))

            def layernorm(dve, pool, src, steps, pool_done, done, first_wait):
                if dve is not None:
                    for t in range(T):
                        first_wait(t)
                        nc.vector.bn_stats(stat[:, t, :], src(t)).then_inc(steps, 1)
                    dve.wait_ge(steps, T)
                    for t in range(T):
                        nc.vector.bn_aggr(mv[:, t, :], stat[:, t, :]).then_inc(steps, 1)
                    dve.wait_ge(steps, 2 * T)
                    nc.vector.tensor_scalar(rstd[:], mv[:, :, 1], EPS, None, ALU.add).then_inc(steps, 1)
                    dve.wait_ge(pool_done, 1)
                    for t in range(T):
                        nc.vector.tensor_scalar(xn[:, t, :], src(t), mv[:, t, 0:1], rstd[:, t:t + 1],
                                                ALU.subtract, ALU.mult).then_inc(done, 1)
                else:
                    pool.wait_ge(steps, 2 * T + 1)
                    nc.gpsimd.tensor_tensor(rstd[:], rstd[:], half_neg[:, 0:T], ALU.pow).then_inc(pool_done, 1)

            with nc.Fori(0, B) as b:
                with nc.semaphore("x_in") as x_in, nc.semaphore("c_in") as c_in, nc.semaphore("m_in") as m_in, \
                        nc.semaphore("steps") as steps, nc.semaphore("root") as root, nc.semaphore("xn_ready") as xn_ready, \
                        nc.semaphore("produced") as produced, nc.semaphore("evacuated") as evacuated, \
                        nc.semaphore("head_steps") as head_steps, nc.semaphore("head_root") as head_root, \
                        nc.semaphore("roped") as roped, nc.semaphore("v_copied") as v_copied, nc.Block() as block:
                    N_CT, N_K2, N_XT, N_QKV, N_V2, N_QK1 = KD, G2, KD, 2 * T, 2 * T, 2 * G1
                    AT_K2 = N_CT
                    AT_XT = AT_K2 + N_K2
                    AT_QKV = AT_XT + N_XT
                    AT_V2 = AT_QKV + N_QKV
                    AT_QK1 = AT_V2 + N_V2

                    @block.sync
                    def _(sp):
                        one = bass.ds(b, 1)
                        sp.dma_start(cb[:], c_v[one].rearrange("a p t d -> p (a t) d")).then_inc(c_in, 16)
                        sp.dma_start(xb[:], x_v[one].rearrange("a p t d -> p (a t) d")).then_inc(x_in, 16)
                        sp.dma_start(mb[:], m_v[one].rearrange("a p t d -> p (a t) d")).then_inc(m_in, 16)
                        sp.wait_ge(m_in, 16)

                    @block.tensor
                    def _(pe):
                        n = 0

                        def free(n):
                            if n >= 8:
                                pe.wait_ge(evacuated, n - 7)

                        pe.wait_ge(c_in, 16)
                        for k in range(KD):
                            for t in range(T):
                                mm = nc.tensor.transpose(bank[:, n % 8, t * P:(t + 1) * P], cb[:, t, k * P:(k + 1) * P], ident[:])
                            mm.then_inc(produced, 1)
                            n += 1
                        pe.wait_ge(evacuated, N_CT)
                        for j in range(G2):
                            free(n)
                            for k in range(KD):
                                mm = nc.tensor.matmul(bank[:, n % 8, :], w_k2[:, k, j * P:(j + 1) * P], cT[:, k, :],
                                                      start=(k == 0), stop=(k == KD - 1))
                            mm.then_inc(produced, 1)
                            n += 1
                        for k in range(KD):
                            free(n)
                            for t in range(T):
                                if k == 0:
                                    pe.wait_ge(xn_ready, t + 1)
                                mm = nc.tensor.transpose(bank[:, n % 8, t * P:(t + 1) * P], xn[:, t, k * P:(k + 1) * P], ident[:])
                            mm.then_inc(produced, 1)
                            n += 1
                        pe.wait_ge(evacuated, AT_QKV)
                        for t in range(T):
                            for lo, hi in ((0, 2 * D), (2 * D, 3 * D)):
                                free(n)
                                for k in range(KD):
                                    mm = nc.tensor.matmul(bank[:, n % 8, 0:hi - lo], xT[:, k, t * P:(t + 1) * P],
                                                          w_qkv[:, k, lo:hi], start=(k == 0), stop=(k == KD - 1))
                                mm.then_inc(produced, 1)
                                n += 1
                        for t in range(T):
                            for half in range(2):
                                free(n)
                                for k in range(KD):
                                    mm = nc.tensor.matmul(bank[:, n % 8, :], cT[:, k, t * P:(t + 1) * P],
                                                          w_v2[:, k, half * 512:(half + 1) * 512],
                                                          start=(k == 0), stop=(k == KD - 1))
                                mm.then_inc(produced, 1)
                                n += 1
                        pe.wait_ge(roped, 1)
                        for a in range(2):
                            for g in range(G1):
                                free(n)
                                for t in range(T):
                                    h = a * H + g * GH
                                    mm = nc.tensor.transpose(bank[:, n % 8, t * P:(t + 1) * P],
                                                             qk_pad[:, t, h:h + GH, :].rearrange("p h s -> p (h s)"), ident[:])
                                mm.then_inc(produced, 1)
                                n += 1

                    @block.scalar
                    def _(act):
                        n = 0

                        def move(dst, width=512):
                            nonlocal n
                            act.wait_ge(produced, n + 1)
                            nc.scalar.copy(dst, bank[:, n % 8, 0:width]).then_inc(evacuated, 1)
                            n += 1

                        for k in range(KD):
                            move(cT[:, k, :])
                        for j in range(G2):
                            move(k2T[:, j, :])
                        for k in range(KD):
                            move(xT[:, k, :])
                        for t in range(T):
                            move(qkv[:, t, 0:2 * D])
                            move(qkv[:, t, 2 * D:3 * D], D)
                        for t in range(T):
                            for half in range(2):
                                move(v2[:, t, half * 512:(half + 1) * 512])
                        for a in range(2):
                            for g in range(G1):
                                move(qk1T[:, a, g, :])

                    @block.vector
                    def _(dve):
                        layernorm(dve, None, lambda t: xb[:, t, :], steps, root, xn_ready,
                                  lambda t: dve.wait_ge(x_in, 16) if t == 0 else None)
                        n = 0

                        def step(ins):
                            nonlocal n
                            n += 1
                            ins.then_inc(head_steps, 1)
                            dve.wait_ge(head_steps, n)

                        HH = HD // 2
                        dve.wait_ge(evacuated, AT_V2)
                        heads = qkv[:, :, 0:2 * D].rearrange("p t (h d) -> p t h d", d=HD)
                        for t in range(T):
                            nc.vector.tensor_copy(v_pad[:, t, :, 0:HD], qkv[:, t, 2 * D:3 * D].rearrange("p (h d) -> p h d", d=HD)
                                                  ).then_inc(v_copied, 1)
                        for t in range(T):
                            step(nc.vector.tensor_reduce(hsum[:, t, :], heads[:, t], AX.X, ALU.add))
                        step(nc.vector.tensor_scalar(hsum[:], hsum[:], 1.0 / HD, None, ALU.mult))
                        for t in range(T):
                            step(nc.vector.tensor_tensor(heads[:, t], heads[:, t], hsum[:, t, :, None].to_broadcast([P, 2 * H, HD]),
                                                         ALU.subtract))
                        for t in range(T):
                            step(nc.vector.tensor_tensor(qk_pad[:, t, :, 0:HD], heads[:, t], heads[:, t], ALU.mult))
                        for t in range(T):
                            step(nc.vector.tensor_reduce(hvar[:, t, :], qk_pad[:, t, :, 0:HD], AX.X, ALU.add))
                        step(nc.vector.tensor_scalar(hvar[:], hvar[:], 1.0 / HD, EPS, ALU.mult, ALU.add))
                        dve.wait_ge(head_root, 1)
                        for t in range(T):
                            step(nc.vector.tensor_tensor(heads[:, t], heads[:, t], hstd[:, t, :, None].to_broadcast([P, 2 * H, HD]),
                                                         ALU.mult))
                        for t in range(T):
                            for a in range(2):
                                src = heads[:, t, a * H:(a + 1) * H, :]
                                dst = qk_pad[:, t, a * H:(a + 1) * H, 0:HD]
                                for half in range(2):
                                    part = slice(half * HH, (half + 1) * HH)
                                    step(nc.vector.tensor_tensor(
                                        dst[:, :, part], src[:, :, 1 - half:HD:2],
                                        gsin[:, t, a:a + 1, part].to_broadcast([P, H, HH]), ALU.mult))
                                step(nc.vector.tensor_tensor(src, src, gcos[:, t, a:a + 1, :].to_broadcast([P, H, HD]), ALU.mult))
                                step(nc.vector.tensor_tensor(dst, dst, src, ALU.add))
                                step(nc.vector.tensor_tensor(dst, dst, bsum[:, t, a:a + 1, :].to_broadcast([P, H, HD]), ALU.add))
                        nc.vector.drain().then_inc(roped, 1)

                    @block.gpsimd
                    def _(pool):
                        layernorm(None, pool, None, steps, root, None, None)
                        pool.wait_ge(head_steps, 4 * T + 2)
                        nc.gpsimd.tensor_tensor(hstd[:], hvar[:], half_neg[:, 0:T * 2 * H].rearrange("p (t h) -> p t h", t=T),
                                                ALU.pow).then_inc(head_root, 1)
                nc.all_engine_barrier(sems_to_clear=range(x_in.num, v_copied.num + 1))

                def attention(name, causal_mode):
                    LEAD = 3
                    U = H * T
                    heads_per_bank = GH if causal_mode else GH2
                    groups = H // heads_per_bank

                    def keys(u):
                        return (u % T + 1) * P if causal_mode else S

                    def evac_on_dve(u):
                        return u % T == 0

                    with nc.semaphore(name + "_scored") as scored, nc.semaphore(name + "_masked") as masked, \
                            nc.semaphore(name + "_exped") as exped, nc.semaphore(name + "_inverted") as inverted, \
                            nc.semaphore(name + "_normed") as normed, nc.semaphore(name + "_turned") as turned, \
                            nc.semaphore(name + "_moved_act") as moved_act, nc.semaphore(name + "_moved_dve") as moved_dve, \
                            nc.semaphore(name + "_valued") as valued, nc.semaphore(name + "_stored") as stored, nc.Block() as block:

                        def moves_before(u):
                            on_dve = sum(evac_on_dve(i) for i in range(u))
                            return u - on_dve, on_dve

                        @block.tensor
                        def _(pe):
                            def scores(u):
                                h, t = divmod(u, T)
                                if u >= 3:
                                    pe.wait_ge(masked, u - 2)
                                if causal_mode:
                                    g, i = divmod(h, GH)
                                    part = slice(SLOT * i, SLOT * i + HD)
                                    q, k = qk1T[part, 0, g, t * P:(t + 1) * P], qk1T[part, 1, g, 0:keys(u)]
                                else:
                                    g, i = divmod(h, GH2)
                                    part = slice(HD2 * i, HD2 * i + HD2)
                                    q, k = q2T[part, g, t * P:(t + 1) * P], k2T[part, g, :]
                                nc.tensor.matmul(bank[:, u % 3, 0:keys(u)], q, k, start=True, stop=True).then_inc(scored, 1)

                            def turn(u):
                                pe.wait_ge(normed, u + 1)
                                if u >= 3:
                                    a, d = moves_before(u - 2)
                                    pe.wait_ge(moved_act, a) if a else None
                                    pe.wait_ge(moved_dve, d) if d else None
                                for kt in range(keys(u) // P):
                                    mm = nc.tensor.transpose(bank[:, 3 + u % 3, kt * P:(kt + 1) * P],
                                                             p_sb[:, u % 3, kt * P:(kt + 1) * P], ident[:])
                                mm.then_inc(turned, 1)

                            def values(h):
                                a, d = moves_before((h + 1) * T)
                                pe.wait_ge(moved_act, a)
                                pe.wait_ge(moved_dve, d)
                                g, i = divmod(h, heads_per_bank)
                                if i == 0 and g >= 2:
                                    pe.wait_ge(stored, g - 1)
                                for kt in range(T):
                                    lo = kt * P if causal_mode else 0
                                    if causal_mode:
                                        part, v = slice(SLOT * i, SLOT * (i + 1)), v_pad[:, kt, h, :]
                                    else:
                                        part, v = slice(HD2 * i, HD2 * (i + 1)), v2[:, kt, h * HD2:(h + 1) * HD2]
                                    mm = nc.tensor.matmul(bank[part, 6 + g % 2, lo:S], v, pT[:, h % 2, kt, lo:S],
                                                          start=(kt == 0), stop=(kt == T - 1))
                                mm.then_inc(valued, 1)

                            for i in range(U + LEAD + 2):
                                if i < U:
                                    scores(i)
                                if LEAD <= i < U + LEAD:
                                    turn(i - LEAD)
                                u = i - LEAD - 1
                                if u >= 0 and u % T == T - 1:
                                    values(u // T)

                        def move(eng, u):
                            eng.wait_ge(turned, u + 1)
                            h, t = divmod(u, T)
                            if h >= 2:
                                eng.wait_ge(valued, h - 1)
                            n = keys(u) // P
                            dst = pT[:, h % 2, 0:n, t * P:(t + 1) * P]
                            src = bank[:, 3 + u % 3, 0:n * P].rearrange("p (k q) -> p k q", k=n)
                            if eng is act_engine:
                                nc.scalar.copy(dst, src).then_inc(moved_act, 1)
                            else:
                                nc.vector.tensor_copy(dst, src).then_inc(moved_dve, 1)

                        act_engine = nc.scalar

                        @block.vector
                        def _(dve):
                            def mask(u):
                                dve.wait_ge(scored, u + 1)
                                if u >= 3:
                                    dve.wait_ge(exped, u - 2)
                                t, n = u % T, keys(u)
                                m = causal[:, S - t * P:S - t * P + n] if causal_mode else mb[:, t, :]
                                nc.vector.tensor_tensor_reduce(
                                    s_sb[:, u % 3, 0:n], bank[:, u % 3, 0:n], m, -SCALE1 if causal_mode else -1.0, BIG,
                                    ALU.add, ALU.min, negmax[:, u:u + 1]).then_inc(masked, 1)

                            def invert(u):
                                dve.wait_ge(exped, u + 1)
                                nc.vector.reciprocal(pinv[:, u:u + 1], psum_row[:, u:u + 1]).then_inc(inverted, 1)

                            for i in range(U + LEAD + 1):
                                if i < U:
                                    mask(i)
                                if 1 <= i <= U:
                                    invert(i - 1)
                                u = i - LEAD
                                if u >= 0 and u < U and evac_on_dve(u):
                                    move(nc.vector, u)

                        @block.scalar
                        def _(act):
                            def exp(u):
                                act.wait_ge(masked, u + 1)
                                if u >= 3:
                                    act.wait_ge(turned, u - 2)
                                n = keys(u)
                                nc.scalar.activation(p_sb[:, u % 3, 0:n], s_sb[:, u % 3, 0:n], ACT.Exp, bias=negmax[:, u:u + 1],
                                                     scale=-1.0, accum_out=psum_row[:, u:u + 1]).then_inc(exped, 1)

                            def store(g):
                                act.wait_ge(valued, (g + 1) * heads_per_bank)
                                dst = o1T[:, g, :] if causal_mode else o2T[:, g, :]
                                nc.scalar.copy(dst, bank[:, 6 + g % 2, :]).then_inc(stored, 1)

                            for i in range(U + LEAD + 3):
                                if i < U:
                                    exp(i)
                                u = i - LEAD
                                if 0 <= u < U and not evac_on_dve(u):
                                    move(nc.scalar, u)
                                u = i - LEAD - 2
                                if u >= 0 and (u + 1) % (T * heads_per_bank) == 0:
                                    store((u + 1) // (T * heads_per_bank) - 1)

                        @block.gpsimd
                        def _(pool):
                            for u in range(U):
                                pool.wait_ge(inverted, u + 1)
                                n = keys(u)
                                nc.gpsimd.tensor_scalar(p_sb[:, u % 3, 0:n], p_sb[:, u % 3, 0:n], pinv[:, u:u + 1], 1.0,
                                                        ALU.mult, ALU.mult).then_inc(normed, 1)
                    nc.all_engine_barrier(sems_to_clear=range(scored.num, stored.num + 1))

                attention("self", True)

                with nc.semaphore("biased") as biased, nc.semaphore("projected") as projected, \
                        nc.semaphore("added") as added, nc.semaphore("m_steps") as steps, nc.semaphore("m_root") as root, \
                        nc.semaphore("m_xn_ready") as xn_ready, nc.semaphore("m_produced") as produced, \
                        nc.semaphore("m_evacuated") as evacuated, nc.Block() as block:

                    @block.gpsimd
                    def _(pool):
                        for t in range(T):
                            nc.gpsimd.tensor_tensor(xb[:, t, :], xb[:, t, :], b_o[:], ALU.add).then_inc(biased, 1)
                        layernorm(None, pool, None, steps, root, None, None)

                    @block.tensor
                    def _(pe):
                        for t in range(T):
                            for g in range(G1):
                                mm = nc.tensor.matmul(bank[:, t, 0:D], o1T[:, g, t * P:(t + 1) * P], w_o1[:, g, :],
                                                      start=(g == 0), stop=(g == G1 - 1))
                            mm.then_inc(projected, 1)
                        for k in range(KD):
                            for t in range(T):
                                if k == 0:
                                    pe.wait_ge(xn_ready, t + 1)
                                mm = nc.tensor.transpose(bank[:, 4 + k, t * P:(t + 1) * P], xn[:, t, k * P:(k + 1) * P], ident[:])
                            mm.then_inc(produced, 1)
                        pe.wait_ge(evacuated, KD)
                        pe.wait_ge(added, T)
                        for j in range(G2):
                            if j >= 4:
                                pe.wait_ge(evacuated, KD + j - 3)
                            for k in range(KD):
                                mm = nc.tensor.matmul(bank[:, j % 4, :], w_q2[:, k, j * P:(j + 1) * P], xT[:, k, :],
                                                      start=(k == 0), stop=(k == KD - 1))
                            mm.then_inc(produced, 1)

                    @block.vector
                    def _(dve):
                        for t in range(T):
                            dve.wait_ge(projected, t + 1)
                            dve.wait_ge(biased, t + 1)
                            nc.vector.tensor_tensor(xb[:, t, :], bank[:, t, 0:D], xb[:, t, :], ALU.add).then_inc(added, 1)
                        layernorm(dve, None, lambda t: xb[:, t, :], steps, root, xn_ready, lambda t: dve.wait_ge(added, t + 1))

                    @block.scalar
                    def _(act):
                        for k in range(KD):
                            act.wait_ge(produced, k + 1)
                            nc.scalar.copy(xT[:, k, :], bank[:, 4 + k, :]).then_inc(evacuated, 1)
                        for j in range(G2):
                            act.wait_ge(produced, KD + j + 1)
                            nc.scalar.copy(q2T[:, j, :], bank[:, j % 4, :]).then_inc(evacuated, 1)
                nc.all_engine_barrier(sems_to_clear=range(biased.num, evacuated.num + 1))

                attention("cross", False)

                with nc.semaphore("r_projected") as projected, nc.semaphore("r_added") as added, \
                        nc.semaphore("r_steps") as steps, nc.semaphore("r_root") as root, nc.semaphore("r_xn_ready") as xn_ready, \
                        nc.semaphore("r_produced") as produced, nc.semaphore("r_evacuated") as evacuated, \
                        nc.semaphore("r_logits") as logits, nc.semaphore("r_picked") as picked, \
                        nc.semaphore("r_exped") as exped, nc.semaphore("r_saved") as saved, nc.Block() as block:

                    @block.sync
                    def _(sp):
                        one = bass.ds(b, 1)
                        sp.wait_ge(added, T)
                        sp.dma_start(out_b[one].rearrange("a p t d -> p (a t) d"), xb[:]).then_inc(saved, 16)
                        sp.wait_ge(evacuated, KD)
                        sp.dma_start(xT_dram[one].rearrange("a p k s -> p (a k) s"), xT[:]).then_inc(saved, 16)
                        sp.wait_ge(saved, 32)

                    @block.gpsimd
                    def _(pool):
                        layernorm(None, pool, None, steps, root, None, None)

                    @block.tensor
                    def _(pe):
                        for t in range(T):
                            for j in range(G2):
                                mm = nc.tensor.matmul(bank[:, t, 0:D], o2T[:, j, t * P:(t + 1) * P], w_o2[:, j, :],
                                                      start=(j == 0), stop=(j == G2 - 1))
                            mm.then_inc(projected, 1)
                        for k in range(KD):
                            for t in range(T):
                                if k == 0:
                                    pe.wait_ge(xn_ready, t + 1)
                                mm = nc.tensor.transpose(bank[:, 4 + k, t * P:(t + 1) * P], xn[:, t, k * P:(k + 1) * P], ident[:])
                            mm.then_inc(produced, 1)
                        pe.wait_ge(evacuated, KD)
                        for t in range(T):
                            for k in range(KD):
                                mm = nc.tensor.matmul(bank[:, 6, t * NE:(t + 1) * NE], xT[:, k, t * P:(t + 1) * P], w_g[:, k, :],
                                                      start=(k == 0), stop=(k == KD - 1))
                        mm.then_inc(logits, 1)

                    @block.scalar
                    def _(act):
                        for k in range(KD):
                            act.wait_ge(produced, k + 1)
                            nc.scalar.copy(xT[:, k, :], bank[:, 4 + k, :]).then_inc(evacuated, 1)
                        act.wait_ge(picked, 3)
                        for t in range(T):
                            nc.scalar.activation(ew[:, t, :], top[:, t, 0:TOP], ACT.Exp, bias=ntop[:, t:t + 1], scale=1.0
                                                 ).then_inc(exped, 1)

                    @block.vector
                    def _(dve):
                        for t in range(T):
                            dve.wait_ge(projected, t + 1)
                            nc.vector.tensor_tensor(xb[:, t, :], bank[:, t, 0:D], xb[:, t, :], ALU.add).then_inc(added, 1)
                        layernorm(dve, None, lambda t: xb[:, t, :], steps, root, xn_ready, lambda t: dve.wait_ge(added, t + 1))
                        n = 0

                        def step(ins):
                            nonlocal n
                            n += 1
                            ins.then_inc(picked, 1)
                            dve.wait_ge(picked, n)

                        dve.wait_ge(logits, 1)
                        step(nc.vector.tensor_copy(logit[:].rearrange("p t e -> p (t e)"), bank[:, 6, 0:T * NE]))
                        for t in range(T):
                            nc.vector.max(top[:, t, :], logit[:, t, :])
                        step(nc.vector.drain())
                        step(nc.vector.tensor_scalar(ntop[:], top[:, :, 0], -1.0, None, ALU.mult))
                        for t in range(T):
                            nc.vector.max_index(topi[:, t, :], top[:, t, :], logit[:, t, :])
                        step(nc.vector.drain())
                        step(nc.vector.tensor_copy(topf[:], topi[:]))
                        dve.wait_ge(exped, T)
                        step(nc.vector.tensor_tensor(esum[:], ew[:, :, 0], ew[:, :, 1], ALU.add))
                        step(nc.vector.reciprocal(esum[:], esum[:]))
                        step(nc.vector.tensor_tensor(ew[:], ew[:], esum[:, :, None].to_broadcast([P, T, TOP]), ALU.mult))
                        for t in range(T):
                            step(nc.vector.tensor_scalar(pick[:, t, :], expert_no[:], topf[:, t, 0:1], ew[:, t, 0:1],
                                                         ALU.is_equal, ALU.mult))
                            step(nc.vector.tensor_scalar(logit[:, t, :], expert_no[:], topf[:, t, 1:2], ew[:, t, 1:2],
                                                         ALU.is_equal, ALU.mult))
                        step(nc.vector.tensor_tensor(comb[:, bass.ds(b * T, T), :], pick[:], logit[:], ALU.add))
                nc.all_engine_barrier(sems_to_clear=range(projected.num, saved.num + 1))

        with ExitStack() as moe:
            def sm(name, shape, dt=F32):
                return moe.enter_context(nc.sbuf_tensor(name, shape, dt))

            x_all = sm("x_all", [P, NT, D])
            xT_all = sm("xT_all", [P, KD, B * S])
            with nc.semaphore("back") as back, nc.Block() as block:
                @block.sync
                def _(sp):
                    sp.dma_start(x_all[:], out_v).then_inc(back, 16)
                    for b in range(B):
                        sp.dma_start(xT_all[:, :, b * S:(b + 1) * S], xT_dram[b]).then_inc(back, 16)
                    sp.wait_ge(back, 16 * (B + 1))
            nc.all_engine_barrier()

            w_gu = sm("w_gu", [P, 2, KD, F2])
            w_dn = sm("w_dn", [P, 2, FT, D])
            sil = sm("sil", [P, 2, S])
            hid = sm("hid", [P, 2, FT, S])
            gu_v = gate_up_w.rearrange("e (k p) f -> e p k f", p=P)
            dn_v = down_w.rearrange("e (k p) f -> e p k f", p=P)
            PAIR = 2
            NU = PAIR * B * FT
            ND = PAIR * B * T

            with nc.Fori(0, NE // PAIR) as pair:
                with nc.semaphore("w_in0") as w_in0, nc.semaphore("w_in1") as w_in1, nc.semaphore("gated") as gated, \
                        nc.semaphore("silued") as silued, nc.semaphore("hidden") as hidden, nc.semaphore("downed") as downed, \
                        nc.semaphore("summed") as summed, nc.Block() as block:
                    w_in = [w_in0, w_in1]

                    @block.sync
                    def _(sp):
                        for i in range(PAIR):
                            one = bass.ds(pair * PAIR + i, 1)
                            sp.dma_start(w_gu[:, i], gu_v[one].rearrange("a p k f -> p (a k) f")).then_inc(w_in[i], 16)
                            sp.dma_start(w_dn[:, i], dn_v[one].rearrange("a p k f -> p (a k) f")).then_inc(w_in[i], 16)

                    @block.tensor
                    def _(pe):
                        def up(u):
                            i, c, f = u // (B * FT), u // FT % B, u % FT
                            if c == 0 and f == 0:
                                pe.wait_ge(w_in[i], 32)
                            if u >= 2:
                                pe.wait_ge(hidden, u - 1)
                            for part in range(2):
                                for k in range(KD):
                                    mm = nc.tensor.matmul(bank[:, 2 * (u % 2) + part, :],
                                                          w_gu[:, i, k, part * F + f * P:part * F + (f + 1) * P],
                                                          xT_all[:, k, c * S:(c + 1) * S], start=(k == 0), stop=(k == KD - 1))
                            mm.then_inc(gated, 1)

                        def down(chunk):
                            i = chunk // B
                            pe.wait_ge(hidden, (chunk + 1) * FT)
                            for t in range(T):
                                d = chunk * T + t
                                if d >= 4:
                                    pe.wait_ge(summed, d - 3)
                                for f in range(FT):
                                    mm = nc.tensor.matmul(bank[:, 4 + d % 4, 0:D], hid[:, chunk % 2, f, t * P:(t + 1) * P],
                                                          w_dn[:, i, f, :], start=(f == 0), stop=(f == FT - 1))
                                mm.then_inc(downed, 1)

                        for u in range(NU + 1):
                            if u < NU:
                                up(u)
                            if u >= FT and u % FT == 0:
                                down(u // FT - 1)

                    @block.scalar
                    def _(act):
                        for u in range(NU):
                            act.wait_ge(gated, u + 1)
                            if u >= 2:
                                act.wait_ge(hidden, u - 1)
                            nc.scalar.activation(sil[:, u % 2, :], bank[:, 2 * (u % 2), :], ACT.Silu).then_inc(silued, 1)

                    @block.vector
                    def _(dve):
                        def multiply(u):
                            chunk = u // FT
                            dve.wait_ge(silued, u + 1)
                            if chunk >= 2:
                                dve.wait_ge(downed, (chunk - 1) * T)
                            nc.vector.tensor_tensor(hid[:, chunk % 2, u % FT, :], bank[:, 2 * (u % 2) + 1, :], sil[:, u % 2, :],
                                                    ALU.mult).then_inc(hidden, 1)

                        def add(d):
                            i, tile = divmod(d, NT)
                            dve.wait_ge(downed, d + 1)
                            if i == 1 and tile == 0:
                                dve.wait_ge(summed, NT)
                            nc.vector.scalar_tensor_tensor(
                                x_all[:, tile, :], bank[:, 4 + d % 4, 0:D], comb[:, tile, bass.ds(pair * PAIR + i, 1)],
                                x_all[:, tile, :], ALU.mult, ALU.add).then_inc(summed, 1)

                        for u in range(NU + 2):
                            if u < NU:
                                multiply(u)
                            if u >= FT + 1 and (u - 1) % FT == 0:
                                for t in range(T):
                                    add(((u - 1) // FT - 1) * T + t)
                nc.all_engine_barrier(sems_to_clear=range(w_in0.num, summed.num + 1))

        with nc.semaphore("out_done") as out_done, nc.Block() as block:
            @block.sync
            def _(sp):
                sp.dma_start(out_v, x_all[:]).then_inc(out_done, 16)
                sp.wait_ge(out_done, 16)


def kernel(x, ctx_1024, fside_Bx1xSxS2_0, L0_attn_Wq, L0_attn_Wk, L0_attn_Wv, L0_attn_q_gamma, L0_attn_q_beta,
           L0_attn_k_gamma, L0_attn_k_beta, L0_attn_Wo, L0_attn_bo, L0_xattn_Wq, L0_xattn_Wk, L0_xattn_Wv, L0_xattn_Wo,
           L0_ffn_gate_w, L0_ffn_gate_up_w, L0_ffn_down_w):
    import numpy as np
    import concourse.bacc as bacc
    from concourse.bass_utils import run_bass_kernel_spmd

    x = np.asarray(x)
    B, S, D = x.shape
    HD = D // 16
    as_np = lambda a: np.ascontiguousarray(np.asarray(a))
    theta = np.arange(S)[:, None] * np.exp(-np.arange(0, HD, 2) / HD * math.log(10000.0))[None, :]
    cos, sin = np.repeat(np.cos(theta), 2, axis=1), np.repeat(np.sin(theta), 2, axis=1)
    sin[:, :HD // 2] *= -1.0
    rope = np.stack([cos, sin]).astype(np.float32)
    wo1 = np.zeros((16, 32, D), np.float32)
    wo1[:, :HD, :] = as_np(L0_attn_Wo).T.reshape(16, HD, D)
    arrays = {
        "x": x, "ctx_in": as_np(ctx_1024), "fside": as_np(fside_Bx1xSxS2_0),
        "wqkv": np.concatenate([as_np(w).T for w in (L0_attn_Wq, L0_attn_Wk, L0_attn_Wv)], axis=1),
        "head_affine": np.stack([as_np(a) for a in (L0_attn_q_gamma, L0_attn_k_gamma, L0_attn_q_beta, L0_attn_k_beta)]),
        "rope": rope, "wo1": wo1.reshape(-1, D), "bo": as_np(L0_attn_bo),
        "wq2": as_np(L0_xattn_Wq).T, "wk2": as_np(L0_xattn_Wk).T, "wv2": as_np(L0_xattn_Wv).T, "wo2": as_np(L0_xattn_Wo).T,
        "gate_w": as_np(L0_ffn_gate_w), "gate_up_w": as_np(L0_ffn_gate_up_w), "down_w": as_np(L0_ffn_down_w),
    }
    arrays = {f"in_{k}": np.ascontiguousarray(a) for k, a in arrays.items()}
    nc = bacc.Bacc("TRN2", target_bir_lowering=False, num_devices=1)
    args = [nc.dram_tensor(k, a.shape, mybir.dt.from_np(a.dtype), kind="ExternalInput").ap() for k, a in arrays.items()]
    args.append(nc.dram_tensor("out_dram", x.shape, F32, kind="ExternalOutput").ap())
    build(nc, *args)
    return run_bass_kernel_spmd(nc, [arrays], core_ids=[0]).results[0]["out_dram"]
```

```python
import math
from contextlib import ExitStack

import concourse.bass as bass
from concourse import mybir

F32 = mybir.dt.float32
F32R = mybir.dt.float32r
U32 = mybir.dt.uint32
I32 = mybir.dt.int32
ALU = mybir.AluOpType
ACT = mybir.ActivationFunctionType
AX = mybir.AxisListType

P = 128
EPS = 1e-5
BIG = 3.0e38
MASKED = -1.0e30
TOP = 2
RSQRT_BITS = float(0x5F3759DF)


def build(nc, x, ctx_in, fside, wqkv, head_affine, rope, wo1, bo, wq2, wk2, wv2, wo2, gate_w, gate_up_w, down_w, out):
    B, S, D = x.shape
    H = 16
    HD = D // H
    E2 = wq2.shape[1]
    HD2 = E2 // H
    T = S // P
    KD = D // P
    SLOT = 32
    GH = P // SLOT
    G1 = H // GH
    GH2 = P // HD2
    G2 = H // GH2
    NE, _, F2 = gate_up_w.shape
    F = F2 // 2
    FT = F // P
    NT = B * T
    SCALE1 = 1.0 / math.sqrt(HD)

    x_v = x.rearrange("b (t p) d -> b p t d", p=P)
    c_v = ctx_in.rearrange("b (t p) d -> b p t d", p=P)
    m_v = fside.rearrange("b o (t p) k -> b p (o t) k", p=P)
    out_b = out.rearrange("b (t p) d -> b p t d", p=P)
    out_v = out.rearrange("b (t p) d -> p (b t) d", p=P)
    TILES = (B * S * TOP + NE * (P - 1)) // P
    TILES += TILES % 2
    SPARE_TILES = TILES - B * S * TOP // P
    REGION = B * S + P
    SPARE = NE * REGION
    ROWS = SPARE + SPARE_TILES * P
    xs_dram = nc.dram_tensor("xs_dram", [ROWS, D], F32, kind="Internal").ap()
    ys_dram = nc.dram_tensor("ys_dram", [TILES * P, D], F32, kind="Internal").ap()

    with ExitStack() as ctx:
        def sb(name, shape, dt=F32):
            return ctx.enter_context(nc.sbuf_tensor(name, shape, dt))

        bank = ctx.enter_context(nc.psum_tensor("bank", [P, 8, 512], F32))

        share = sb("share", [P, NT, TOP])
        choice = sb("choice", [P, TOP, NT, NE])
        xs_row = sb("xs_row", [P, TOP, NT])
        used = sb("used", [P, NE])
        ident = sb("ident", [P, P])
        zeros = sb("zeros", [P, D])
        half_neg = sb("half_neg", [P, T])
        expert_no = sb("expert_no", [P, NE])
        ys_row = sb("ys_row", [P, TOP, NT], U32)
        region = sb("region", [P, NE])
        xn = sb("xn", [P, T, D])
        batch_slot = sb("batch_slot", [P, TOP, T], U32)

        scattered = ctx.enter_context(nc.semaphore("scattered"))

        def scatter(n):
            t, j = divmod(n, TOP)
            nc.gpsimd.indirect_dma_start(
                out=xs_dram, out_offset=bass.IndirectOffsetOnAxis(ap=batch_slot[:, j, t:t + 1], axis=0),
                in_=xn[:, t, :], in_offset=None).then_inc(scattered, 16)

        def f32(ap):
            return ap.bitcast(F32)

        with ExitStack() as att:
            def sa(name, shape, dt=F32):
                return att.enter_context(nc.sbuf_tensor(name, shape, dt))

            w_qkv = sa("w_qkv", [P, KD, 3 * D])
            w_o1 = sa("w_o1", [P, G1, D])
            w_q2 = sa("w_q2", [P, KD, E2])
            w_k2 = sa("w_k2", [P, KD, E2])
            w_v2 = sa("w_v2", [P, KD, E2])
            w_o2 = sa("w_o2", [P, G2, D])
            w_g = sa("w_g", [P, KD, NE])
            b_o = sa("b_o", [P, D])
            affine = sa("affine", [P, 4, HD])
            cs = sa("cs", [P, T, 2, HD])
            gcos = sa("gcos", [P, T, 2 * GH, HD])
            gsin = sa("gsin", [P, T, 2 * GH, HD])
            bsum = sa("bsum", [P, T, 2 * GH, HD])
            causal = sa("causal", [P, 2 * S])

            xb = sa("xb", [P, T, D])
            xa = sa("xa", [P, T, D])
            cb = xa
            mb = sa("mb", [P, T, S])
            xT = sa("xT", [P, KD, S])
            cT = sa("cT", [P, KD, S])
            with nc.sbuf_tensor("qkv", [P, T, 3 * D], F32) as qkv:
                pass
            kHL = sa("kHL", [P, 6 * S], F32R)
            kH = kHL[:, 0:2 * GH2 * S].rearrange("p (r i s) -> p r i s", r=2, i=GH2)
            kL = kHL[:, 2 * GH2 * S:].rearrange("p (r s) -> p r s", r=2)
            stat = sa("stat", [P, T, 6])
            mv = sa("mv", [P, T, 2])
            rstd = sa("rstd", [P, T])
            o2T = sa("o2T", [P, G2, S])
            o1T = o2T[:, 0:G1, :]
            s_sb = sa("s_sb", [P, 3, S])
            p_sb = sa("p_sb", [P, 5, S])
            pH = sa("pH", [P, 2, T, S], F32R)
            pL = sa("pL", [P, 2, T, S], F32R)
            negmax = sa("negmax", [P, H * T])
            psum_row = sa("psum_row", [P, H * T])
            pinv = sa("pinv", [P, H * T])
            logit = sa("logit", [P, T, NE])
            top = sa("top", [P, T, 8])
            topi = sa("topi", [P, T, 8], U32)
            topf = sa("topf", [P, T, 8])
            ntop = sa("ntop", [P, T])
            ew = sa("ew", [P, T, TOP])
            esum = sa("esum", [P, T])
            chosen = sa("chosen", [P, TOP, T, NE])
            either = sa("either", [P, T, NE])
            total = sa("total", [P, T, NE])
            rank = sa("rank", [P, T, NE])
            picked_row = sa("picked_row", [P, TOP, T, NE])
            slot_f = sa("slot_f", [P, TOP, T])
            before = sa("before", [P, P])
            ones = sa("ones", [P, P])

            with nc.semaphore("loaded") as loaded, nc.semaphore("pool_set") as pool_set, \
                    nc.semaphore("tab") as tab, \
                    nc.sbuf_tensor("btmp", [P, T, 2 * GH, HD], F32) as btmp, nc.Block() as block:
                LOADS = 12

                @block.sync
                def _(sp):
                    sp.dma_start(w_qkv[:], wqkv.rearrange("(k p) n -> p k n", p=P)).then_inc(loaded, 16)
                    sp.dma_start(w_k2[:], wk2.rearrange("(k p) n -> p k n", p=P)).then_inc(loaded, 16)
                    sp.dma_start(w_v2[:], wv2.rearrange("(k p) n -> p k n", p=P)).then_inc(loaded, 16)
                    sp.dma_start(w_q2[:], wq2.rearrange("(k p) n -> p k n", p=P)).then_inc(loaded, 16)
                    sp.dma_start(w_o1[:], wo1.rearrange("(g p) n -> p g n", p=P)).then_inc(loaded, 16)
                    sp.dma_start(w_o2[:], wo2.rearrange("(g p) n -> p g n", p=P)).then_inc(loaded, 16)
                    sp.dma_start(w_g[:], gate_w.rearrange("(k p) n -> p k n", p=P)).then_inc(loaded, 16)
                    sp.dma_start(b_o[:], bo.partition_broadcast(P)).then_inc(loaded, 16)
                    for i in range(2):
                        sp.dma_start(affine[:, 2 * i:2 * i + 2, :].rearrange("p a d -> p (a d)"),
                                     head_affine[2 * i:2 * i + 2, :].rearrange("a d -> (a d)").partition_broadcast(P)
                                     ).then_inc(loaded, 16)
                    for i in range(2):
                        sp.dma_start(cs[:, :, i, :], rope[i].rearrange("(t p) d -> p t d", p=P)).then_inc(loaded, 16)
                    sp.wait_ge(loaded, 16 * LOADS)

                @block.gpsimd
                def _(pool):
                    pool.memset(ident[:], 0.0).then_inc(pool_set, 1)
                    pool.memset(causal[:], 0.0).then_inc(pool_set, 1)
                    pool.memset(half_neg[:], -0.5).then_inc(pool_set, 1)
                    pool.iota(expert_no[:], [[1, NE]], base=0, channel_multiplier=0,
                              allow_small_or_imprecise_dtypes=True).then_inc(pool_set, 1)
                    pool.iota(region[:], [[REGION, NE]], base=0, channel_multiplier=0,
                              allow_small_or_imprecise_dtypes=True).then_inc(pool_set, 1)
                    pool.memset(before[:], 1.0).then_inc(pool_set, 1)
                    pool.memset(ones[:], 1.0).then_inc(pool_set, 1)
                    pool.memset(zeros[:], 0.0).then_inc(pool_set, 1)
                    pool.memset(used[:], 0.0).then_inc(pool_set, 1)
                    pool.wait_ge(pool_set, 9)
                    pool.affine_select(out=before[:], in_=before[:], compare_op=ALU.is_gt, fill=0.0, base=0,
                                       pattern=[[1, P]], channel_multiplier=-1).then_inc(pool_set, 1)
                    pool.affine_select(out=ident[:], in_=ident[:], compare_op=ALU.not_equal, fill=1.0, base=0,
                                       pattern=[[-1, P]], channel_multiplier=1).then_inc(pool_set, 1)
                    pool.affine_select(out=causal[:], in_=causal[:], compare_op=ALU.is_ge, fill=MASKED, base=S,
                                       pattern=[[-1, 2 * S]], channel_multiplier=1).then_inc(pool_set, 1)
                    pool.memset(xn[:], 0.0).then_inc(pool_set, 1)
                    for n in range(T * TOP):
                        pool.iota(batch_slot[:, n % TOP, n // TOP:n // TOP + 1], [[0, 1]], base=SPARE + n % SPARE_TILES * P,
                                  channel_multiplier=1).then_inc(pool_set, 1)
                    pool.wait_ge(pool_set, 13 + T * TOP)
                    for i in range(SPARE_TILES):
                        pool.dma_start(xs_dram[SPARE + i * P:SPARE + (i + 1) * P, :], zeros[:]).then_inc(scattered, 16)
                    pool.wait_ge(scattered, 16 * SPARE_TILES)

                @block.vector
                def _(dve):
                    dve.wait_ge(loaded, 16 * LOADS)
                    HH = HD // 2
                    n = 0
                    for i in range(2 * GH):
                        a = i // GH
                        for (dst, src, rotated) in ((gcos, a, False), (gsin, a, True), (bsum, 2 + a, False),
                                                    (btmp, 2 + a, True)):
                            if not rotated:
                                nc.vector.tensor_tensor(dst[:, :, i, :], cs[:, :, 0, :],
                                                        affine[:, src:src + 1, :].to_broadcast([P, T, HD]),
                                                        ALU.mult).then_inc(tab, 1)
                                n += 1
                                continue
                            for half in range(2):
                                nc.vector.tensor_tensor(
                                    dst[:, :, i, half * HH:(half + 1) * HH], cs[:, :, 1, half * HH:(half + 1) * HH],
                                    affine[:, src:src + 1, 1 - half:HD:2].to_broadcast([P, T, HH]),
                                    ALU.mult).then_inc(tab, 1)
                                n += 1
                    dve.wait_ge(tab, n)
                    nc.vector.tensor_tensor(bsum[:], bsum[:], btmp[:], ALU.add).then_inc(tab, 1)
                    dve.wait_ge(tab, n + 1)
            nc.all_engine_barrier(sems_to_clear=range(loaded.num, tab.num + 1))

            def ln_vector(dve, src, dst, wait_src, wait_dst, steps, root, done):
                for t in range(T):
                    wait_src(t)
                    nc.vector.bn_stats(stat[:, t, :], src[:, t, :]).then_inc(steps, 1)
                dve.wait_ge(steps, T)
                for t in range(T):
                    nc.vector.bn_aggr(mv[:, t, :], stat[:, t, :]).then_inc(steps, 1)
                dve.wait_ge(steps, 2 * T)
                nc.vector.tensor_scalar(rstd[:], mv[:, :, 1], EPS, None, ALU.add).then_inc(steps, 1)
                dve.wait_ge(root, 1)
                wait_dst()
                for t in range(T):
                    nc.vector.tensor_scalar(dst[:, t, :], src[:, t, :], mv[:, t, 0:1], rstd[:, t:t + 1],
                                            ALU.subtract, ALU.mult).then_inc(done, 1)

            def ln_pool(pool, steps, root):
                pool.wait_ge(steps, 2 * T + 1)
                nc.gpsimd.tensor_tensor(rstd[:], rstd[:], half_neg[:, 0:T], ALU.pow).then_inc(root, 1)

            QKV_PARTS = ((0, 2 * D), (2 * D, 3 * D))

            with ExitStack() as stage:
                def sem(name):
                    return stage.enter_context(nc.semaphore(name))

                xn0 = stage.enter_context(nc.sbuf_tensor("xn0", [P, T, D], F32))
                xT0 = stage.enter_context(nc.sbuf_tensor("xT0", [P, KD, S], F32))
                x_in, steps, root, xn_ready, produced, evacuated = (
                    sem("p_x_in"), sem("p_steps"), sem("p_root"), sem("p_xn_ready"), sem("p_produced"), sem("p_evacuated"))
                block = stage.enter_context(nc.Block())

                @block.sync
                def _(sp):
                    sp.dma_start(xa[:], x_v[0]).then_inc(x_in, 16)

                @block.gpsimd
                def _(pool):
                    ln_pool(pool, steps, root)

                @block.vector
                def _(dve):
                    ln_vector(dve, xa, xn0, lambda t: dve.wait_ge(x_in, 16), lambda: None, steps, root, xn_ready)

                @block.tensor
                def _(pe):
                    for k in range(KD):
                        for t in range(T):
                            if k == 0:
                                pe.wait_ge(xn_ready, t + 1)
                            mm = nc.tensor.transpose(bank[:, k, t * P:(t + 1) * P], xn0[:, t, k * P:(k + 1) * P], ident[:])
                        mm.then_inc(produced, 1)
                    pe.wait_ge(evacuated, KD)
                    for n in range(2 * T):
                        t, (lo, hi) = n // 2, QKV_PARTS[n % 2]
                        if n >= 6:
                            pe.wait_ge(evacuated, KD + n - 5)
                        for k in range(KD):
                            mm = nc.tensor.matmul(bank[:, 2 + n % 6, 0:hi - lo], xT0[:, k, t * P:(t + 1) * P], w_qkv[:, k, lo:hi],
                                                  start=(k == 0), stop=(k == KD - 1))
                        mm.then_inc(produced, 1)

                @block.scalar
                def _(act):
                    for k in range(KD):
                        act.wait_ge(produced, k + 1)
                        nc.scalar.copy(xT0[:, k, :], bank[:, k, :]).then_inc(evacuated, 1)
                    for n in range(2 * T):
                        t, (lo, hi) = n // 2, QKV_PARTS[n % 2]
                        act.wait_ge(produced, KD + n + 1)
                        nc.scalar.copy(qkv[:, t, lo:hi], bank[:, 2 + n % 6, 0:hi - lo]).then_inc(evacuated, 1)
            nc.all_engine_barrier(sems_to_clear=range(x_in.num, evacuated.num + 1))

            TURN_LAG, HIGH_LAG, LOW_LAG, VALUES_LAG = 4, 3, 5, 10
            VALUE_STEPS = 2
            U = H * T
            S_BANK, T_BANK, O_BANK, J_BANK = 0, 2, 5, 7
            NPS = 5


            def values_at(i):
                h, k = divmod(i - VALUES_LAG, T)
                each = T // VALUE_STEPS
                return [(h, k * each + n) for n in range(each)] if 0 <= h < H and k < VALUE_STEPS else []

            def head_out(i, after):
                h, k = divmod(i - VALUES_LAG - VALUE_STEPS + 1 - after, T)
                return h if 0 <= h < H and k == 0 else None

            STEPS = U - T + VALUES_LAG + VALUE_STEPS

            class Soft:

                def __init__(self, sem, keys, mask, scale):
                    self.keys, self.mask, self.scale = keys, mask, scale
                    self.scored = sem("scored")
                    self.masked = sem("masked")
                    self.exped = sem("exped")
                    self.inverted = sem("inverted")
                    self.normed = sem("normed")
                    self.turned = sem("turned")
                    self.high = sem("high")
                    self.low = sem("low")
                    self.valued = sem("valued")

                def mask_scores(self, dve, u):
                    dve.wait_ge(self.scored, u + 1)
                    if u >= 3:
                        dve.wait_ge(self.exped, u - 2)
                    n = self.keys(u)
                    nc.vector.tensor_tensor_reduce(s_sb[:, u % 3, 0:n], bank[:, S_BANK + u % 2, 0:n], self.mask(u), -self.scale,
                                                   BIG, ALU.add, ALU.min, negmax[:, u:u + 1]).then_inc(self.masked, 1)

                def exp(self, act, u):
                    act.wait_ge(self.masked, u + 1)
                    if u >= NPS:
                        act.wait_ge(self.turned, u - NPS + 1)
                    n = self.keys(u)
                    nc.scalar.activation(p_sb[:, u % NPS, 0:n], s_sb[:, u % 3, 0:n], ACT.Exp, bias=negmax[:, u:u + 1],
                                         scale=-1.0, accum_out=psum_row[:, u:u + 1]).then_inc(self.exped, 1)

                def invert(self, dve, u):
                    dve.wait_ge(self.exped, u + 1)
                    nc.vector.reciprocal(pinv[:, u:u + 1], psum_row[:, u:u + 1]).then_inc(self.inverted, 1)

                def norm(self, pool, u):
                    pool.wait_ge(self.inverted, u + 1)
                    n = self.keys(u)
                    nc.gpsimd.tensor_scalar(p_sb[:, u % NPS, 0:n], p_sb[:, u % NPS, 0:n], pinv[:, u:u + 1], 1.0,
                                            ALU.mult, ALU.mult).then_inc(self.normed, 1)

                def turn(self, pe, u):
                    pe.wait_ge(self.normed, u + 1)
                    if u >= 3:
                        pe.wait_ge(self.low, u - 2)
                    for kt in range(self.keys(u) // P):
                        mm = nc.tensor.transpose(bank[:, T_BANK + u % 3, kt * P:(kt + 1) * P],
                                                 p_sb[:, u % NPS, kt * P:(kt + 1) * P], ident[:])
                    mm.then_inc(self.turned, 1)

                def halves(self, u, dst):
                    h, t = divmod(u, T)
                    n = self.keys(u) // P
                    return (dst[:, h % 2, 0:n, t * P:(t + 1) * P],
                            bank[:, T_BANK + u % 3, 0:n * P].rearrange("p (k q) -> p k q", k=n))

                def move_high(self, act, u):
                    act.wait_ge(self.turned, u + 1)
                    if u >= 2 * T:
                        act.wait_ge(self.valued, (u // T - 1) * T)
                    dst, src = self.halves(u, pH)
                    nc.scalar.copy(dst, src).then_inc(self.high, 1)

                def move_low(self, dve, u):
                    dve.wait_ge(self.high, u + 1)
                    dst, src = self.halves(u, pL)
                    nc.vector.tensor_tensor(dst, src, f32(self.halves(u, pH)[0]), ALU.subtract).then_inc(self.low, 1)

                def values(self, pe, h, kt, stationary, rows, first_key_only):
                    if kt == 0:
                        pe.wait_ge(self.low, (h + 1) * T)
                    lo = kt * P if first_key_only else 0
                    for part in (pH, pL):
                        mm = nc.tensor.matmul(bank[0:rows, O_BANK + h % 2, lo:S], stationary, part[:, h % 2, kt, lo:S],
                                              start=(kt == 0 and part is pH), stop=(kt == T - 1 and part is pL))
                    mm.then_inc(self.valued, 1)

            def self_attention():
                with ExitStack() as stage:
                    def sem(name):
                        return stage.enter_context(nc.semaphore("s_" + name))

                    def ss(name, shape, dt=F32):
                        return stage.enter_context(nc.sbuf_tensor(name, shape, dt))

                    v_pad = ss("v_pad", [P, T, H, SLOT], F32R)
                    tok = ss("tok", [P, T, 3, GH, SLOT], F32R)
                    qkT = ss("qkT", [P, 2, 3, S], F32R)
                    cen = ss("cen", [P, T, 2 * GH, HD])
                    tmp = ss("tmp", [P, T, 2 * GH, HD])
                    rq = ss("rq", [P, T, 2 * GH, HD])
                    hsum = ss("hsum", [P, T * 2 * GH])
                    hvar = ss("hvar", [P, T * 2 * GH])
                    hstd = ss("hstd", [P, T * 2 * GH])

                    first = c_in = sem("c_in")
                    m_in, v_high, v_low, rope_steps, first_low = sem("m_in"), sem("v_high"), sem("v_low"), sem("rope_steps"), sem("first_low")
                    split_high, split_low, qk_turned, qk_moved = sem("split_high"), sem("split_low"), sem("qk_turned"), sem("qk_moved")
                    soft = Soft(sem, lambda u: (u % T + 1) * P,
                                lambda u: causal[:, S - u % T * P:S - u % T * P + (u % T + 1) * P], SCALE1)
                    biased, stored = sem("biased"), sem("stored")
                    last = stored
                    block = stage.enter_context(nc.Block())
                    UG = GH * T
                    HH = HD // 2
                    NEWTON = [step + str(n) for n in range(3) for step in ("square", "times", "better")]
                    PARTS = ["sum", "center", "squares", "squares_sum", "variance", "shift", "guess", "half", *NEWTON,
                             "scale", "sin0", "sin1", "cos", "add", "beta"]
                    ROPE_UP_TO = {0: "sum", 1: "center", 2: "squares", 3: "guess", 4: "times1", 5: "better2", 6: "scale",
                                  7: "sin1", 8: "cos", 9: "beta"}
                    SPLIT_AT, TURN_AT = 10, 12
                    BIAS_AT = 4
                    SCATTER_AT = {g * UG + 4 * n + 2: g * 2 + n for g in range(G1) for n in range(2)}

                    def turn_bank(g, a):
                        return J_BANK if g else O_BANK + a

                    def lower(engine, a):
                        side = slice(HD, 2 * HD) if a < 2 else slice(0, HD)
                        high = slice(0, HD) if a < 2 else slice(HD, 2 * HD)
                        return engine.tensor_tensor(tok[:, :, a, :, side], rq[:, :, min(a, 1) * GH:(min(a, 1) + 1) * GH, :],
                                                    f32(tok[:, :, a, :, high]), ALU.subtract)

                    def group(g):
                        return qkv[:, :, 2 * GH * HD * g:2 * GH * HD * (g + 1)]

                    @block.sync
                    def _(sp):
                        one = bass.ds(b, 1)
                        sp.dma_start(mb[:], m_v[one].rearrange("a p t d -> p (a t) d")).then_inc(m_in, 16)
                        sp.wait_ge(biased, T)
                        sp.dma_start(cb[:], c_v[one].rearrange("a p t d -> p (a t) d")).then_inc(c_in, 16)
                        sp.wait_ge(c_in, 16)
                        sp.wait_ge(m_in, 16)

                    @block.vector
                    def _(dve):
                        def rope(g, part):
                            k = PARTS.index(part)
                            if g or k:
                                dve.wait_ge(rope_steps, len(PARTS) * g + k)
                            x4 = group(g).rearrange("p t (h d) -> p t h d", d=HD)
                            flat = lambda a: a[:].rearrange("p t h d -> p (t h) d")
                            wide = lambda a: a[:, :, None].to_broadcast([P, T * 2 * GH, HD])
                            if part == "sum":
                                ins = nc.vector.tensor_reduce(hsum[:].rearrange("p (t h) -> p t h", t=T), x4, AX.X, ALU.add)
                            elif part == "center":
                                ins = nc.vector.scalar_tensor_tensor(cen[:].rearrange("p t h d -> p t h d"), wide(hsum).rearrange(
                                    "p (t h) d -> p t h d", t=T), -1.0 / HD, x4, ALU.mult, ALU.add)
                            elif part == "squares":
                                ins = nc.vector.tensor_tensor(tmp[:], cen[:], cen[:], ALU.mult)
                            elif part == "squares_sum":
                                ins = nc.vector.tensor_reduce(hvar[:], flat(tmp), AX.X, ALU.add)
                            elif part == "variance":
                                ins = nc.vector.tensor_scalar(hvar[:], hvar[:], 1.0 / HD, EPS, ALU.mult, ALU.add)
                            elif part == "shift":
                                ins = nc.vector.tensor_scalar(hstd[:].bitcast(I32), hvar[:].bitcast(I32), 1, None, ALU.logical_shift_right)
                            elif part == "guess":
                                ins = nc.vector.tensor_scalar(hstd[:].bitcast(I32), hstd[:].bitcast(I32), -1.0, RSQRT_BITS, ALU.mult, ALU.add)
                            elif part == "half":
                                ins = nc.vector.tensor_scalar(hvar[:], hvar[:], -0.5, None, ALU.mult)
                            elif part.startswith("square"):
                                ins = nc.vector.tensor_tensor(hsum[:], hstd[:], hstd[:], ALU.mult)
                            elif part.startswith("times"):
                                ins = nc.vector.tensor_tensor(hsum[:], hsum[:], hvar[:], ALU.mult)
                            elif part.startswith("better"):
                                ins = nc.vector.scalar_tensor_tensor(hstd[:], hsum[:], 1.5, hstd[:], ALU.add, ALU.mult)
                            elif part == "scale":
                                ins = nc.vector.tensor_tensor(flat(cen), flat(cen), wide(hstd), ALU.mult)
                            elif part in ("sin0", "sin1"):
                                half = int(part[-1])
                                cols = slice(half * HH, (half + 1) * HH)
                                ins = nc.vector.tensor_tensor(flat(tmp)[:, :, cols], flat(cen)[:, :, 1 - half:HD:2],
                                                              flat(gsin)[:, :, cols], ALU.mult)
                            elif part == "cos":
                                ins = nc.vector.tensor_tensor(cen[:], cen[:], gcos[:], ALU.mult)
                            elif part == "add":
                                ins = nc.vector.tensor_tensor(cen[:], cen[:], tmp[:], ALU.add)
                            else:
                                if g >= 2:
                                    dve.wait_ge(split_low, 3 * (g - 1))
                                ins = nc.vector.tensor_tensor(rq[:], cen[:], bsum[:], ALU.add)
                            ins.then_inc(rope_steps, 1)

                        for part in PARTS:
                            rope(0, part)
                        done = 0
                        for a in range(3):
                            dve.wait_ge(split_high, a // 2 + 1)
                            lower(nc.vector, a).then_inc(first_low, 1)
                        for i in range(U + LOW_LAG):
                            if i < U:
                                soft.mask_scores(dve, i)
                            if 1 <= i <= U:
                                soft.invert(dve, i - 1)
                            if i >= LOW_LAG:
                                soft.move_low(dve, i - LOW_LAG)
                            g, k = divmod(i, UG)
                            if g < G1 - 1:
                                end = PARTS.index(ROPE_UP_TO[k]) + 1 if k in ROPE_UP_TO else done
                                for part in PARTS[done:end]:
                                    rope(g + 1, part)
                                done = end % len(PARTS)

                    @block.gpsimd
                    def _(pool):
                        v = qkv[:, :, 2 * D:3 * D].rearrange("p t (h d) -> p t h d", d=HD)
                        pool.wait_ge(v_high, 1)
                        for t in range(T):
                            nc.gpsimd.tensor_tensor(v_pad[:, t, :, HD:2 * HD], v[:, t], f32(v_pad[:, t, :, 0:HD]),
                                                    ALU.subtract).then_inc(v_low, 1)
                        for i in range(U + 1):
                            if i >= 1:
                                soft.norm(pool, i - 1)
                            if BIAS_AT <= i < BIAS_AT + T:
                                t = i - BIAS_AT
                                nc.gpsimd.tensor_tensor(xb[:, t, :], xa[:, t, :], b_o[:], ALU.add).then_inc(biased, 1)
                            g, k = divmod(i, UG)
                            if g < G1 - 1:
                                a = k - SPLIT_AT
                                if 0 <= a < 3:
                                    pool.wait_ge(split_high, 2 * (g + 1) + a // 2 + 1)
                                    lower(nc.gpsimd, a).then_inc(split_low, 1)
                            if i in SCATTER_AT:
                                scatter(SCATTER_AT[i])

                    @block.scalar
                    def _(act):
                        def split_upper(g):
                            act.wait_ge(rope_steps, len(PARTS) * (g + 1))
                            if g:
                                act.wait_ge(qk_turned, 3 * g)
                            nc.scalar.copy(tok[:, :, 0:2, :, 0:HD].rearrange("p t a h d -> p t (a h) d"), rq[:]).then_inc(split_high, 1)
                            nc.scalar.copy(tok[:, :, 2, :, HD:2 * HD], rq[:, :, GH:2 * GH, :]).then_inc(split_high, 1)

                        def move_qk(g, a):
                            act.wait_ge(qk_turned, 3 * g + a + 1)
                            if g >= 2:
                                act.wait_ge(soft.scored, UG * (g - 1))
                            nc.scalar.copy(qkT[:, g % 2, a, :], bank[:, turn_bank(g, a), :]).then_inc(qk_moved, 1)

                        def store(h):
                            g, i = divmod(h, GH)
                            act.wait_ge(soft.valued, T * (h + 1))
                            nc.scalar.copy(o1T[SLOT * i:SLOT * (i + 1), g, :], bank[0:SLOT, O_BANK + h % 2, :]).then_inc(stored, 1)

                        nc.scalar.copy(v_pad[:, :, :, 0:HD], qkv[:, :, 2 * D:3 * D].rearrange("p t (h d) -> p t h d", d=HD)
                                       ).then_inc(v_high, 1)
                        split_upper(0)
                        for a in range(3):
                            move_qk(0, a)
                        for i in range(STEPS + 1):
                            if i < U:
                                soft.exp(act, i)
                            g, k = divmod(i, UG)
                            if g < G1 - 1:
                                if k == SPLIT_AT:
                                    split_upper(g + 1)
                                if TURN_AT <= k < TURN_AT + 3:
                                    move_qk(g + 1, k - TURN_AT)
                            if HIGH_LAG <= i < U + HIGH_LAG:
                                soft.move_high(act, i - HIGH_LAG)
                            if head_out(i, 1) is not None:
                                store(head_out(i, 1))

                    @block.tensor
                    def _(pe):
                        def turn_qk(g, a):
                            if g == 0:
                                pe.wait_ge(first_low, a + 1)
                            else:
                                pe.wait_ge(split_low, 3 * (g - 1) + a + 1)
                                pe.wait_ge(qk_moved, 3 * g + a)
                            for t in range(T):
                                mm = nc.tensor.transpose(bank[:, turn_bank(g, a), t * P:(t + 1) * P],
                                                         f32(tok[:, t, a, :, :].rearrange("p h d -> p (h d)")), ident[:])
                            mm.then_inc(qk_turned, 1)

                        def scores(u):
                            h, t = divmod(u, T)
                            g, i = divmod(h, GH)
                            if u % UG == 0:
                                pe.wait_ge(qk_moved, 3 * (g + 1))
                            if u >= 2:
                                pe.wait_ge(soft.masked, u - 1)
                            part = slice(SLOT * i, SLOT * (i + 1))
                            n = max(soft.keys(u), 2 * P)
                            for k in (1, 2):
                                mm = nc.tensor.matmul(bank[:, S_BANK + u % 2, 0:n], qkT[part, g % 2, 0, t * P:(t + 1) * P],
                                                      qkT[part, g % 2, k, 0:n], start=(k == 1), stop=(k == 2))
                            mm.then_inc(soft.scored, 1)

                        for a in range(3):
                            turn_qk(0, a)
                        for i in range(STEPS):
                            if i < U:
                                scores(i)
                            if TURN_LAG <= i < U + TURN_LAG:
                                soft.turn(pe, i - TURN_LAG)
                            for h, kt in values_at(i):
                                if h == 0:
                                    pe.wait_ge(v_low, T)
                                if kt == 0 and h >= 2:
                                    pe.wait_ge(stored, h - 1)
                                soft.values(pe, h, kt, v_pad[:, kt, h, :], SLOT, True)
                            g, k = divmod(i, UG)
                            if g < G1 - 1 and TURN_AT <= k < TURN_AT + 3:
                                turn_qk(g + 1, k - TURN_AT)
                nc.all_engine_barrier(sems_to_clear=range(first.num, last.num + 1))

            def project_pair(w, src, j, ks=range(KD)):
                for k in ks:
                    mm = nc.tensor.matmul(bank[:, J_BANK, :], w[:, k, j * P:(j + 1) * P], src[:, k, :],
                                          start=(k == 0), stop=(k == KD - 1))
                return mm

            LOWER, UPPER = slice(0, P // 2), slice(P // 2, P)

            def k_high(j, done):
                for i, part in enumerate((LOWER, UPPER)):
                    nc.scalar.copy(kH[part, j % 2, i, :], bank[part, J_BANK, :]).then_inc(done, 1)

            def k_low(j, done):
                for i, part in enumerate((LOWER, UPPER)):
                    nc.vector.tensor_tensor(kL[part, j % 2, :], bank[part, J_BANK, :], f32(kH[part, j % 2, i, :]),
                                            ALU.subtract).then_inc(done, 1)

            def k_twice(sp, j, done):
                for i, (src, dst) in enumerate(((LOWER, UPPER), (UPPER, LOWER))):
                    sp.dma_start(f32(kH[dst, j % 2, i, :]), f32(kH[src, j % 2, i, :])).then_inc(done, 16)

            def middle(v2s):
                with ExitStack() as stage:
                    def sem(name):
                        return stage.enter_context(nc.semaphore("m_" + name))

                    first = projected = sem("projected")
                    added, steps, root, xn_ready = sem("added"), sem("steps"), sem("root"), sem("xn_ready")
                    turned, moved, v_made, v_high, v_low = sem("turned"), sem("moved"), sem("v_made"), sem("v_high"), sem("v_low")
                    k_made, k_is_high, k_is_low, k_is_twice = sem("k_made"), sem("k_high"), sem("k_low"), sem("k_twice")
                    last = k_is_twice
                    block = stage.enter_context(nc.Block())
                    VJ = 2 * T

                    @block.sync
                    def _(sp):
                        sp.wait_ge(k_is_high, 2)
                        k_twice(sp, 0, k_is_twice)
                        sp.wait_ge(k_is_twice, 32)

                    @block.gpsimd
                    def _(pool):
                        ln_pool(pool, steps, root)

                    @block.tensor
                    def _(pe):
                        for t in range(T):
                            for g in range(G1):
                                mm = nc.tensor.matmul(bank[:, t, 0:D], o1T[:, g, t * P:(t + 1) * P], w_o1[:, g, :],
                                                      start=(g == 0), stop=(g == G1 - 1))
                            mm.then_inc(projected, 1)
                            if t == 0:
                                for k in range(KD):
                                    for tt in range(T):
                                        mm = nc.tensor.transpose(bank[:, 4 + k, tt * P:(tt + 1) * P], cb[:, tt, k * P:(k + 1) * P], ident[:])
                                    mm.then_inc(turned, 1)
                        pe.wait_ge(moved, KD)
                        project_pair(w_k2, cT, 0).then_inc(k_made, 1)
                        for n in range(VJ):
                            t, half = divmod(n, 2)
                            if n >= 2:
                                pe.wait_ge(v_low, n - 1)
                            elif n == 1:
                                pe.wait_ge(k_is_low, 2)
                            for k in range(KD):
                                mm = nc.tensor.matmul(bank[:, 6 + n % 2, :], cT[:, k, t * P:(t + 1) * P],
                                                      w_v2[:, k, half * 512:(half + 1) * 512], start=(k == 0), stop=(k == KD - 1))
                            mm.then_inc(v_made, 1)
                        for k in range(KD):
                            for t in range(T):
                                if k == 0:
                                    pe.wait_ge(xn_ready, t + 1)
                                mm = nc.tensor.transpose(bank[:, 4 + k, t * P:(t + 1) * P], xn[:, t, k * P:(k + 1) * P], ident[:])
                            mm.then_inc(turned, 1)

                    def v_half(n, side):
                        t, half = divmod(n, 2)
                        heads = H // 2
                        return v2s[:, t, half * heads:(half + 1) * heads, side * HD2:(side + 1) * HD2]

                    @block.scalar
                    def _(act):
                        for k in range(KD):
                            act.wait_ge(turned, k + 1)
                            nc.scalar.copy(cT[:, k, :], bank[:, 4 + k, :]).then_inc(moved, 1)
                        act.wait_ge(k_made, 1)
                        k_high(0, k_is_high)
                        for n in range(VJ):
                            act.wait_ge(v_made, n + 1)
                            nc.scalar.copy(v_half(n, 0), bank[:, 6 + n % 2, :].rearrange("p (h d) -> p h d", d=HD2)).then_inc(v_high, 1)
                        for k in range(KD):
                            act.wait_ge(turned, KD + k + 1)
                            nc.scalar.copy(xT[:, k, :], bank[:, 4 + k, :]).then_inc(moved, 1)

                    @block.vector
                    def _(dve):
                        def v_lower(n):
                            dve.wait_ge(v_high, n + 1)
                            nc.vector.tensor_tensor(v_half(n, 1), bank[:, 6 + n % 2, :].rearrange("p (h d) -> p h d", d=HD2),
                                                    f32(v_half(n, 0)), ALU.subtract).then_inc(v_low, 1)

                        for t in range(T):
                            dve.wait_ge(projected, t + 1)
                            nc.vector.tensor_tensor(xb[:, t, :], bank[:, t, 0:D], xb[:, t, :], ALU.add).then_inc(added, 1)
                        dve.wait_ge(k_is_high, 2)
                        k_low(0, k_is_low)
                        v_lower(0)
                        v_lower(1)
                        ln_vector(dve, xb, xn, lambda t: dve.wait_ge(added, t + 1),
                                  lambda: dve.wait_ge(scattered, 16 * T * TOP * b + 16 * (SPARE_TILES + T * TOP)),
                                  steps, root, xn_ready)
                        for n in range(2, VJ):
                            v_lower(n)
                nc.all_engine_barrier(sems_to_clear=range(first.num, last.num + 1))

            def cross_attention(v2s):
                with ExitStack() as stage:
                    def sem(name):
                        return stage.enter_context(nc.semaphore("c_" + name))

                    def ss(name, shape, dt=F32):
                        return stage.enter_context(nc.sbuf_tensor(name, shape, dt))

                    qS = ss("qS", [P, 2, 2, S], F32R)
                    out_low = ss("out_low", [P // 2, S])

                    first = x_in = sem("x_in")
                    q_made, q_high, q_low = sem("q_made"), sem("q_high"), sem("q_low")
                    k_made, k_is_high, k_is_low = sem("k_made"), sem("k_high"), sem("k_low")
                    k_is_twice = [sem("k_twice0"), sem("k_twice1")]
                    soft = Soft(sem, lambda u: S, lambda u: mb[:, u % T, :], 1.0)
                    low_out, stored = sem("low_out"), sem("stored")
                    last = stored
                    block = stage.enter_context(nc.Block())
                    UG = GH2 * T
                    K_AT, Q_AT = 0, UG // 2
                    K_END, Q_END = K_AT + KD - 1, Q_AT + KD - 1

                    @block.sync
                    def _(sp):
                        sp.dma_start(xa[:], x_v[bass.ds(b_next, 1)].rearrange("a p t d -> p (a t) d")).then_inc(x_in, 16)
                        for j in range(1, G2):
                            sp.wait_ge(k_is_high, 2 * j)
                            k_twice(sp, j, k_is_twice[j % 2])
                        sp.wait_ge(x_in, 16)

                    @block.tensor
                    def _(pe):
                        def scores(u):
                            h, t = divmod(u, T)
                            j, i = divmod(h, GH2)
                            if u % UG == 0:
                                pe.wait_ge(q_low, 2 * (j + 1))
                                if j:
                                    pe.wait_ge(k_is_low, 2 * j)
                                    pe.wait_ge(k_is_twice[j % 2], 32 * ((j + 1) // 2))
                            if u >= 2:
                                pe.wait_ge(soft.masked, u - 1)
                            mine = (LOWER, UPPER)[i]
                            dst = bank[:, S_BANK + u % 2, :]
                            q = qS[:, j % 2, i, t * P:(t + 1) * P]
                            nc.tensor.matmul(dst, q, kH[:, j % 2, i, :], start=True, stop=False)
                            nc.tensor.matmul(dst, q[mine], kL[mine, j % 2, :], start=False, stop=True).then_inc(soft.scored, 1)

                        project_pair(w_q2, xT, 0).then_inc(q_made, 1)
                        for i in range(STEPS):
                            if i < U:
                                scores(i)
                            if TURN_LAG <= i < U + TURN_LAG:
                                soft.turn(pe, i - TURN_LAG)
                            j, k = divmod(i, UG)
                            if j < G2 - 1 and K_AT <= k <= K_END:
                                if k == K_AT and j:
                                    pe.wait_ge(q_low, 2 * (j + 1))
                                mm = project_pair(w_k2, cT, j + 1, [k - K_AT])
                                if k == K_END:
                                    mm.then_inc(k_made, 1)
                            if j < G2 - 1 and Q_AT <= k <= Q_END:
                                if k == Q_AT:
                                    pe.wait_ge(k_is_low, 2 * (j + 1))
                                mm = project_pair(w_q2, xT, j + 1, [k - Q_AT])
                                if k == Q_END:
                                    mm.then_inc(q_made, 1)
                            for h, kt in values_at(i):
                                if kt == 0 and h >= 2:
                                    pe.wait_ge(stored, h - 1)
                                soft.values(pe, h, kt, v2s[:, kt, h, :], P, False)

                    @block.scalar
                    def _(act):
                        def q_upper(j):
                            act.wait_ge(q_made, j + 1)
                            if j >= 2:
                                act.wait_ge(soft.scored, UG * (j - 1))
                            for i, part in enumerate((LOWER, UPPER)):
                                nc.scalar.copy(qS[part, j % 2, i, :], bank[part, J_BANK, :]).then_inc(q_high, 1)

                        def k_upper(j):
                            act.wait_ge(k_made, j)
                            if j >= 2:
                                act.wait_ge(soft.scored, UG * (j - 1))
                            k_high(j, k_is_high)

                        def lower_out(h):
                            act.wait_ge(soft.valued, T * (h + 1))
                            if h:
                                act.wait_ge(stored, h)
                            nc.scalar.copy(out_low[:], bank[UPPER, O_BANK + h % 2, :]).then_inc(low_out, 1)

                        q_upper(0)
                        for i in range(STEPS + 1):
                            if i < U:
                                soft.exp(act, i)
                            if HIGH_LAG <= i < U + HIGH_LAG:
                                soft.move_high(act, i - HIGH_LAG)
                            j, k = divmod(i, UG)
                            if j < G2 - 1 and k == K_END:
                                k_upper(j + 1)
                            if j < G2 - 1 and k == Q_END:
                                q_upper(j + 1)
                            if head_out(i, 1) is not None:
                                lower_out(head_out(i, 1))

                    @block.vector
                    def _(dve):
                        def q_lower(j):
                            for i, (src, dst) in enumerate(((LOWER, UPPER), (UPPER, LOWER))):
                                dve.wait_ge(q_high, 2 * j + i + 1)
                                nc.vector.tensor_tensor(qS[dst, j % 2, i, :], bank[src, J_BANK, :], f32(qS[src, j % 2, i, :]),
                                                        ALU.subtract).then_inc(q_low, 1)

                        def k_lower(j):
                            dve.wait_ge(k_is_high, 2 * j)
                            k_low(j, k_is_low)

                        def store(h):
                            dve.wait_ge(low_out, h + 1)
                            nc.vector.tensor_tensor(o2T[(LOWER, UPPER)[h % 2], h // 2, :], bank[LOWER, O_BANK + h % 2, :],
                                                    out_low[:], ALU.add).then_inc(stored, 1)

                        q_lower(0)
                        for i in range(STEPS + 2):
                            if i < U:
                                soft.mask_scores(dve, i)
                            if 1 <= i <= U:
                                soft.invert(dve, i - 1)
                            if LOW_LAG <= i < U + LOW_LAG:
                                soft.move_low(dve, i - LOW_LAG)
                            j, k = divmod(i, UG)
                            if j < G2 - 1 and k == K_END + 1:
                                k_lower(j + 1)
                            if j < G2 - 1 and k == Q_END + 1:
                                q_lower(j + 1)
                            if head_out(i, 2) is not None:
                                store(head_out(i, 2))

                    @block.gpsimd
                    def _(pool):
                        for u in range(U):
                            soft.norm(pool, u)
                nc.all_engine_barrier(sems_to_clear=range(first.num, last.num + 1))

            def route():
                with ExitStack() as stage:
                    def sem(name):
                        return stage.enter_context(nc.semaphore("r_" + name))

                    xna = stage.enter_context(nc.sbuf_tensor("xna", [P, T, D], F32))
                    xTa = stage.enter_context(nc.sbuf_tensor("xTa", [P, KD, S], F32))
                    first = projected = sem("projected")
                    added, steps, root, xn_ready = sem("added"), sem("steps"), sem("root"), sem("xn_ready")
                    steps_a, root_a, xna_ready = sem("steps_a"), sem("root_a"), sem("xna_ready")
                    turned, moved, logits, picked, exped = sem("turned"), sem("moved"), sem("logits"), sem("picked"), sem("exped")
                    turned_a, moved_a, qkv_made, qkv_moved = sem("turned_a"), sem("moved_a"), sem("qkv_made"), sem("qkv_moved")
                    chosen_ready, ranked, slotted, saved = sem("chosen"), sem("ranked"), sem("slotted"), sem("saved")
                    last = saved
                    block = stage.enter_context(nc.Block())
                    ROUTER_BANK, RANK_BANK, TOTAL_BANK = 0, 1, 2

                    @block.sync
                    def _(sp):
                        sp.wait_ge(added, T)
                        sp.dma_start(out_b[bass.ds(b, 1)].rearrange("a p t d -> p (a t) d"), xb[:]).then_inc(saved, 16)
                        sp.wait_ge(saved, 16)

                    @block.gpsimd
                    def _(pool):
                        ln_pool(pool, steps_a, root_a)
                        ln_pool(pool, steps, root)

                    @block.tensor
                    def _(pe):
                        def turn(src, ready, done):
                            for k in range(KD):
                                for t in range(T):
                                    if k == 0:
                                        pe.wait_ge(ready, t + 1)
                                    mm = nc.tensor.transpose(bank[:, 4 + k, t * P:(t + 1) * P], src[:, t, k * P:(k + 1) * P], ident[:])
                                mm.then_inc(done, 1)

                        def project(n):
                            t, (lo, hi) = n // 2, QKV_PARTS[n % 2]
                            if n >= 2:
                                pe.wait_ge(qkv_moved, n - 1)
                            for k in range(KD):
                                mm = nc.tensor.matmul(bank[:, 6 + n % 2, 0:hi - lo], xTa[:, k, t * P:(t + 1) * P], w_qkv[:, k, lo:hi],
                                                      start=(k == 0), stop=(k == KD - 1))
                            mm.then_inc(qkv_made, 1)

                        for t in range(T):
                            for j in range(G2):
                                mm = nc.tensor.matmul(bank[:, t, 0:D], o2T[:, j, t * P:(t + 1) * P], w_o2[:, j, :],
                                                      start=(j == 0), stop=(j == G2 - 1))
                            mm.then_inc(projected, 1)
                            if t == 1:
                                turn(xna, xna_ready, turned_a)
                        pe.wait_ge(moved_a, KD)
                        for n in range(T):
                            project(n)
                        turn(xn, xn_ready, turned)
                        project(T)
                        pe.wait_ge(moved, KD)
                        for t in range(T):
                            for k in range(KD):
                                mm = nc.tensor.matmul(bank[:, ROUTER_BANK, t * NE:(t + 1) * NE], xT[:, k, t * P:(t + 1) * P],
                                                      w_g[:, k, :], start=(k == 0), stop=(k == KD - 1))
                        mm.then_inc(logits, 1)
                        for n in range(T + 1, 2 * T):
                            project(n)
                        pe.wait_ge(chosen_ready, 1)
                        flat = either[:].rearrange("p t e -> p (t e)")
                        nc.tensor.matmul(bank[:, RANK_BANK, 0:T * NE], before[:], flat, start=True, stop=True)
                        nc.tensor.matmul(bank[:, TOTAL_BANK, 0:T * NE], ones[:], flat, start=True, stop=True).then_inc(ranked, 1)

                    @block.scalar
                    def _(act):
                        def move(n):
                            t, (lo, hi) = n // 2, QKV_PARTS[n % 2]
                            act.wait_ge(qkv_made, n + 1)
                            nc.scalar.copy(qkv[:, t, lo:hi], bank[:, 6 + n % 2, 0:hi - lo]).then_inc(qkv_moved, 1)

                        for k in range(KD):
                            act.wait_ge(turned_a, k + 1)
                            nc.scalar.copy(xTa[:, k, :], bank[:, 4 + k, :]).then_inc(moved_a, 1)
                        for n in range(T):
                            move(n)
                        for k in range(KD):
                            act.wait_ge(turned, k + 1)
                            nc.scalar.copy(xT[:, k, :], bank[:, 4 + k, :]).then_inc(moved, 1)
                        move(T)
                        move(T + 1)
                        act.wait_ge(picked, 3)
                        for t in range(T):
                            nc.scalar.activation(ew[:, t, :], top[:, t, 0:TOP], ACT.Exp, bias=ntop[:, t:t + 1], scale=1.0
                                                 ).then_inc(exped, 1)
                        for n in range(T + 2, 2 * T):
                            move(n)

                    @block.vector
                    def _(dve):
                        ln_vector(dve, xa, xna, lambda t: None, lambda: None, steps_a, root_a, xna_ready)
                        for t in range(T):
                            dve.wait_ge(projected, t + 1)
                            nc.vector.tensor_tensor(xb[:, t, :], bank[:, t, 0:D], xb[:, t, :], ALU.add).then_inc(added, 1)
                        ln_vector(dve, xb, xn, lambda t: dve.wait_ge(added, t + 1), lambda: dve.wait_ge(xna_ready, T),
                                  steps, root, xn_ready)
                        n = 0

                        def step(ins):
                            nonlocal n
                            n += 1
                            ins.then_inc(picked, 1)
                            dve.wait_ge(picked, n)

                        dve.wait_ge(logits, 1)
                        step(nc.vector.tensor_copy(logit[:].rearrange("p t e -> p (t e)"), bank[:, ROUTER_BANK, 0:T * NE]))
                        for t in range(T):
                            nc.vector.max(top[:, t, :], logit[:, t, :])
                        step(nc.vector.drain())
                        step(nc.vector.tensor_scalar(ntop[:], top[:, :, 0], -1.0, None, ALU.mult))
                        for t in range(T):
                            nc.vector.max_index(topi[:, t, :], top[:, t, :], logit[:, t, :])
                        step(nc.vector.drain())
                        step(nc.vector.tensor_copy(topf[:], topi[:]))
                        for j in range(TOP):
                            for t in range(T):
                                nc.vector.tensor_scalar(chosen[:, j, t, :], expert_no[:], topf[:, t, j:j + 1], None, ALU.is_equal)
                        step(nc.vector.drain())
                        nc.vector.tensor_tensor(either[:], chosen[:, 0], chosen[:, 1], ALU.add).then_inc(chosen_ready, 1)
                        dve.wait_ge(exped, T)
                        step(nc.vector.tensor_tensor(esum[:], ew[:, :, 0], ew[:, :, 1], ALU.add))
                        step(nc.vector.reciprocal(esum[:], esum[:]))
                        nc.vector.tensor_tensor(share[:, bass.ds(b * T, T), :], ew[:], esum[:, :, None].to_broadcast([P, T, TOP]),
                                                ALU.mult)
                        dve.wait_ge(ranked, 1)
                        step(nc.vector.tensor_copy(total[:].rearrange("p t e -> p (t e)"), bank[:, TOTAL_BANK, 0:T * NE]))
                        for t in range(T):
                            step(nc.vector.tensor_tensor(rank[:, t, :], used[:], region[:], ALU.add))
                            step(nc.vector.tensor_tensor(used[:], used[:], total[:, t, :], ALU.add))
                        step(nc.vector.tensor_tensor(rank[:].rearrange("p t e -> p (t e)"), bank[:, RANK_BANK, 0:T * NE],
                                                     rank[:].rearrange("p t e -> p (t e)"), ALU.add))
                        for j in range(TOP):
                            step(nc.vector.tensor_tensor(picked_row[:, j], chosen[:, j], rank[:], ALU.mult))
                            step(nc.vector.tensor_reduce(slot_f[:, j, :], picked_row[:, j], AX.X, ALU.add))
                        nc.vector.tensor_copy(batch_slot[:], slot_f[:]).then_inc(slotted, 1)
                        nc.vector.tensor_copy(xs_row[:, :, bass.ds(b * T, T)], slot_f[:])
                        for j in range(TOP):
                            nc.vector.tensor_copy(choice[:, j, bass.ds(b * T, T), :], chosen[:, j])
                nc.all_engine_barrier(sems_to_clear=range(first.num, last.num + 1))

            with nc.Fori(0, B) as b:
                b_next = (b + 1) % B
                self_attention()
                with ExitStack() as cross:
                    v2s = cross.enter_context(nc.sbuf_tensor("v2s", [P, T, H, 2 * HD2], F32R))
                    middle(v2s)
                    cross_attention(v2s)
                route()

        with ExitStack() as moe:
            def sm(name, shape, dt=F32):
                return moe.enter_context(nc.sbuf_tensor(name, shape, dt))

            w_raw = sm("w_raw", [P, 2, KD, F2])
            w_guH = sm("w_guH", [P, NE * KD, F2], F32R)
            w_guL = sm("w_guL", [P, NE * KD, F2], F32R)
            w_dn = sm("w_dn", [P, NE * FT, D])
            pad_f = sm("pad_f", [P, NE])
            pad_row = sm("pad_row", [P, NE], U32)
            tiles_f = sm("tiles_f", [P, NE])
            tiles_i = sm("tiles_i", [P, NE], U32)
            ends = sm("ends", [P, NE])
            tile_no = sm("tile_no", [P, TILES])
            past = sm("past", [P, TILES, NE])
            skipped = sm("skipped", [P, TILES, NE])
            t_expert = sm("t_expert", [P, TILES])
            t_start = sm("t_start", [P, TILES])
            t_row = sm("t_row", [P, TILES])
            expert_of = sm("expert_of", [P, TILES], U32)
            row_of = sm("row_of", [P, TILES], U32)
            shift = sm("shift", [P, NE])
            shifted = sm("shifted", [P, NT, NE])
            ys_row_f = sm("ys_row_f", [P, TOP, NT])
            xs = sm("xs", [P, 2, D])
            xsH = sm("xsH", [P, 2, KD * P], F32R)
            xsL = sm("xsL", [P, 2, KD * P], F32R)
            sil = sm("sil", [P, 2, F])
            hid = sm("hid", [P, 2, F])
            hidT = sm("hidT", [P, 2, F])
            ys = sm("ys", [P, 2, D])

            with ExitStack() as sems:
                def sem(name):
                    return sems.enter_context(nc.semaphore(name))

                w0_in, w0_high, w_steps, w_ready = sem("w0_in"), sem("w0_high"), sem("w_steps"), sem("w_ready")
                w_in = [sem("w_in0"), sem("w_in1")]
                pad_steps, pad_ready, padded = sem("pad_steps"), sem("pad_ready"), sem("padded")
                map_steps, map_ready, no_set = sem("map_steps"), sem("map_ready"), sem("no_set")
                loaded = [sem("loaded0"), sem("loaded1")]
                stored = [sem("stored0"), sem("stored1")]
                turned, xs_high, xs_low, gated, upped = sem("e_turned"), sem("xs_high"), sem("xs_low"), sem("gated"), sem("upped")
                silued, hidden, h_turned, hidT_ready = sem("silued"), sem("hidden"), sem("h_turned"), sem("hidT_ready")
                downed, ys_ready = sem("downed"), sem("ys_ready")
                block = sems.enter_context(nc.Block())
                XT_BANK, GATE_BANK, UP_BANK, HT_BANK, DOWN_BANK = 0, 1, 3, 5, 6
                PAIRS = TILES // 2

                def raw(e):
                    return ((w_raw[:, e % 2], gate_up_w[e].rearrange("(k p) f -> p k f", p=P)),
                            (w_dn[:, e * FT:(e + 1) * FT], down_w[e].rearrange("(k p) f -> p k f", p=P)))

                def upper(engine, e):
                    return engine(w_guH[:, e * KD:(e + 1) * KD, :], w_raw[:, e % 2])

                def lower(engine, e):
                    return engine.tensor_tensor(w_guL[:, e * KD:(e + 1) * KD, :], w_raw[:, e % 2],
                                                f32(w_guH[:, e * KD:(e + 1) * KD, :]), ALU.subtract)

                @block.sync
                def _(sp):
                    for dst, src in raw(0):
                        sp.dma_start(dst, src).then_inc(w0_in, 16)
                    sp.wait_ge(pad_ready, 1)
                    for e in range(NE):
                        row = sp.value_load(pad_row[0:1, e:e + 1], min_val=0, max_val=SPARE - P)
                        sp.dma_start(xs_dram[bass.ds(row, P), :], zeros[:]).then_inc(padded, 16)
                    sp.wait_ge(padded, 16 * NE)
                    sp.wait_ge(scattered, 16 * (SPARE_TILES + T * TOP * (B + 1)))
                    sp.wait_ge(map_ready, 1)

                    def load(i, q):
                        row = sp.value_load(row_of[0:1, bass.ds(i, 1)], min_val=0, max_val=ROWS - P)
                        sp.dma_start(xs[:, q, :], xs_dram[bass.ds(row, P), :]).then_inc(loaded[q], 16)

                    def load_next(it):
                        for q in range(2):
                            sp.wait_ge(turned, 2 * it + q + 1)
                            load(2 * it + q + 2, q)

                    def store(it):
                        for q in range(2):
                            sp.wait_ge(ys_ready, 2 * it + q + 3)
                            sp.dma_start(ys_dram[bass.ds((2 * it + q) * P, P), :], ys[:, q, :]).then_inc(stored[q], 16)

                    load(0, 0)
                    load(1, 1)
                    for q in range(2):
                        sp.sem_inc(stored[q], 16)
                    load_next(0)
                    with sp.Fori(1, PAIRS - 1) as it:
                        load_next(it)
                        store(it - 1)
                    store(PAIRS - 2)
                    store(PAIRS - 1)
                    for q in range(2):
                        sp.wait_ge(stored[q], 16 * (PAIRS + 1))

                @block.gpsimd
                def _(pool):
                    pool.iota(tile_no[:], [[1, TILES]], base=0, channel_multiplier=0,
                              allow_small_or_imprecise_dtypes=True).then_inc(no_set, 1)
                    for n in range(T * TOP):
                        scatter(n)

                    def fetch(e):
                        for dst, src in raw(e):
                            pool.dma_start(dst, src).then_inc(w_in[e % 2], 16)

                    pool.wait_ge(turned, 1)
                    fetch(1)
                    pool.wait_ge(w_ready, 1)
                    for e in range(1, NE):
                        if e + 1 < NE:
                            fetch(e + 1)
                        pool.wait_ge(w_in[e % 2], 16 * 2 * ((e + 1) // 2))
                        upper(nc.gpsimd.tensor_copy, e).then_inc(w_steps, 1)
                        pool.wait_ge(w_steps, 2 * e - 1)
                        lower(nc.gpsimd, e).then_inc(w_steps, 1)
                        pool.wait_ge(w_steps, 2 * e)
                        pool.sem_inc(w_ready, 1)

                @block.tensor
                def _(pe):
                    def turn(i, q):
                        pe.wait_ge(loaded[q], 16 * i)
                        for k in range(KD):
                            mm = nc.tensor.transpose(bank[:, XT_BANK, k * P:(k + 1) * P], xs[:, q, k * P:(k + 1) * P], ident[:])
                        mm.then_inc(turned, 1)

                    def expert(i):
                        return pe.value_load(expert_of[0:1, bass.ds(i, 1)], min_val=0, max_val=NE - 1)

                    def widen(q, e, first_bank, column, done):
                        products = [(x, w, k) for k in range(KD) for x, w in ((xsH, w_guH), (xsH, w_guL), (xsL, w_guH))]
                        for n, (x, w, k) in enumerate(products):
                            mm = nc.tensor.matmul(bank[:, first_bank + q, :], x[:, q, k * P:(k + 1) * P],
                                                  w[:, bass.ds(e * KD + k, 1), column:column + F].rearrange("p a f -> p (a f)"),
                                                  start=(n == 0), stop=(n == len(products) - 1))
                        mm.then_inc(done, 1)

                    def turn_hidden(i, q):
                        pe.wait_ge(hidden, i + 2)
                        for f in range(FT):
                            mm = nc.tensor.transpose(bank[:, HT_BANK, f * P:(f + 1) * P], hid[:, q, f * P:(f + 1) * P], ident[:])
                        mm.then_inc(h_turned, 1)

                    def down(i, q, e):
                        pe.wait_ge(hidT_ready, i + 1)
                        pe.wait_ge(ys_ready, i + 1)
                        for f in range(FT):
                            mm = nc.tensor.matmul(bank[:, DOWN_BANK + q, 0:D], hidT[:, q, f * P:(f + 1) * P],
                                                  w_dn[:, bass.ds(e * FT + f, 1), :].rearrange("p a d -> p (a d)"),
                                                  start=(f == 0), stop=(f == FT - 1))
                        mm.then_inc(downed, 1)

                    pe.wait_ge(map_ready, 1)
                    turn(1, 0)
                    pe.wait_ge(xs_low, 1)
                    e = expert(0)
                    pe.wait_ge(w_ready, e + 1)
                    widen(0, e, GATE_BANK, 0, gated)
                    turn(1, 1)
                    widen(0, e, UP_BANK, F, upped)

                    def tile_step(it, j, last=False):
                        i = 2 * it + j
                        q, r = j, 1 - j
                        e, e_next = expert(i), expert(i + 1)
                        pe.wait_ge(xs_low, i + 2)
                        pe.wait_ge(w_ready, e_next + 1)
                        widen(r, e_next, GATE_BANK, 0, gated)
                        turn_hidden(i, q)
                        if not last:
                            turn(it + 2, q)
                        widen(r, e_next, UP_BANK, F, upped)
                        down(i, q, e)

                    with pe.Fori(0, PAIRS - 1) as it:
                        tile_step(it, 0)
                        tile_step(it, 1)
                    tile_step(PAIRS - 1, 0, last=True)
                    turn_hidden(TILES - 1, 1)
                    down(TILES - 1, 1, expert(TILES - 1))

                @block.scalar
                def _(act):
                    def move_x(i, q):
                        act.wait_ge(turned, i + 1)
                        nc.scalar.copy(xsH[:, q, :], bank[:, XT_BANK, 0:KD * P]).then_inc(xs_high, 1)

                    def silu(i, q):
                        act.wait_ge(gated, i + 1)
                        act.wait_ge(hidden, i)
                        nc.scalar.activation(sil[:, q, :], bank[:, GATE_BANK + q, :], ACT.Silu).then_inc(silued, 1)

                    def move_y(it, j):
                        act.wait_ge(downed, 2 * it + j + 1)
                        act.wait_ge(stored[j], 16 * it + 16)
                        nc.scalar.copy(ys[:, j, :], bank[:, DOWN_BANK + j, 0:D]).then_inc(ys_ready, 1)

                    act.wait_ge(w0_in, 32)
                    upper(nc.scalar.copy, 0).then_inc(w0_high, 1)
                    act.sem_inc(ys_ready, 2)
                    move_x(0, 0)
                    act.wait_ge(gated, 1)
                    nc.scalar.activation(sil[:, 0, :], bank[:, GATE_BANK, :], ACT.Silu).then_inc(silued, 1)
                    move_x(1, 1)
                    with act.Fori(0, PAIRS - 1) as it:
                        for j in range(2):
                            silu(2 * it + j + 1, 1 - j)
                            move_x(2 * it + j + 2, j)
                            move_y(it, j)
                    silu(TILES - 1, 1)
                    move_y(PAIRS - 1, 0)
                    move_y(PAIRS - 1, 1)

                @block.vector
                def _(dve):
                    n = 0

                    def step(ins):
                        nonlocal n
                        n += 1
                        ins.then_inc(map_steps, 1)
                        dve.wait_ge(map_steps, n)

                    nc.vector.tensor_tensor(pad_f[:], used[:], region[:], ALU.add).then_inc(pad_steps, 1)
                    dve.wait_ge(pad_steps, 1)
                    nc.vector.tensor_copy(pad_row[:], pad_f[:]).then_inc(pad_ready, 1)
                    LOG_P = P.bit_length() - 1
                    step(nc.vector.tensor_scalar(tiles_f[:], used[:], float(P - 1), None, ALU.add))
                    step(nc.vector.tensor_copy(tiles_i[:], tiles_f[:]))
                    step(nc.vector.tensor_scalar(tiles_i[:], tiles_i[:], LOG_P, None, ALU.logical_shift_right))
                    step(nc.vector.tensor_copy(tiles_f[:], tiles_i[:]))
                    step(nc.vector.tensor_copy(ends[:], tiles_f[:]))
                    for e in range(1, NE):
                        step(nc.vector.tensor_tensor(ends[:, e:e + 1], ends[:, e:e + 1], ends[:, e - 1:e], ALU.add))
                    dve.wait_ge(no_set, 1)
                    shape = [P, TILES, NE]
                    step(nc.vector.tensor_tensor(past[:], tile_no[:, :, None].to_broadcast(shape), ends[:, None, :].to_broadcast(shape),
                                                 ALU.is_ge))
                    step(nc.vector.tensor_reduce(t_expert[:], past[:], AX.X, ALU.add))
                    step(nc.vector.tensor_tensor(skipped[:], past[:], tiles_f[:, None, :].to_broadcast(shape), ALU.mult))
                    step(nc.vector.tensor_reduce(t_start[:], skipped[:], AX.X, ALU.add))
                    step(nc.vector.tensor_tensor(t_row[:], tile_no[:], t_start[:], ALU.subtract))
                    step(nc.vector.tensor_scalar(t_row[:], t_row[:], float(P), None, ALU.mult))
                    step(nc.vector.scalar_tensor_tensor(t_row[:], t_expert[:], float(REGION), t_row[:], ALU.mult, ALU.add))
                    step(nc.vector.tensor_scalar(t_expert[:], t_expert[:], float(NE - 1), None, ALU.min))
                    step(nc.vector.tensor_copy(expert_of[:], t_expert[:]))
                    step(nc.vector.tensor_copy(row_of[:], t_row[:]))
                    dve.sem_inc(map_ready, 1)
                    dve.sem_inc(hidden, 1)

                    def multiply(i, q):
                        dve.wait_ge(silued, i + 1)
                        dve.wait_ge(upped, i + 1)
                        nc.vector.tensor_tensor(hid[:, q, :], bank[:, UP_BANK + q, :], sil[:, q, :], ALU.mult).then_inc(hidden, 1)

                    def move_hidden(i, q):
                        dve.wait_ge(h_turned, i + 1)
                        nc.vector.tensor_copy(hidT[:, q, :], bank[:, HT_BANK, :]).then_inc(hidT_ready, 1)

                    def x_lower(i, q):
                        dve.wait_ge(xs_high, i + 1)
                        nc.vector.tensor_tensor(xsL[:, q, :], bank[:, XT_BANK, 0:KD * P], f32(xsH[:, q, :]), ALU.subtract
                                                ).then_inc(xs_low, 1)

                    dve.wait_ge(w0_high, 1)
                    lower(nc.vector, 0).then_inc(w_ready, 1)
                    x_lower(0, 0)
                    x_lower(1, 1)
                    multiply(0, 0)
                    with dve.Fori(0, PAIRS - 1) as it:
                        for j in range(2):
                            move_hidden(2 * it + j, j)
                            x_lower(2 * it + j + 2, j)
                            multiply(2 * it + j + 1, 1 - j)
                    move_hidden(TILES - 2, 0)
                    multiply(TILES - 1, 1)
                    move_hidden(TILES - 1, 1)

                    step(nc.vector.tensor_tensor(shift[:], ends[:], tiles_f[:], ALU.subtract))
                    step(nc.vector.tensor_scalar(shift[:], shift[:], float(P), None, ALU.mult))
                    step(nc.vector.scalar_tensor_tensor(shift[:], expert_no[:], -float(REGION), shift[:], ALU.mult, ALU.add))
                    for j in range(TOP):
                        step(nc.vector.tensor_tensor(shifted[:], choice[:, j], shift[:, None, :].to_broadcast([P, NT, NE]), ALU.mult))
                        step(nc.vector.tensor_reduce(ys_row_f[:, j, :], shifted[:], AX.X, ALU.add))
                        step(nc.vector.tensor_tensor(ys_row_f[:, j, :], ys_row_f[:, j, :], xs_row[:, j, :], ALU.add))
                    nc.vector.tensor_copy(ys_row[:], ys_row_f[:])

            nc.all_engine_barrier()

        RING = 4
        with ExitStack() as sems:
            def sem(name):
                return sems.enter_context(nc.semaphore(name))

            x_all = sems.enter_context(nc.sbuf_tensor("x_all", [P, NT, D], F32))
            yg = sems.enter_context(nc.sbuf_tensor("yg", [P, RING, TOP, D], F32))
            x_in = [sem(f"x_in{b}") for b in range(B)]

            gathered = [sem(f"gathered{i}") for i in range(RING)]
            combined, out_done = sem("combined"), sem("out_done")
            block = sems.enter_context(nc.Block())

            @block.gpsimd
            def _(pool):
                for t in range(NT):
                    if t >= RING:
                        pool.wait_ge(combined, TOP * (t - RING + 1))
                    for j in range(TOP):
                        pool.indirect_dma_start(
                            out=yg[:, t % RING, j, :], out_offset=None, in_=ys_dram,
                            in_offset=bass.IndirectOffsetOnAxis(ap=ys_row[:, j, t:t + 1], axis=0)).then_inc(gathered[t % RING], 16)

            @block.vector
            def _(dve):
                for t in range(NT):
                    if t % T == 0:
                        dve.wait_ge(x_in[t // T], 16)
                    dve.wait_ge(gathered[t % RING], 16 * TOP * (t // RING + 1))
                    for j in range(TOP):
                        if j:
                            dve.wait_ge(combined, TOP * t + j)
                        nc.vector.scalar_tensor_tensor(x_all[:, t, :], yg[:, t % RING, j, :], share[:, t, j:j + 1],
                                                       x_all[:, t, :], ALU.mult, ALU.add).then_inc(combined, 1)

            @block.sync
            def _(sp):
                for b in range(B):
                    sp.dma_start(x_all[:, b * T:(b + 1) * T, :], out_v[:, b * T:(b + 1) * T, :]).then_inc(x_in[b], 16)
                for b in range(B):
                    sp.wait_ge(combined, TOP * T * (b + 1))
                    sp.dma_start(out_v[:, b * T:(b + 1) * T, :], x_all[:, b * T:(b + 1) * T, :]).then_inc(out_done, 16)
                sp.wait_ge(out_done, 16 * B)


def kernel(x, ctx_1024, fside_Bx1xSxS2_0, L0_attn_Wq, L0_attn_Wk, L0_attn_Wv, L0_attn_q_gamma, L0_attn_q_beta,
           L0_attn_k_gamma, L0_attn_k_beta, L0_attn_Wo, L0_attn_bo, L0_xattn_Wq, L0_xattn_Wk, L0_xattn_Wv, L0_xattn_Wo,
           L0_ffn_gate_w, L0_ffn_gate_up_w, L0_ffn_down_w):
    import numpy as np
    import concourse.bacc as bacc
    from concourse.bass_utils import run_bass_kernel_spmd

    x = np.asarray(x)
    B, S, D = x.shape
    HD = D // 16
    as_np = lambda a: np.ascontiguousarray(np.asarray(a))
    theta = np.arange(S)[:, None] * np.exp(-np.arange(0, HD, 2) / HD * math.log(10000.0))[None, :]
    cos, sin = np.repeat(np.cos(theta), 2, axis=1), np.repeat(np.sin(theta), 2, axis=1)
    sin[:, :HD // 2] *= -1.0
    rope = np.stack([cos, sin]).astype(np.float32)
    wo1 = np.repeat(as_np(L0_attn_Wo).T.reshape(16, 1, HD, D), 2, axis=1)
    wq, wk = (as_np(w).T.reshape(D, 4, D // 4) for w in (L0_attn_Wq, L0_attn_Wk))
    wqk = np.stack([wq, wk], axis=2).reshape(D, 2 * D)
    arrays = {
        "x": x, "ctx_in": as_np(ctx_1024), "fside": as_np(fside_Bx1xSxS2_0),
        "wqkv": np.concatenate([wqk, as_np(L0_attn_Wv).T], axis=1),
        "head_affine": np.stack([as_np(a) for a in (L0_attn_q_gamma, L0_attn_k_gamma, L0_attn_q_beta, L0_attn_k_beta)]),
        "rope": rope, "wo1": wo1.reshape(-1, D), "bo": as_np(L0_attn_bo),
        "wq2": as_np(L0_xattn_Wq).T, "wk2": as_np(L0_xattn_Wk).T, "wv2": as_np(L0_xattn_Wv).T, "wo2": as_np(L0_xattn_Wo).T,
        "gate_w": as_np(L0_ffn_gate_w), "gate_up_w": as_np(L0_ffn_gate_up_w), "down_w": as_np(L0_ffn_down_w),
    }
    arrays = {f"in_{k}": np.ascontiguousarray(a) for k, a in arrays.items()}
    nc = bacc.Bacc("TRN2", target_bir_lowering=False, num_devices=1)
    args = [nc.dram_tensor(k, a.shape, mybir.dt.from_np(a.dtype), kind="ExternalInput").ap() for k, a in arrays.items()]
    args.append(nc.dram_tensor("out_dram", x.shape, F32, kind="ExternalOutput").ap())
    build(nc, *args)
    return run_bass_kernel_spmd(nc, [arrays], core_ids=[0]).results[0]["out_dram"]
```

```python
import math
from contextlib import ExitStack

import concourse.bass as bass
from concourse import mybir

F32 = mybir.dt.float32
F32R = mybir.dt.float32r
U32 = mybir.dt.uint32
I32 = mybir.dt.int32
ALU = mybir.AluOpType
ACT = mybir.ActivationFunctionType
AX = mybir.AxisListType

P = 128
EPS = 1e-5
BIG = 3.0e38
MASKED = -1.0e30
TOP = 2
RSQRT_BITS = float(0x5F3759DF)


def build(nc, x, ctx_in, fside, wqkv, head_affine, rope, wo1, bo, wq2, wk2, wv2, wo2, gate_w, gate_up_w, down_w, out):
    B, S, D = x.shape
    H = 16
    HD = D // H
    E2 = wq2.shape[1]
    HD2 = E2 // H
    T = S // P
    KD = D // P
    SLOT = 32
    GH = P // SLOT
    G1 = H // GH
    GH2 = P // HD2
    G2 = H // GH2
    NE, _, F2 = gate_up_w.shape
    F = F2 // 2
    FT = F // P
    NT = B * T
    SCALE1 = 1.0 / math.sqrt(HD)

    x_v = x.rearrange("b (t p) d -> b p t d", p=P)
    c_v = ctx_in.rearrange("b (t p) d -> b p t d", p=P)
    m_v = fside.rearrange("b o (t p) k -> b p (o t) k", p=P)
    out_b = out.rearrange("b (t p) d -> b p t d", p=P)
    out_v = out.rearrange("b (t p) d -> p (b t) d", p=P)
    TILES = (B * S * TOP + NE * (P - 1)) // P
    assert TILES % 2 == 1
    SPARE_TILES = TILES - B * S * TOP // P
    REGION = B * S + P
    SPARE = NE * REGION
    ROWS = SPARE + T * TOP * P
    assert T * TOP >= SPARE_TILES
    xs_dram = nc.dram_tensor("xs_dram", [ROWS, D], F32, kind="Internal").ap()
    ys_dram = nc.dram_tensor("ys_dram", [TILES * P, D], F32, kind="Internal").ap()

    with ExitStack() as ctx:
        def sb(name, shape, dt=F32):
            return ctx.enter_context(nc.sbuf_tensor(name, shape, dt))

        bank = ctx.enter_context(nc.psum_tensor("bank", [P, 8, 512], F32))

        share = sb("share", [P, NT, TOP])
        choice = sb("choice", [P, TOP, NT, NE])
        xs_row = sb("xs_row", [P, TOP, NT])
        next_row = sb("next_row", [P, NE])
        ident = sb("ident", [P, P])
        zeros = sb("zeros", [P, D])
        half_neg = sb("half_neg", [P, T])
        expert_no = sb("expert_no", [P, NE])
        ys_row = sb("ys_row", [P, TOP, NT], U32)
        region = sb("region", [P, NE])
        xn = sb("xn", [P, T, D])
        batch_slot = sb("batch_slot", [P, TOP, T], U32)

        scattered = ctx.enter_context(nc.semaphore("scattered"))

        def scatter(n):
            t, j = divmod(n, TOP)
            nc.gpsimd.indirect_dma_start(
                out=xs_dram, out_offset=bass.IndirectOffsetOnAxis(ap=batch_slot[:, j, t:t + 1], axis=0),
                in_=xn[:, t, :], in_offset=None).then_inc(scattered, 16)

        def f32(ap):
            return ap.bitcast(F32)

        with ExitStack() as att:
            def sa(name, shape, dt=F32):
                return att.enter_context(nc.sbuf_tensor(name, shape, dt))

            w_qkv = sa("w_qkv", [P, KD, 3 * D])
            w_o1 = sa("w_o1", [P, G1, D])
            w_q2 = sa("w_q2", [P, KD, E2])
            w_k2 = sa("w_k2", [P, KD, E2])
            w_v2 = sa("w_v2", [P, KD, E2])
            w_o2 = sa("w_o2", [P, G2, D])
            w_g = sa("w_g", [P, KD, NE])
            b_o = sa("b_o", [P, D])
            gcos = sa("gcos", [P, T, 2 * GH, HD])
            gsin = sa("gsin", [P, T, 2 * GH, HD])
            bsum = sa("bsum", [P, T, 2 * GH, HD])
            causal = sa("causal", [P, S + P])

            xb = sa("xb", [P, T, D])
            xa = sa("xa", [P, T, D])
            cb = xa
            mb = sa("mb", [P, T, S])
            xT = sa("xT", [P, KD, S])
            cT = sa("cT", [P, KD, S])
            xTa = sa("xTa", [P, KD, S])
            with nc.sbuf_tensor("qkv", [P, T, 3 * D], F32) as qkv:
                pass
            kHL = sa("kHL", [P, 6 * S], F32R)
            kH = kHL[:, 0:2 * GH2 * S].rearrange("p (r i s) -> p r i s", r=2, i=GH2)
            kL = kHL[:, 2 * GH2 * S:].rearrange("p (r s) -> p r s", r=2)
            stat = sa("stat", [P, T, 6])
            mv = sa("mv", [P, T, 2])
            rstd = sa("rstd", [P, T])
            o2T = sa("o2T", [P, G2, S])
            o1T = o2T[:, 0:G1, :]
            s_sb = sa("s_sb", [P, 3, S])
            p_sb = sa("p_sb", [P, 5, S])
            pH = sa("pH", [P, 2, T, S], F32R)
            pL = sa("pL", [P, 2, T, S], F32R)
            negmax = sa("negmax", [P, H * T])
            psum_row = sa("psum_row", [P, H * T])
            logit = sa("logit", [P, T, NE])
            top = sa("top", [P, T, 8])
            topi = sa("topi", [P, T, 8], U32)
            topf = sa("topf", [P, T, 8])
            ntop = sa("ntop", [P, T])
            ew = sa("ew", [P, T, TOP])
            esum = sa("esum", [P, T])
            chosen = sa("chosen", [P, TOP, T, NE])
            either = sa("either", [P, T, NE])
            rank = sa("rank", [P, T, NE])
            picked_row = sa("picked_row", [P, TOP, T, NE])
            slot_f = sa("slot_f", [P, TOP, T])
            before = sa("before", [P, P])
            ones = sa("ones", [P, P])

            with ExitStack() as shared:
                def sr(name, shape, dt=F32):
                    return shared.enter_context(nc.sbuf_tensor(name, shape, dt))
                v_pad = sr("v_pad", [P, T, H, SLOT], F32R)
                qkT = sr("qkT", [P, 2, 3, S], F32R)
                tok = sr("tok", [P, T, 3, GH, SLOT], F32R)
                rq = sr("rq", [P, T, 2 * GH, HD])
                cen = sr("cen", [P, T, 2 * GH, HD])
                tmp = sr("tmp", [P, T, 2 * GH, HD])
                hsum = sr("hsum", [P, T * 2 * GH])
                hvar = sr("hvar", [P, T * 2 * GH])
                hstd = sr("hstd", [P, T * 2 * GH])
            ROPE_SPACE = T * H * SLOT + 2 * 3 * S + T * GH * (3 * SLOT + 3 * 2 * HD + 3 * 2)

            loaded_later = att.enter_context(nc.semaphore("loaded_later"))
            with nc.semaphore("loaded") as loaded, nc.semaphore("pool_set") as pool_set, \
                    nc.semaphore("tab") as tab, \
                    nc.sbuf_tensor("affine", [P, 4, HD], F32) as affine, \
                    nc.sbuf_tensor("cs", [P, T, 2, HD], F32) as cs, \
                    nc.sbuf_tensor("btmp", [P, T, 2 * GH, HD], F32) as btmp, nc.Block() as block:
                LOADS = 6
                LATER_LOADS = 7

                @block.sync
                def _(sp):
                    for i in range(2):
                        sp.dma_start(affine[:, 2 * i:2 * i + 2, :].rearrange("p a d -> p (a d)"),
                                     head_affine[2 * i:2 * i + 2, :].rearrange("a d -> (a d)").partition_broadcast(P)
                                     ).then_inc(loaded, 16)
                    for i in range(2):
                        sp.dma_start(cs[:, :, i, :], rope[i].rearrange("(t p) d -> p t d", p=P)).then_inc(loaded, 16)
                    sp.dma_start(xa[:], x_v[0]).then_inc(loaded, 16)
                    sp.dma_start(w_qkv[:], wqkv.rearrange("(k p) n -> p k n", p=P)).then_inc(loaded, 16)
                    sp.dma_start(w_k2[:], wk2.rearrange("(k p) n -> p k n", p=P)).then_inc(loaded_later, 16)
                    sp.dma_start(w_v2[:], wv2.rearrange("(k p) n -> p k n", p=P)).then_inc(loaded_later, 16)
                    sp.dma_start(w_q2[:], wq2.rearrange("(k p) n -> p k n", p=P)).then_inc(loaded_later, 16)
                    sp.dma_start(w_o1[:], wo1.rearrange("(g p) n -> p g n", p=P)).then_inc(loaded_later, 16)
                    sp.dma_start(w_o2[:], wo2.rearrange("(g p) n -> p g n", p=P)).then_inc(loaded_later, 16)
                    sp.dma_start(w_g[:], gate_w.rearrange("(k p) n -> p k n", p=P)).then_inc(loaded_later, 16)
                    sp.dma_start(b_o[:], bo.partition_broadcast(P)).then_inc(loaded_later, 16)
                    sp.wait_ge(loaded, 16 * LOADS)

                @block.gpsimd
                def _(pool):
                    pool.memset(ident[:], 0.0).then_inc(pool_set, 1)
                    pool.memset(causal[:], 0.0).then_inc(pool_set, 1)
                    pool.memset(half_neg[:], -0.5).then_inc(pool_set, 1)
                    pool.iota(expert_no[:], [[1, NE]], base=0, channel_multiplier=0,
                              allow_small_or_imprecise_dtypes=True).then_inc(pool_set, 1)
                    pool.iota(region[:], [[REGION, NE]], base=0, channel_multiplier=0,
                              allow_small_or_imprecise_dtypes=True).then_inc(pool_set, 1)
                    pool.memset(before[:], 1.0).then_inc(pool_set, 1)
                    pool.memset(ones[:], 1.0).then_inc(pool_set, 1)
                    pool.memset(zeros[:], 0.0).then_inc(pool_set, 1)
                    pool.iota(next_row[:], [[REGION, NE]], base=0, channel_multiplier=0,
                              allow_small_or_imprecise_dtypes=True).then_inc(pool_set, 1)
                    pool.wait_ge(pool_set, 9)
                    pool.affine_select(out=before[:], in_=before[:], compare_op=ALU.is_gt, fill=0.0, base=0,
                                       pattern=[[1, P]], channel_multiplier=-1).then_inc(pool_set, 1)
                    pool.affine_select(out=ident[:], in_=ident[:], compare_op=ALU.not_equal, fill=1.0, base=0,
                                       pattern=[[-1, P]], channel_multiplier=1).then_inc(pool_set, 1)
                    pool.affine_select(out=causal[:], in_=causal[:], compare_op=ALU.is_ge, fill=MASKED, base=S,
                                       pattern=[[-1, S + P]], channel_multiplier=1).then_inc(pool_set, 1)
                    pool.memset(xn[:], 0.0).then_inc(pool_set, 1)
                    for n in range(T * TOP):
                        pool.iota(batch_slot[:, n % TOP, n // TOP:n // TOP + 1], [[0, 1]], base=SPARE + n * P,
                                  channel_multiplier=1).then_inc(pool_set, 1)
                    pool.wait_ge(pool_set, 13 + T * TOP)

                @block.vector
                def _(dve):
                    dve.wait_ge(loaded, 16 * LOADS)
                    HH = HD // 2
                    n = 0
                    for i in range(2 * GH):
                        a = i // GH
                        for (dst, src, rotated) in ((gcos, a, False), (gsin, a, True), (bsum, 2 + a, False),
                                                    (btmp, 2 + a, True)):
                            if not rotated:
                                nc.vector.tensor_tensor(dst[:, :, i, :], cs[:, :, 0, :],
                                                        affine[:, src:src + 1, :].to_broadcast([P, T, HD]),
                                                        ALU.mult).then_inc(tab, 1)
                                n += 1
                                continue
                            for half in range(2):
                                nc.vector.tensor_tensor(
                                    dst[:, :, i, half * HH:(half + 1) * HH], cs[:, :, 1, half * HH:(half + 1) * HH],
                                    affine[:, src:src + 1, 1 - half:HD:2].to_broadcast([P, T, HH]),
                                    ALU.mult).then_inc(tab, 1)
                                n += 1
                    dve.wait_ge(tab, n)
                    nc.vector.tensor_tensor(bsum[:], bsum[:], btmp[:], ALU.add).then_inc(tab, 1)
                    dve.wait_ge(tab, n + 1)
            nc.all_engine_barrier(sems_to_clear=range(loaded.num, tab.num + 1))

            def ln_stats(dve, src, wait_src, steps):
                for t in range(T):
                    wait_src(t)
                    nc.vector.bn_stats(stat[:, t, :], src[:, t, :]).then_inc(steps, 1)
                dve.wait_ge(steps, T)
                for t in range(T):
                    nc.vector.bn_aggr(mv[:, t, :], stat[:, t, :]).then_inc(steps, 1)
                dve.wait_ge(steps, 2 * T)
                nc.vector.tensor_scalar(rstd[:], mv[:, :, 1], EPS, None, ALU.add).then_inc(steps, 1)

            def ln_apply(dve, src, dst, root, done):
                dve.wait_ge(root, 1)
                for t in range(T):
                    nc.vector.tensor_scalar(dst[:, t, :], src[:, t, :], mv[:, t, 0:1], rstd[:, t:t + 1],
                                            ALU.subtract, ALU.mult).then_inc(done, 1)

            def ln_pool(pool, steps, root):
                pool.wait_ge(steps, 2 * T + 1)
                nc.gpsimd.tensor_tensor(rstd[:], rstd[:], half_neg[:, 0:T], ALU.pow).then_inc(root, 1)

            QKV_PARTS = ((0, 2 * D), (2 * D, 3 * D))
            QKV_ORDER = [(t, part) for part in QKV_PARTS for t in range(T)]

            HH = HD // 2
            NEWTON = [step + str(n) for n in range(3) for step in ("square", "times", "better")]
            PARTS = ["sum", "center", "squares", "squares_sum", "variance", "shift", "guess", "half", *NEWTON,
                     "scale", "sin0", "sin1", "cos", "add", "beta"]

            def lower(engine, a):
                side = slice(HD, 2 * HD) if a < 2 else slice(0, HD)
                high = slice(0, HD) if a < 2 else slice(HD, 2 * HD)
                return engine.tensor_tensor(tok[:, :, a, :, side], rq[:, :, min(a, 1) * GH:(min(a, 1) + 1) * GH, :],
                                            f32(tok[:, :, a, :, high]), ALU.subtract)

            def group(g):
                return qkv[:, :, 2 * GH * HD * g:2 * GH * HD * (g + 1)]

            def rope_step(dve, g, part, steps, before, split_low=None):
                k = PARTS.index(part)
                if before + k:
                    dve.wait_ge(steps, before + k)
                x4 = group(g).rearrange("p t (h d) -> p t h d", d=HD)
                flat = lambda a: a[:].rearrange("p t h d -> p (t h) d")
                wide = lambda a: a[:, :, None].to_broadcast([P, T * 2 * GH, HD])
                if part == "sum":
                    ins = nc.vector.tensor_reduce(hsum[:].rearrange("p (t h) -> p t h", t=T), x4, AX.X, ALU.add)
                elif part == "center":
                    ins = nc.vector.scalar_tensor_tensor(cen[:].rearrange("p t h d -> p t h d"), wide(hsum).rearrange(
                        "p (t h) d -> p t h d", t=T), -1.0 / HD, x4, ALU.mult, ALU.add)
                elif part == "squares":
                    ins = nc.vector.tensor_tensor(tmp[:], cen[:], cen[:], ALU.mult)
                elif part == "squares_sum":
                    ins = nc.vector.tensor_reduce(hvar[:], flat(tmp), AX.X, ALU.add)
                elif part == "variance":
                    ins = nc.vector.tensor_scalar(hvar[:], hvar[:], 1.0 / HD, EPS, ALU.mult, ALU.add)
                elif part == "shift":
                    ins = nc.vector.tensor_scalar(hstd[:].bitcast(I32), hvar[:].bitcast(I32), 1, None, ALU.logical_shift_right)
                elif part == "guess":
                    ins = nc.vector.tensor_scalar(hstd[:].bitcast(I32), hstd[:].bitcast(I32), -1.0, RSQRT_BITS, ALU.mult, ALU.add)
                elif part == "half":
                    ins = nc.vector.tensor_scalar(hvar[:], hvar[:], -0.5, None, ALU.mult)
                elif part.startswith("square"):
                    ins = nc.vector.tensor_tensor(hsum[:], hstd[:], hstd[:], ALU.mult)
                elif part.startswith("times"):
                    ins = nc.vector.tensor_tensor(hsum[:], hsum[:], hvar[:], ALU.mult)
                elif part.startswith("better"):
                    ins = nc.vector.scalar_tensor_tensor(hstd[:], hsum[:], 1.5, hstd[:], ALU.add, ALU.mult)
                elif part == "scale":
                    ins = nc.vector.tensor_tensor(flat(cen), flat(cen), wide(hstd), ALU.mult)
                elif part in ("sin0", "sin1"):
                    half = int(part[-1])
                    cols = slice(half * HH, (half + 1) * HH)
                    ins = nc.vector.tensor_tensor(flat(tmp)[:, :, cols], flat(cen)[:, :, 1 - half:HD:2],
                                                  flat(gsin)[:, :, cols], ALU.mult)
                elif part == "cos":
                    ins = nc.vector.tensor_tensor(cen[:], cen[:], gcos[:], ALU.mult)
                elif part == "add":
                    ins = nc.vector.tensor_tensor(cen[:], cen[:], tmp[:], ALU.add)
                else:
                    if g >= 2:
                        dve.wait_ge(split_low, 3 * (g - 1))
                    ins = nc.vector.tensor_tensor(rq[:], cen[:], bsum[:], ALU.add)
                ins.then_inc(steps, 1)

            def upper(act, a):
                if a == 0:
                    return nc.scalar.copy(tok[:, :, 0:2, :, 0:HD].rearrange("p t a h d -> p t (a h) d"), rq[:])
                return nc.scalar.copy(tok[:, :, 2, :, HD:2 * HD], rq[:, :, GH:2 * GH, :])

            FIRST_BANK = 3

            def first_upper(act, steps, done):
                act.wait_ge(steps, len(PARTS))
                for a in range(2):
                    upper(act, a).then_inc(done, 1)

            def first_lower(dve, ready, done):
                for a in range(3):
                    dve.wait_ge(ready, a // 2 + 1)
                    lower(nc.vector, a).then_inc(done, 1)

            def turn(out_bank, tiles):
                for t, tile in enumerate(tiles):
                    mm = nc.tensor.transpose(bank[:, out_bank, t * P:(t + 1) * P], tile, ident[:])
                return mm

            def tok_tiles(a):
                return [f32(tok[:, t, a, :, :].rearrange("p h d -> p (h d)")) for t in range(T)]

            def first_turn(pe, ready, done):
                for a in range(3):
                    pe.wait_ge(ready, a + 1)
                    turn(FIRST_BANK + a, tok_tiles(a)).then_inc(done, 1)

            def first_move(act, ready, done):
                for a in range(3):
                    act.wait_ge(ready, a + 1)
                    nc.scalar.copy(qkT[:, 0, a, :], bank[:, FIRST_BANK + a, :]).then_inc(done, 1)

            v_rows = qkv[:, :, 2 * D:3 * D].rearrange("p t (h d) -> p t h d", d=HD)

            def v_upper(act, ready, count, done):
                act.wait_ge(ready, count)
                nc.scalar.copy(v_pad[:, :, :, 0:HD], v_rows).then_inc(done, 1)

            def v_lower(pool, ready, done):
                pool.wait_ge(ready, 1)
                for t in range(T):
                    nc.gpsimd.tensor_tensor(v_pad[:, t, :, HD:2 * HD], v_rows[:, t], f32(v_pad[:, t, :, 0:HD]),
                                            ALU.subtract).then_inc(done, 1)

            with ExitStack() as stage:
                def sem(name):
                    return stage.enter_context(nc.semaphore(name))

                stage.enter_context(nc.sbuf_tensor("rope_space_p", [P, ROPE_SPACE], F32))
                xn0 = stage.enter_context(nc.sbuf_tensor("xn0", [P, T, D], F32))
                xT0 = stage.enter_context(nc.sbuf_tensor("xT0", [P, KD, S], F32))
                first, root, xn_ready, produced, evacuated = (
                    sem("p_steps"), sem("p_root"), sem("p_xn_ready"), sem("p_produced"), sem("p_evacuated"))
                steps = first
                rope_steps, split_high, split_low = sem("p_rope_steps"), sem("p_split_high"), sem("p_split_low")
                qk_turned, qk_moved, v_high, v_low = sem("p_qk_turned"), sem("p_qk_moved"), sem("p_v_high"), sem("p_v_low")
                block = stage.enter_context(nc.Block())

                @block.sync
                def _(sp):
                    sp.wait_ge(loaded_later, 16 * LATER_LOADS)

                @block.gpsimd
                def _(pool):
                    ln_pool(pool, steps, root)
                    v_lower(pool, v_high, v_low)

                @block.vector
                def _(dve):
                    ln_stats(dve, xa, lambda t: None, steps)
                    ln_apply(dve, xa, xn0, root, xn_ready)
                    dve.wait_ge(evacuated, KD + T)
                    for part in PARTS:
                        rope_step(dve, 0, part, rope_steps, 0)
                    first_lower(dve, split_high, split_low)

                @block.tensor
                def _(pe):
                    for k in range(KD):
                        for t in range(T):
                            if k == 0:
                                pe.wait_ge(xn_ready, t + 1)
                            mm = nc.tensor.transpose(bank[:, k, t * P:(t + 1) * P], xn0[:, t, k * P:(k + 1) * P], ident[:])
                        mm.then_inc(produced, 1)
                    pe.wait_ge(evacuated, KD)
                    for n, (t, (lo, hi)) in enumerate(QKV_ORDER):
                        if n >= 6:
                            pe.wait_ge(evacuated, KD + n - 5)
                        for k in range(KD):
                            mm = nc.tensor.matmul(bank[:, 2 + n % 6, 0:hi - lo], xT0[:, k, t * P:(t + 1) * P], w_qkv[:, k, lo:hi],
                                                  start=(k == 0), stop=(k == KD - 1))
                        mm.then_inc(produced, 1)
                    pe.wait_ge(evacuated, KD + 2 * T)
                    first_turn(pe, split_low, qk_turned)

                @block.scalar
                def _(act):
                    for k in range(KD):
                        act.wait_ge(produced, k + 1)
                        nc.scalar.copy(xT0[:, k, :], bank[:, k, :]).then_inc(evacuated, 1)
                    for n, (t, (lo, hi)) in enumerate(QKV_ORDER):
                        act.wait_ge(produced, KD + n + 1)
                        nc.scalar.copy(qkv[:, t, lo:hi], bank[:, 2 + n % 6, 0:hi - lo]).then_inc(evacuated, 1)
                    first_upper(act, rope_steps, split_high)
                    v_upper(act, evacuated, KD + 2 * T, v_high)
                    first_move(act, qk_turned, qk_moved)
            nc.all_engine_barrier(sems_to_clear=range(first.num, v_low.num + 1))

            TURN_LAG, HIGH_LAG, LOW_LAG, VALUES_LAG = 4, 3, 5, 10
            VALUE_STEPS = 2
            TILE_ORDER = (0, 3, 1, 2)
            U = H * T
            S_BANK, T_BANK, O_BANK, J_BANK = 0, 2, 5, 7
            NPS = 5


            def unit(u):
                return u // T, TILE_ORDER[u % T]

            def values_at(i):
                h, k = divmod(i - VALUES_LAG, T)
                each = T // VALUE_STEPS
                return [(h, k * each + n) for n in range(each)] if 0 <= h < H and k < VALUE_STEPS else []

            def head_out(i, after):
                h, k = divmod(i - VALUES_LAG - VALUE_STEPS + 1 - after, T)
                return h if 0 <= h < H and k == 0 else None

            STEPS = U - T + VALUES_LAG + VALUE_STEPS

            class Soft:

                def __init__(self, sem, keys, mask, scale):
                    self.keys, self.mask, self.scale = keys, mask, scale
                    self.scored = sem("scored")
                    self.masked = sem("masked")
                    self.exped = sem("exped")
                    self.inverted = sem("inverted")
                    self.normed = sem("normed")
                    self.turned = sem("turned")
                    self.high = sem("high")
                    self.low = sem("low")
                    self.valued = sem("valued")

                def mask_scores(self, dve, u):
                    dve.wait_ge(self.scored, u + 1)
                    if u >= 3:
                        dve.wait_ge(self.exped, u - 2)
                    n = self.keys(u)
                    nc.vector.tensor_tensor_reduce(s_sb[:, u % 3, 0:n], bank[:, S_BANK + u % 2, 0:n], self.mask(u), -self.scale,
                                                   BIG, ALU.add, ALU.min, negmax[:, u:u + 1]).then_inc(self.masked, 1)

                def exp(self, act, u):
                    act.wait_ge(self.masked, u + 1)
                    if u >= NPS:
                        act.wait_ge(self.turned, u - NPS + 1)
                    n = self.keys(u)
                    nc.scalar.activation(p_sb[:, u % NPS, 0:n], s_sb[:, u % 3, 0:n], ACT.Exp, bias=negmax[:, u:u + 1],
                                         scale=-1.0, accum_out=psum_row[:, u:u + 1]).then_inc(self.exped, 1)

                def invert(self, dve, u):
                    dve.wait_ge(self.exped, u + 1)
                    nc.vector.reciprocal(psum_row[:, u:u + 1], psum_row[:, u:u + 1]).then_inc(self.inverted, 1)

                def norm(self, pool, u):
                    pool.wait_ge(self.inverted, u + 1)
                    n = self.keys(u)
                    nc.gpsimd.tensor_scalar(p_sb[:, u % NPS, 0:n], p_sb[:, u % NPS, 0:n], psum_row[:, u:u + 1], 1.0,
                                            ALU.mult, ALU.mult).then_inc(self.normed, 1)

                def turn(self, pe, u):
                    pe.wait_ge(self.normed, u + 1)
                    if u >= 3:
                        pe.wait_ge(self.low, u - 2)
                    for kt in range(self.keys(u) // P):
                        mm = nc.tensor.transpose(bank[:, T_BANK + u % 3, kt * P:(kt + 1) * P],
                                                 p_sb[:, u % NPS, kt * P:(kt + 1) * P], ident[:])
                    mm.then_inc(self.turned, 1)

                def halves(self, u, dst):
                    h, t = unit(u)
                    n = self.keys(u) // P
                    return (dst[:, h % 2, 0:n, t * P:(t + 1) * P],
                            bank[:, T_BANK + u % 3, 0:n * P].rearrange("p (k q) -> p k q", k=n))

                def move_high(self, act, u):
                    act.wait_ge(self.turned, u + 1)
                    if u >= 2 * T:
                        act.wait_ge(self.valued, (u // T - 1) * T)
                    dst, src = self.halves(u, pH)
                    nc.scalar.copy(dst, src).then_inc(self.high, 1)

                def move_low(self, dve, u):
                    dve.wait_ge(self.high, u + 1)
                    dst, src = self.halves(u, pL)
                    nc.vector.tensor_tensor(dst, src, f32(self.halves(u, pH)[0]), ALU.subtract).then_inc(self.low, 1)

                def values(self, pe, h, kt, stationary, rows, first_key_only):
                    if kt == 0:
                        pe.wait_ge(self.low, (h + 1) * T)
                    lo = kt * P if first_key_only else 0
                    for part in (pH, pL):
                        mm = nc.tensor.matmul(bank[0:rows, O_BANK + h % 2, lo:S], stationary, part[:, h % 2, kt, lo:S],
                                              start=(kt == 0 and part is pH), stop=(kt == T - 1 and part is pL))
                    mm.then_inc(self.valued, 1)

            def self_attention():
                with ExitStack() as stage:
                    def sem(name):
                        return stage.enter_context(nc.semaphore("s_" + name))

                    def ss(name, shape, dt=F32):
                        return stage.enter_context(nc.sbuf_tensor(name, shape, dt))

                    ss("rope_space_s", [P, ROPE_SPACE])

                    first = c_in = sem("c_in")
                    m_in, rope_steps = sem("m_in"), sem("rope_steps")
                    split_high, split_low, qk_turned, qk_moved = sem("split_high"), sem("split_low"), sem("qk_turned"), sem("qk_moved")
                    soft = Soft(sem, lambda u: (unit(u)[1] + 1) * P,
                                lambda u: causal[:, S - unit(u)[1] * P:S + P], SCALE1)
                    biased, stored = sem("biased"), sem("stored")
                    c_turned, c_moved, k_made = sem("c_turned"), sem("c_moved"), sem("k_made")
                    k_is_high, k_is_low, k_is_twice = sem("k_high"), sem("k_low"), sem("k_twice")
                    last = k_is_twice
                    block = stage.enter_context(nc.Block())
                    UG = GH * T
                    ROPE_UP_TO = {0: "sum", 1: "center", 2: "squares", 3: "guess", 4: "times1", 5: "better2", 6: "scale",
                                  7: "sin1", 8: "cos", 9: "beta"}
                    SPLIT_AT, TURN_AT = 10, 12
                    BIAS_AT = 4
                    C_AT = {U - 16: 0, U - 12: 1}
                    K_AT = U - 8
                    SCATTER_AT = {g * UG + 4 * n + 2: g * 2 + n for g in range(G1) for n in range(2)}

                    @block.sync
                    def _(sp):
                        one = bass.ds(b, 1)
                        sp.dma_start(mb[:], m_v[one].rearrange("a p t d -> p (a t) d")).then_inc(m_in, 16)
                        sp.wait_ge(biased, T)
                        sp.dma_start(cb[:], c_v[one].rearrange("a p t d -> p (a t) d")).then_inc(c_in, 16)
                        sp.wait_ge(c_in, 16)
                        sp.wait_ge(m_in, 16)
                        sp.wait_ge(k_is_high, 2)
                        k_twice(sp, 0, k_is_twice)
                        sp.wait_ge(k_is_twice, 32)

                    @block.vector
                    def _(dve):
                        done = 0
                        for i in range(U + LOW_LAG):
                            if i < U:
                                soft.mask_scores(dve, i)
                            if 1 <= i <= U:
                                soft.invert(dve, i - 1)
                            if i >= LOW_LAG:
                                soft.move_low(dve, i - LOW_LAG)
                            g, k = divmod(i, UG)
                            if g < G1 - 1:
                                end = PARTS.index(ROPE_UP_TO[k]) + 1 if k in ROPE_UP_TO else done
                                for part in PARTS[done:end]:
                                    rope_step(dve, g + 1, part, rope_steps, len(PARTS) * g, split_low)
                                done = end % len(PARTS)
                            if i == K_AT + KD + 1:
                                dve.wait_ge(k_is_high, 2)
                                k_low(0, k_is_low)

                    @block.gpsimd
                    def _(pool):
                        for i in range(U + 1):
                            if i >= 1:
                                soft.norm(pool, i - 1)
                            if BIAS_AT <= i < BIAS_AT + T:
                                t = i - BIAS_AT
                                nc.gpsimd.tensor_tensor(xb[:, t, :], xa[:, t, :], b_o[:], ALU.add).then_inc(biased, 1)
                            g, k = divmod(i, UG)
                            if g < G1 - 1:
                                a = k - SPLIT_AT
                                if 0 <= a < 3:
                                    pool.wait_ge(split_high, 2 * g + a // 2 + 1)
                                    lower(nc.gpsimd, a).then_inc(split_low, 1)
                            if i in SCATTER_AT:
                                scatter(SCATTER_AT[i])

                    @block.scalar
                    def _(act):
                        def split_upper(g):
                            act.wait_ge(rope_steps, len(PARTS) * g)
                            if g >= 2:
                                act.wait_ge(qk_turned, 3 * (g - 1))
                            for a in range(2):
                                upper(act, a).then_inc(split_high, 1)

                        def move_qk(g, a):
                            act.wait_ge(qk_turned, 3 * (g - 1) + a + 1)
                            if g >= 2:
                                act.wait_ge(soft.scored, UG * (g - 1))
                            nc.scalar.copy(qkT[:, g % 2, a, :], bank[:, J_BANK, :]).then_inc(qk_moved, 1)

                        def store(h):
                            g, i = divmod(h, GH)
                            act.wait_ge(soft.valued, T * (h + 1))
                            nc.scalar.copy(o1T[SLOT * i:SLOT * (i + 1), g, :], bank[0:SLOT, O_BANK + h % 2, :]).then_inc(stored, 1)

                        for i in range(STEPS + 1):
                            if i < U:
                                soft.exp(act, i)
                            g, k = divmod(i, UG)
                            if g < G1 - 1:
                                if k == SPLIT_AT:
                                    split_upper(g + 1)
                                if TURN_AT <= k < TURN_AT + 3:
                                    move_qk(g + 1, k - TURN_AT)
                            if HIGH_LAG <= i < U + HIGH_LAG:
                                soft.move_high(act, i - HIGH_LAG)
                            if i - 1 in C_AT:
                                k = C_AT[i - 1]
                                act.wait_ge(c_turned, k + 1)
                                nc.scalar.copy(cT[:, k, :], bank[:, J_BANK, :]).then_inc(c_moved, 1)
                            if i == K_AT + KD:
                                act.wait_ge(k_made, KD)
                                k_high(0, k_is_high)
                            if head_out(i, 1) is not None:
                                store(head_out(i, 1))

                    @block.tensor
                    def _(pe):
                        def turn_qk(g, a):
                            pe.wait_ge(split_low, 3 * (g - 1) + a + 1)
                            if g >= 2 or a:
                                pe.wait_ge(qk_moved, 3 * (g - 1) + a)
                            turn(J_BANK, tok_tiles(a)).then_inc(qk_turned, 1)

                        def scores(u):
                            h, t = unit(u)
                            g, i = divmod(h, GH)
                            if u % UG == 0 and g:
                                pe.wait_ge(qk_moved, 3 * g)
                            if u >= 2:
                                pe.wait_ge(soft.masked, u - 1)
                            part = slice(SLOT * i, SLOT * (i + 1))
                            n = max(soft.keys(u), 2 * P)
                            for k in (1, 2):
                                mm = nc.tensor.matmul(bank[:, S_BANK + u % 2, 0:n], qkT[part, g % 2, 0, t * P:(t + 1) * P],
                                                      qkT[part, g % 2, k, 0:n], start=(k == 1), stop=(k == 2))
                            mm.then_inc(soft.scored, 1)

                        for i in range(STEPS):
                            if i < U:
                                scores(i)
                            if TURN_LAG <= i < U + TURN_LAG:
                                soft.turn(pe, i - TURN_LAG)
                            for h, kt in values_at(i):
                                if kt == 0 and h >= 2:
                                    pe.wait_ge(stored, h - 1)
                                soft.values(pe, h, kt, v_pad[:, kt, h, :], SLOT, True)
                            g, k = divmod(i, UG)
                            if g < G1 - 1 and TURN_AT <= k < TURN_AT + 3:
                                turn_qk(g + 1, k - TURN_AT)
                            if i in C_AT:
                                k = C_AT[i]
                                if k:
                                    pe.wait_ge(c_moved, k)
                                else:
                                    pe.wait_ge(qk_moved, 3 * (G1 - 1))
                                    pe.wait_ge(c_in, 16)
                                turn(J_BANK, [cb[:, t, k * P:(k + 1) * P] for t in range(T)]).then_inc(c_turned, 1)
                            if K_AT <= i < K_AT + KD:
                                pe.wait_ge(c_moved, KD)
                                project_pair(w_k2, cT, 0, [i - K_AT]).then_inc(k_made, 1)
                nc.all_engine_barrier(sems_to_clear=range(first.num, last.num + 1))

            def project_qkv(to, n):
                t, (lo, hi) = QKV_ORDER[n]
                for k in range(KD):
                    mm = nc.tensor.matmul(bank[:, to, 0:hi - lo], xTa[:, k, t * P:(t + 1) * P], w_qkv[:, k, lo:hi],
                                          start=(k == 0), stop=(k == KD - 1))
                return mm

            def move_qkv(at, n):
                t, (lo, hi) = QKV_ORDER[n]
                return nc.scalar.copy(qkv[:, t, lo:hi], bank[:, at, 0:hi - lo])

            def project_pair(w, src, j, ks=range(KD)):
                for k in ks:
                    mm = nc.tensor.matmul(bank[:, J_BANK, :], w[:, k, j * P:(j + 1) * P], src[:, k, :],
                                          start=(k == 0), stop=(k == KD - 1))
                return mm

            LOWER, UPPER = slice(0, P // 2), slice(P // 2, P)

            def k_high(j, done):
                for i, part in enumerate((LOWER, UPPER)):
                    nc.scalar.copy(kH[part, j % 2, i, :], bank[part, J_BANK, :]).then_inc(done, 1)

            def k_low(j, done):
                for i, part in enumerate((LOWER, UPPER)):
                    nc.vector.tensor_tensor(kL[part, j % 2, :], bank[part, J_BANK, :], f32(kH[part, j % 2, i, :]),
                                            ALU.subtract).then_inc(done, 1)

            def k_twice(sp, j, done):
                for i, (src, dst) in enumerate(((LOWER, UPPER), (UPPER, LOWER))):
                    sp.dma_start(f32(kH[dst, j % 2, i, :]), f32(kH[src, j % 2, i, :])).then_inc(done, 16)

            def middle(v2s):
                with ExitStack() as stage:
                    def sem(name):
                        return stage.enter_context(nc.semaphore("m_" + name))

                    first = projected = sem("projected")
                    added, steps, root, xn_ready = sem("added"), sem("steps"), sem("root"), sem("xn_ready")
                    turned, v_made, v_high, v_low = sem("turned"), sem("v_made"), sem("v_high"), sem("v_low")
                    x_in, steps_a, root_a, xna_ready = sem("x_in"), sem("steps_a"), sem("root_a"), sem("xna_ready")
                    last = xna_ready
                    xna = o2T[:, G1:2 * G1, :].rearrange("p g s -> p (g s)")[:, 0:T * D].rearrange("p (t d) -> p t d", d=D)
                    block = stage.enter_context(nc.Block())
                    V_BANK, V_RING = 4, 4
                    VJ = 2 * T

                    @block.sync
                    def _(sp):
                        sp.dma_start(xa[:], x_v[bass.ds(b_next, 1)].rearrange("a p t d -> p (a t) d")).then_inc(x_in, 16)
                        sp.wait_ge(x_in, 16)

                    @block.gpsimd
                    def _(pool):
                        ln_pool(pool, steps, root)
                        ln_pool(pool, steps_a, root_a)

                    @block.tensor
                    def _(pe):
                        for t in range(T):
                            for g in range(G1):
                                mm = nc.tensor.matmul(bank[:, t, 0:D], o1T[:, g, t * P:(t + 1) * P], w_o1[:, g, :],
                                                      start=(g == 0), stop=(g == G1 - 1))
                            mm.then_inc(projected, 1)
                        for n in range(VJ):
                            t, half = divmod(n, 2)
                            if n >= V_RING:
                                pe.wait_ge(v_low, n - V_RING + 1)
                            for k in range(KD):
                                mm = nc.tensor.matmul(bank[:, V_BANK + n % V_RING, :], cT[:, k, t * P:(t + 1) * P],
                                                      w_v2[:, k, half * 512:(half + 1) * 512], start=(k == 0), stop=(k == KD - 1))
                            mm.then_inc(v_made, 1)
                        pe.wait_ge(v_low, VJ - 2)
                        for first_bank, src, ready in ((V_BANK, xn, xn_ready), (V_BANK - 2, xna, xna_ready)):
                            for k in range(KD):
                                pe.wait_ge(ready, T)
                                turn(first_bank + k, [src[:, t, k * P:(k + 1) * P] for t in range(T)]).then_inc(turned, 1)

                    def v_half(n, side):
                        t, half = divmod(n, 2)
                        heads = H // 2
                        return v2s[:, t, half * heads:(half + 1) * heads, side * HD2:(side + 1) * HD2]

                    @block.scalar
                    def _(act):
                        for n in range(VJ):
                            act.wait_ge(v_made, n + 1)
                            nc.scalar.copy(v_half(n, 0), bank[:, V_BANK + n % V_RING, :].rearrange("p (h d) -> p h d", d=HD2)).then_inc(v_high, 1)
                        for k in range(KD):
                            act.wait_ge(turned, k + 1)
                            nc.scalar.copy(xT[:, k, :], bank[:, V_BANK + k, :])
                        for k in range(KD):
                            act.wait_ge(turned, KD + k + 1)
                            nc.scalar.copy(xTa[:, k, :], bank[:, V_BANK - 2 + k, :])

                    @block.vector
                    def _(dve):
                        def v2_lower(n):
                            dve.wait_ge(v_high, n + 1)
                            nc.vector.tensor_tensor(v_half(n, 1), bank[:, V_BANK + n % V_RING, :].rearrange("p (h d) -> p h d", d=HD2),
                                                    f32(v_half(n, 0)), ALU.subtract).then_inc(v_low, 1)

                        for t in range(T):
                            dve.wait_ge(projected, t + 1)
                            nc.vector.tensor_tensor(xb[:, t, :], bank[:, t, 0:D], xb[:, t, :], ALU.add).then_inc(added, 1)
                        v2_lower(0)
                        ln_stats(dve, xb, lambda t: dve.wait_ge(added, t + 1), steps)
                        v2_lower(1)
                        dve.wait_ge(scattered, 16 * T * TOP * b + 16 * T * TOP)
                        ln_apply(dve, xb, xn, root, xn_ready)
                        v2_lower(2)
                        v2_lower(3)
                        dve.wait_ge(xn_ready, T)
                        ln_stats(dve, xa, lambda t: dve.wait_ge(x_in, 16), steps_a)
                        v2_lower(4)
                        ln_apply(dve, xa, xna, root_a, xna_ready)
                        for n in range(5, VJ):
                            v2_lower(n)
                nc.all_engine_barrier(sems_to_clear=range(first.num, last.num + 1))

            def cross_attention(v2s):
                with ExitStack() as stage:
                    def sem(name):
                        return stage.enter_context(nc.semaphore("c_" + name))

                    def ss(name, shape, dt=F32):
                        return stage.enter_context(nc.sbuf_tensor(name, shape, dt))

                    qS = ss("qS", [P, 2, 2, S], F32R)
                    out_low = ss("out_low", [P // 2, S])

                    first = q_made = sem("q_made")
                    q_high, q_low, qkv_made, qkv_moved = sem("q_high"), sem("q_low"), sem("qkv_made"), sem("qkv_moved")
                    k_made, k_is_high, k_is_low = sem("k_made"), sem("k_high"), sem("k_low")
                    k_is_twice = [sem("k_twice0"), sem("k_twice1")]
                    soft = Soft(sem, lambda u: S, lambda u: mb[:, unit(u)[1], :], 1.0)
                    low_out, stored = sem("low_out"), sem("stored")
                    last = stored
                    block = stage.enter_context(nc.Block())
                    UG = GH2 * T
                    K_AT, Q_AT = 0, UG // 2
                    K_END, Q_END = K_AT + KD - 1, Q_AT + KD - 1
                    QK_AT = {U: 0, U + 1: 1, STEPS - 1: 2, STEPS: 3}
                    QK_BANK = (J_BANK, S_BANK, S_BANK + 1)

                    @block.sync
                    def _(sp):
                        for j in range(1, G2):
                            sp.wait_ge(k_is_high, 2 * j)
                            k_twice(sp, j, k_is_twice[j % 2])

                    @block.tensor
                    def _(pe):
                        def scores(u):
                            h, t = unit(u)
                            j, i = divmod(h, GH2)
                            if u % UG == 0:
                                pe.wait_ge(q_low, 2 * (j + 1))
                                if j:
                                    pe.wait_ge(k_is_low, 2 * j)
                                    pe.wait_ge(k_is_twice[j % 2], 32 * ((j + 1) // 2))
                            if u >= 2:
                                pe.wait_ge(soft.masked, u - 1)
                            mine = (LOWER, UPPER)[i]
                            dst = bank[:, S_BANK + u % 2, :]
                            q = qS[:, j % 2, i, t * P:(t + 1) * P]
                            nc.tensor.matmul(dst, q, kH[:, j % 2, i, :], start=True, stop=False)
                            nc.tensor.matmul(dst, q[mine], kL[mine, j % 2, :], start=False, stop=True).then_inc(soft.scored, 1)

                        project_pair(w_q2, xT, 0).then_inc(q_made, 1)
                        for i in range(STEPS + 1):
                            if i < U:
                                scores(i)
                            if TURN_LAG <= i < U + TURN_LAG:
                                soft.turn(pe, i - TURN_LAG)
                            j, k = divmod(i, UG)
                            if j < G2 - 1 and K_AT <= k <= K_END:
                                if k == K_AT and j:
                                    pe.wait_ge(q_low, 2 * (j + 1))
                                mm = project_pair(w_k2, cT, j + 1, [k - K_AT])
                                if k == K_END:
                                    mm.then_inc(k_made, 1)
                            if j < G2 - 1 and Q_AT <= k <= Q_END:
                                if k == Q_AT:
                                    pe.wait_ge(k_is_low, 2 * (j + 1))
                                mm = project_pair(w_q2, xT, j + 1, [k - Q_AT])
                                if k == Q_END:
                                    mm.then_inc(q_made, 1)
                            for h, kt in values_at(i):
                                if kt == 0 and h >= 2:
                                    pe.wait_ge(stored, h - 1)
                                soft.values(pe, h, kt, v2s[:, kt, h, :], P, False)
                            if i in QK_AT:
                                n = QK_AT[i]
                                if n in (1, 2):
                                    pe.wait_ge(soft.masked, U - 2 + n)
                                if n == 3:
                                    pe.wait_ge(qkv_moved, 1)
                                project_qkv(QK_BANK[n % 3], n).then_inc(qkv_made, 1)

                    @block.scalar
                    def _(act):
                        def q_upper(j):
                            act.wait_ge(q_made, j + 1)
                            if j >= 2:
                                act.wait_ge(soft.scored, UG * (j - 1))
                            for i, part in enumerate((LOWER, UPPER)):
                                nc.scalar.copy(qS[part, j % 2, i, :], bank[part, J_BANK, :]).then_inc(q_high, 1)

                        def k_upper(j):
                            act.wait_ge(k_made, j)
                            if j >= 2:
                                act.wait_ge(soft.scored, UG * (j - 1))
                            k_high(j, k_is_high)

                        def lower_out(h):
                            act.wait_ge(soft.valued, T * (h + 1))
                            if h:
                                act.wait_ge(stored, h)
                            nc.scalar.copy(out_low[:], bank[UPPER, O_BANK + h % 2, :]).then_inc(low_out, 1)

                        q_upper(0)
                        for i in range(STEPS + 2):
                            if i < U:
                                soft.exp(act, i)
                            if HIGH_LAG <= i < U + HIGH_LAG:
                                soft.move_high(act, i - HIGH_LAG)
                            j, k = divmod(i, UG)
                            if j < G2 - 1 and k == K_END:
                                k_upper(j + 1)
                            if j < G2 - 1 and k == Q_END:
                                q_upper(j + 1)
                            if head_out(i, 1) is not None:
                                lower_out(head_out(i, 1))
                            if i - 1 in QK_AT:
                                n = QK_AT[i - 1]
                                act.wait_ge(qkv_made, n + 1)
                                move_qkv(QK_BANK[n % 3], n).then_inc(qkv_moved, 1)

                    @block.vector
                    def _(dve):
                        def q_lower(j):
                            for i, (src, dst) in enumerate(((LOWER, UPPER), (UPPER, LOWER))):
                                dve.wait_ge(q_high, 2 * j + i + 1)
                                nc.vector.tensor_tensor(qS[dst, j % 2, i, :], bank[src, J_BANK, :], f32(qS[src, j % 2, i, :]),
                                                        ALU.subtract).then_inc(q_low, 1)

                        def k_lower(j):
                            dve.wait_ge(k_is_high, 2 * j)
                            k_low(j, k_is_low)

                        def store(h):
                            dve.wait_ge(low_out, h + 1)
                            nc.vector.tensor_tensor(o2T[(LOWER, UPPER)[h % 2], h // 2, :], bank[LOWER, O_BANK + h % 2, :],
                                                    out_low[:], ALU.add).then_inc(stored, 1)

                        q_lower(0)
                        for i in range(STEPS + 2):
                            if i < U:
                                soft.mask_scores(dve, i)
                            if 1 <= i <= U:
                                soft.invert(dve, i - 1)
                            if LOW_LAG <= i < U + LOW_LAG:
                                soft.move_low(dve, i - LOW_LAG)
                            j, k = divmod(i, UG)
                            if j < G2 - 1 and k == K_END + 1:
                                k_lower(j + 1)
                            if j < G2 - 1 and k == Q_END + 1:
                                q_lower(j + 1)
                            if head_out(i, 2) is not None:
                                store(head_out(i, 2))

                    @block.gpsimd
                    def _(pool):
                        for u in range(U):
                            soft.norm(pool, u)
                nc.all_engine_barrier(sems_to_clear=range(first.num, last.num + 1))

            def route():
                with ExitStack() as stage:
                    def sem(name):
                        return stage.enter_context(nc.semaphore("r_" + name))

                    stage.enter_context(nc.sbuf_tensor("rope_space_r", [P, ROPE_SPACE], F32))
                    first = projected = sem("projected")
                    added, steps, root, xn_ready = sem("added"), sem("steps"), sem("root"), sem("xn_ready")
                    turned, moved, logits, picked, shifted_ready, exped = (sem("turned"), sem("moved"), sem("logits"),
                                                                           sem("picked"), sem("shifted"), sem("exped"))
                    v_made, v_moved, v_high, v_low = sem("v_made"), sem("v_moved"), sem("v_high"), sem("v_low")
                    chosen_ready, ranked, slotted, saved = sem("chosen"), sem("ranked"), sem("slotted"), sem("saved")
                    rope_steps, split_high, split_low = sem("rope_steps"), sem("split_high"), sem("split_low")
                    qk_turned, qk_moved = sem("qk_turned"), sem("qk_moved")
                    last = qk_moved
                    block = stage.enter_context(nc.Block())
                    ADD_AFTER = [PARTS.index("guess"), PARTS.index("sin1")]
                    O2_BANK, V_BANK, XN_BANK = (0, 1, 2, 0), 6, 1
                    ROUTER_BANK, RANK_BANK, TOTAL_BANK = 0, 6, 7

                    @block.sync
                    def _(sp):
                        sp.wait_ge(added, T)
                        sp.dma_start(out_b[bass.ds(b, 1)].rearrange("a p t d -> p (a t) d"), xb[:]).then_inc(saved, 16)
                        sp.wait_ge(saved, 16)

                    @block.gpsimd
                    def _(pool):
                        ln_pool(pool, steps, root)
                        v_lower(pool, v_high, v_low)

                    @block.tensor
                    def _(pe):
                        for t in range(T):
                            if t == T - 1:
                                pe.wait_ge(added, 1)
                            for j in range(G2):
                                mm = nc.tensor.matmul(bank[:, O2_BANK[t], 0:D], o2T[:, j, t * P:(t + 1) * P], w_o2[:, j, :],
                                                      start=(j == 0), stop=(j == G2 - 1))
                            mm.then_inc(projected, 1)
                        for n in range(T):
                            if n >= 2:
                                pe.wait_ge(v_moved, n - 1)
                            project_qkv(V_BANK + n % 2, T + n).then_inc(v_made, 1)
                        first_turn(pe, split_low, qk_turned)
                        for k in range(KD):
                            pe.wait_ge(xn_ready, T)
                            turn(XN_BANK + k, [xn[:, t, k * P:(k + 1) * P] for t in range(T)]).then_inc(turned, 1)
                        pe.wait_ge(moved, KD)
                        for t in range(T):
                            for k in range(KD):
                                mm = nc.tensor.matmul(bank[:, ROUTER_BANK, t * NE:(t + 1) * NE], xT[:, k, t * P:(t + 1) * P],
                                                      w_g[:, k, :], start=(k == 0), stop=(k == KD - 1))
                        mm.then_inc(logits, 1)
                        pe.wait_ge(chosen_ready, 1)
                        flat = either[:].rearrange("p t e -> p (t e)")
                        nc.tensor.matmul(bank[:, RANK_BANK, 0:T * NE], before[:], flat, start=True, stop=True)
                        nc.tensor.matmul(bank[:, TOTAL_BANK, 0:T * NE], ones[:], flat, start=True, stop=True).then_inc(ranked, 1)

                    @block.scalar
                    def _(act):
                        first_upper(act, rope_steps, split_high)
                        for n in range(T):
                            act.wait_ge(v_made, n + 1)
                            move_qkv(V_BANK + n % 2, T + n).then_inc(v_moved, 1)
                        first_move(act, qk_turned, qk_moved)
                        for k in range(KD):
                            act.wait_ge(turned, k + 1)
                            nc.scalar.copy(xT[:, k, :], bank[:, XN_BANK + k, :]).then_inc(moved, 1)
                        v_upper(act, v_moved, T, v_high)
                        act.wait_ge(shifted_ready, 1)
                        for t in range(T):
                            nc.scalar.activation(ew[:, t, :], top[:, t, 0:TOP], ACT.Exp, bias=ntop[:, t:t + 1], scale=1.0
                                                 ).then_inc(exped, 1)

                    @block.vector
                    def _(dve):
                        def add(t):
                            dve.wait_ge(projected, t + 1)
                            nc.vector.tensor_tensor(xb[:, t, :], bank[:, O2_BANK[t], 0:D], xb[:, t, :], ALU.add).then_inc(added, 1)

                        for n, part in enumerate(PARTS):
                            rope_step(dve, 0, part, rope_steps, 0)
                            if n in ADD_AFTER:
                                add(ADD_AFTER.index(n))
                        first_lower(dve, split_high, split_low)
                        for t in range(len(ADD_AFTER), T):
                            add(t)
                        ln_stats(dve, xb, lambda t: dve.wait_ge(added, t + 1), steps)
                        ln_apply(dve, xb, xn, root, xn_ready)
                        n = 0

                        def step(*instructions):
                            nonlocal n
                            n += len(instructions)
                            for ins in instructions:
                                ins.then_inc(picked, 1)
                            dve.wait_ge(picked, n)

                        tiles = lambda a: a.rearrange("p (t e) -> p t e", t=T)
                        dve.wait_ge(logits, 1)
                        step(nc.vector.tensor_copy(logit[:], tiles(bank[:, ROUTER_BANK, 0:T * NE])))
                        step(*[nc.vector.max(top[:, t, :], logit[:, t, :]) for t in range(T)])
                        nc.vector.tensor_scalar(ntop[:], top[:, :, 0], -1.0, None, ALU.mult).then_inc(shifted_ready, 1)
                        step(*[nc.vector.max_index(topi[:, t, :], top[:, t, :], logit[:, t, :]) for t in range(T)])
                        step(nc.vector.tensor_copy(topf[:], topi[:]))
                        step(*[nc.vector.tensor_tensor(chosen[:, j], expert_no[:, None, :].to_broadcast([P, T, NE]),
                                                       topf[:, :, j:j + 1].to_broadcast([P, T, NE]), ALU.is_equal)
                               for j in range(TOP)])
                        nc.vector.tensor_tensor(either[:], chosen[:, 0], chosen[:, 1], ALU.add).then_inc(chosen_ready, 1)
                        dve.wait_ge(exped, T)
                        step(nc.vector.tensor_tensor(esum[:], ew[:, :, 0], ew[:, :, 1], ALU.add))
                        step(nc.vector.reciprocal(esum[:], esum[:]))
                        nc.vector.tensor_tensor(share[:, bass.ds(b * T, T), :], ew[:], esum[:, :, None].to_broadcast([P, T, TOP]),
                                                ALU.mult)
                        for j in range(TOP):
                            nc.vector.tensor_copy(choice[:, j, bass.ds(b * T, T), :], chosen[:, j])
                        dve.wait_ge(ranked, 1)
                        step(nc.vector.tensor_copy(rank[:, 0, :], next_row[:]))
                        for t in range(T):
                            step(nc.vector.tensor_tensor(rank[:, t + 1, :] if t + 1 < T else next_row[:],
                                                         tiles(bank[:, TOTAL_BANK, 0:T * NE])[:, t], rank[:, t, :], ALU.add))
                        step(nc.vector.tensor_tensor(rank[:], tiles(bank[:, RANK_BANK, 0:T * NE]), rank[:], ALU.add))
                        step(*[nc.vector.tensor_tensor(picked_row[:, j], chosen[:, j], rank[:], ALU.mult) for j in range(TOP)])
                        step(*[nc.vector.tensor_reduce(slot_f[:, j, :], picked_row[:, j], AX.X, ALU.add) for j in range(TOP)])
                        nc.vector.tensor_copy(batch_slot[:], slot_f[:]).then_inc(slotted, 1)
                        nc.vector.tensor_copy(xs_row[:, :, bass.ds(b * T, T)], slot_f[:])
                nc.all_engine_barrier(sems_to_clear=range(first.num, last.num + 1))

            with nc.Fori(0, B) as b:
                b_next = (b + 1) % B
                self_attention()
                with ExitStack() as cross:
                    v2s = cross.enter_context(nc.sbuf_tensor("v2s", [P, T, H, 2 * HD2], F32R))
                    middle(v2s)
                    cross_attention(v2s)
                route()

        with ExitStack() as moe:
            def sm(name, shape, dt=F32):
                return moe.enter_context(nc.sbuf_tensor(name, shape, dt))

            w_raw = sm("w_raw", [P, 2, KD, F2])
            w_guH = sm("w_guH", [P, NE * KD, F2], F32R)
            w_guL = sm("w_guL", [P, NE * KD, F2], F32R)
            w_dn = sm("w_dn", [P, NE * FT, D])
            used = sm("used", [P, NE])
            pad_row = sm("pad_row", [P, NE], U32)
            tiles_f = sm("tiles_f", [P, NE])
            tiles_i = sm("tiles_i", [P, NE], U32)
            ends = sm("ends", [P, NE])
            tile_no = sm("tile_no", [P, TILES])
            past = sm("past", [P, TILES, NE])
            skipped = sm("skipped", [P, TILES, NE])
            t_expert = sm("t_expert", [P, TILES])
            t_start = sm("t_start", [P, TILES])
            t_row = sm("t_row", [P, TILES])
            expert_of = sm("expert_of", [P, TILES], U32)
            row_of = sm("row_of", [P, TILES], U32)
            shift = sm("shift", [P, NE])
            shifted = sm("shifted", [P, NT, NE])
            ys_row_f = sm("ys_row_f", [P, TOP, NT])
            xs = sm("xs", [P, 2, D])
            xsH = sm("xsH", [P, 2, KD * P], F32R)
            xsL = sm("xsL", [P, 2, KD * P], F32R)
            sil = sm("sil", [P, 2, F])
            hid = sm("hid", [P, 2, F])
            hidT = sm("hidT", [P, 2, F])
            ys = sm("ys", [P, 2, D])

            with ExitStack() as sems:
                def sem(name):
                    return sems.enter_context(nc.semaphore(name))

                w0_in, w0_high, w_steps, w_ready = sem("w0_in"), sem("w0_high"), sem("w_steps"), sem("w_ready")
                w_in = [sem("w_in0"), sem("w_in1")]
                pad_ready, padded = sem("pad_ready"), sem("padded")
                map_steps, map_ready, no_set = sem("map_steps"), sem("map_ready"), sem("no_set")
                loaded = [sem("loaded0"), sem("loaded1")]
                stored = [sem("stored0"), sem("stored1")]
                turned, xs_high, xs_low, gated, upped = sem("e_turned"), sem("xs_high"), sem("xs_low"), sem("gated"), sem("upped")
                silued, hidden, h_turned, hidT_ready = sem("silued"), sem("hidden"), sem("h_turned"), sem("hidT_ready")
                downed, ys_ready = sem("downed"), sem("ys_ready")
                block = sems.enter_context(nc.Block())
                XT_BANK, GATE_BANK, UP_BANK, HT_BANK, DOWN_BANK = 0, 1, 3, 5, 6
                PAIRS = TILES // 2

                def raw(e):
                    return ((w_raw[:, e % 2], gate_up_w[e].rearrange("(k p) f -> p k f", p=P)),
                            (w_dn[:, e * FT:(e + 1) * FT], down_w[e].rearrange("(k p) f -> p k f", p=P)))

                def upper(engine, e):
                    return engine(w_guH[:, e * KD:(e + 1) * KD, :], w_raw[:, e % 2])

                def lower(engine, e):
                    return engine.tensor_tensor(w_guL[:, e * KD:(e + 1) * KD, :], w_raw[:, e % 2],
                                                f32(w_guH[:, e * KD:(e + 1) * KD, :]), ALU.subtract)

                @block.sync
                def _(sp):
                    for dst, src in raw(0):
                        sp.dma_start(dst, src).then_inc(w0_in, 16)
                    sp.wait_ge(pad_ready, 1)
                    for e in range(NE):
                        row = sp.value_load(pad_row[0:1, e:e + 1], min_val=0, max_val=SPARE - P)
                        sp.dma_start(xs_dram[bass.ds(row, P), :], zeros[:]).then_inc(padded, 16)
                    sp.wait_ge(padded, 16 * NE)
                    sp.wait_ge(scattered, 16 * T * TOP * (B + 1))
                    sp.wait_ge(map_ready, 1)

                    def load(i, q):
                        row = sp.value_load(row_of[0:1, bass.ds(i, 1)], min_val=0, max_val=ROWS - P)
                        sp.dma_start(xs[:, q, :], xs_dram[bass.ds(row, P), :]).then_inc(loaded[q], 16)

                    def load_next(it, more=True):
                        for q in range(2 if more else 1):
                            sp.wait_ge(turned, 2 * it + q + 1)
                            load(2 * it + q + 2, q)

                    def store(it, more=True):
                        for q in range(2 if more else 1):
                            sp.wait_ge(ys_ready, 2 * it + q + 3)
                            sp.dma_start(ys_dram[bass.ds((2 * it + q) * P, P), :], ys[:, q, :]).then_inc(stored[q], 16)

                    load(0, 0)
                    load(1, 1)
                    for q in range(2):
                        sp.sem_inc(stored[q], 16)
                    load_next(0)
                    with sp.Fori(1, PAIRS - 1) as it:
                        load_next(it)
                        store(it - 1)
                    load_next(PAIRS - 1, more=False)
                    store(PAIRS - 2)
                    store(PAIRS - 1)
                    store(PAIRS, more=False)
                    for q in range(2):
                        sp.wait_ge(stored[q], 16 * (PAIRS + 2 - q))

                @block.gpsimd
                def _(pool):
                    pool.iota(tile_no[:], [[1, TILES]], base=0, channel_multiplier=0,
                              allow_small_or_imprecise_dtypes=True).then_inc(no_set, 1)
                    for n in range(T * TOP):
                        scatter(n)

                    def fetch(e):
                        for dst, src in raw(e):
                            pool.dma_start(dst, src).then_inc(w_in[e % 2], 16)

                    pool.wait_ge(turned, 1)
                    fetch(1)
                    pool.wait_ge(w_ready, 1)
                    for e in range(1, NE):
                        if e + 1 < NE:
                            fetch(e + 1)
                        pool.wait_ge(w_in[e % 2], 16 * 2 * ((e + 1) // 2))
                        upper(nc.gpsimd.tensor_copy, e).then_inc(w_steps, 1)
                        pool.wait_ge(w_steps, 2 * e - 1)
                        lower(nc.gpsimd, e).then_inc(w_steps, 1)
                        pool.wait_ge(w_steps, 2 * e)
                        pool.sem_inc(w_ready, 1)

                @block.tensor
                def _(pe):
                    def turn(i, q):
                        pe.wait_ge(loaded[q], 16 * i)
                        for k in range(KD):
                            mm = nc.tensor.transpose(bank[:, XT_BANK, k * P:(k + 1) * P], xs[:, q, k * P:(k + 1) * P], ident[:])
                        mm.then_inc(turned, 1)

                    def expert(i):
                        return pe.value_load(expert_of[0:1, bass.ds(i, 1)], min_val=0, max_val=NE - 1)

                    def widen(q, e, first_bank, column, done):
                        products = [(x, w, k) for k in range(KD) for x, w in ((xsH, w_guH), (xsH, w_guL), (xsL, w_guH))]
                        for n, (x, w, k) in enumerate(products):
                            mm = nc.tensor.matmul(bank[:, first_bank + q, :], x[:, q, k * P:(k + 1) * P],
                                                  w[:, bass.ds(e * KD + k, 1), column:column + F].rearrange("p a f -> p (a f)"),
                                                  start=(n == 0), stop=(n == len(products) - 1))
                        mm.then_inc(done, 1)

                    def turn_hidden(i, q):
                        pe.wait_ge(hidden, i + 2)
                        for f in range(FT):
                            mm = nc.tensor.transpose(bank[:, HT_BANK, f * P:(f + 1) * P], hid[:, q, f * P:(f + 1) * P], ident[:])
                        mm.then_inc(h_turned, 1)

                    def down(i, q, e):
                        pe.wait_ge(hidT_ready, i + 1)
                        pe.wait_ge(ys_ready, i + 1)
                        for f in range(FT):
                            mm = nc.tensor.matmul(bank[:, DOWN_BANK + q, 0:D], hidT[:, q, f * P:(f + 1) * P],
                                                  w_dn[:, bass.ds(e * FT + f, 1), :].rearrange("p a d -> p (a d)"),
                                                  start=(f == 0), stop=(f == FT - 1))
                        mm.then_inc(downed, 1)

                    pe.wait_ge(map_ready, 1)
                    turn(1, 0)
                    pe.wait_ge(xs_low, 1)
                    e = expert(0)
                    pe.wait_ge(w_ready, e + 1)
                    widen(0, e, GATE_BANK, 0, gated)
                    turn(1, 1)
                    widen(0, e, UP_BANK, F, upped)

                    def tile_step(it, j, last=False):
                        i = 2 * it + j
                        q, r = j, 1 - j
                        e, e_next = expert(i), expert(i + 1)
                        pe.wait_ge(xs_low, i + 2)
                        pe.wait_ge(w_ready, e_next + 1)
                        widen(r, e_next, GATE_BANK, 0, gated)
                        turn_hidden(i, q)
                        if not last:
                            turn(it + 2, q)
                        widen(r, e_next, UP_BANK, F, upped)
                        down(i, q, e)

                    with pe.Fori(0, PAIRS - 1) as it:
                        tile_step(it, 0)
                        tile_step(it, 1)
                    tile_step(PAIRS - 1, 0)
                    tile_step(PAIRS - 1, 1, last=True)
                    turn_hidden(TILES - 1, 0)
                    down(TILES - 1, 0, expert(TILES - 1))

                @block.scalar
                def _(act):
                    def move_x(i, q):
                        act.wait_ge(turned, i + 1)
                        nc.scalar.copy(xsH[:, q, :], bank[:, XT_BANK, 0:KD * P]).then_inc(xs_high, 1)

                    def silu(i, q):
                        act.wait_ge(gated, i + 1)
                        act.wait_ge(hidden, i)
                        nc.scalar.activation(sil[:, q, :], bank[:, GATE_BANK + q, :], ACT.Silu).then_inc(silued, 1)

                    def move_y(it, j):
                        act.wait_ge(downed, 2 * it + j + 1)
                        act.wait_ge(stored[j], 16 * it + 16)
                        nc.scalar.copy(ys[:, j, :], bank[:, DOWN_BANK + j, 0:D]).then_inc(ys_ready, 1)

                    act.wait_ge(w0_in, 32)
                    upper(nc.scalar.copy, 0).then_inc(w0_high, 1)
                    act.sem_inc(ys_ready, 2)
                    move_x(0, 0)
                    act.wait_ge(gated, 1)
                    nc.scalar.activation(sil[:, 0, :], bank[:, GATE_BANK, :], ACT.Silu).then_inc(silued, 1)
                    move_x(1, 1)
                    with act.Fori(0, PAIRS - 1) as it:
                        for j in range(2):
                            silu(2 * it + j + 1, 1 - j)
                            move_x(2 * it + j + 2, j)
                            move_y(it, j)
                    silu(TILES - 2, 1)
                    move_x(TILES - 1, 0)
                    move_y(PAIRS - 1, 0)
                    silu(TILES - 1, 0)
                    move_y(PAIRS - 1, 1)
                    move_y(PAIRS, 0)

                @block.vector
                def _(dve):
                    n = 0

                    def step(ins):
                        nonlocal n
                        n += 1
                        ins.then_inc(map_steps, 1)
                        dve.wait_ge(map_steps, n)

                    nc.vector.tensor_copy(pad_row[:], next_row[:]).then_inc(pad_ready, 1)
                    step(nc.vector.tensor_tensor(used[:], next_row[:], region[:], ALU.subtract))
                    LOG_P = P.bit_length() - 1
                    step(nc.vector.tensor_scalar(tiles_f[:], used[:], float(P - 1), None, ALU.add))
                    step(nc.vector.tensor_copy(tiles_i[:], tiles_f[:]))
                    step(nc.vector.tensor_scalar(tiles_i[:], tiles_i[:], LOG_P, None, ALU.logical_shift_right))
                    step(nc.vector.tensor_copy(tiles_f[:], tiles_i[:]))
                    step(nc.vector.tensor_copy(ends[:], tiles_f[:]))
                    for e in range(1, NE):
                        step(nc.vector.tensor_tensor(ends[:, e:e + 1], ends[:, e:e + 1], ends[:, e - 1:e], ALU.add))
                    dve.wait_ge(no_set, 1)
                    shape = [P, TILES, NE]
                    step(nc.vector.tensor_tensor(past[:], tile_no[:, :, None].to_broadcast(shape), ends[:, None, :].to_broadcast(shape),
                                                 ALU.is_ge))
                    step(nc.vector.tensor_reduce(t_expert[:], past[:], AX.X, ALU.add))
                    step(nc.vector.tensor_tensor(skipped[:], past[:], tiles_f[:, None, :].to_broadcast(shape), ALU.mult))
                    step(nc.vector.tensor_reduce(t_start[:], skipped[:], AX.X, ALU.add))
                    step(nc.vector.tensor_tensor(t_row[:], tile_no[:], t_start[:], ALU.subtract))
                    step(nc.vector.tensor_scalar(t_row[:], t_row[:], float(P), None, ALU.mult))
                    step(nc.vector.scalar_tensor_tensor(t_row[:], t_expert[:], float(REGION), t_row[:], ALU.mult, ALU.add))
                    step(nc.vector.tensor_scalar(t_expert[:], t_expert[:], float(NE - 1), None, ALU.min))
                    step(nc.vector.tensor_copy(expert_of[:], t_expert[:]))
                    step(nc.vector.tensor_copy(row_of[:], t_row[:]))
                    dve.sem_inc(map_ready, 1)
                    dve.sem_inc(hidden, 1)

                    def multiply(i, q):
                        dve.wait_ge(silued, i + 1)
                        dve.wait_ge(upped, i + 1)
                        nc.vector.tensor_tensor(hid[:, q, :], bank[:, UP_BANK + q, :], sil[:, q, :], ALU.mult).then_inc(hidden, 1)

                    def move_hidden(i, q):
                        dve.wait_ge(h_turned, i + 1)
                        nc.vector.tensor_copy(hidT[:, q, :], bank[:, HT_BANK, :]).then_inc(hidT_ready, 1)

                    def x_lower(i, q):
                        dve.wait_ge(xs_high, i + 1)
                        nc.vector.tensor_tensor(xsL[:, q, :], bank[:, XT_BANK, 0:KD * P], f32(xsH[:, q, :]), ALU.subtract
                                                ).then_inc(xs_low, 1)

                    dve.wait_ge(w0_high, 1)
                    lower(nc.vector, 0).then_inc(w_ready, 1)
                    x_lower(0, 0)
                    x_lower(1, 1)
                    multiply(0, 0)
                    with dve.Fori(0, PAIRS - 1) as it:
                        for j in range(2):
                            move_hidden(2 * it + j, j)
                            x_lower(2 * it + j + 2, j)
                            multiply(2 * it + j + 1, 1 - j)
                    move_hidden(TILES - 3, 0)
                    x_lower(TILES - 1, 0)
                    multiply(TILES - 2, 1)
                    move_hidden(TILES - 2, 1)
                    multiply(TILES - 1, 0)
                    move_hidden(TILES - 1, 0)

                    step(nc.vector.tensor_tensor(shift[:], ends[:], tiles_f[:], ALU.subtract))
                    step(nc.vector.tensor_scalar(shift[:], shift[:], float(P), None, ALU.mult))
                    step(nc.vector.scalar_tensor_tensor(shift[:], expert_no[:], -float(REGION), shift[:], ALU.mult, ALU.add))
                    for j in range(TOP):
                        step(nc.vector.tensor_tensor(shifted[:], choice[:, j], shift[:, None, :].to_broadcast([P, NT, NE]), ALU.mult))
                        step(nc.vector.tensor_reduce(ys_row_f[:, j, :], shifted[:], AX.X, ALU.add))
                        step(nc.vector.tensor_tensor(ys_row_f[:, j, :], ys_row_f[:, j, :], xs_row[:, j, :], ALU.add))
                    nc.vector.tensor_copy(ys_row[:], ys_row_f[:])

            nc.all_engine_barrier()

        RING = 4
        with ExitStack() as sems:
            def sem(name):
                return sems.enter_context(nc.semaphore(name))

            x_all = sems.enter_context(nc.sbuf_tensor("x_all", [P, NT, D], F32))
            yg = sems.enter_context(nc.sbuf_tensor("yg", [P, RING, TOP, D], F32))
            x_in = [sem(f"x_in{b}") for b in range(B)]

            gathered = [sem(f"gathered{i}") for i in range(RING)]
            combined, out_done = sem("combined"), sem("out_done")
            block = sems.enter_context(nc.Block())

            @block.gpsimd
            def _(pool):
                for t in range(NT):
                    if t >= RING:
                        pool.wait_ge(combined, TOP * (t - RING + 1))
                    for j in range(TOP):
                        pool.indirect_dma_start(
                            out=yg[:, t % RING, j, :], out_offset=None, in_=ys_dram,
                            in_offset=bass.IndirectOffsetOnAxis(ap=ys_row[:, j, t:t + 1], axis=0)).then_inc(gathered[t % RING], 16)

            @block.vector
            def _(dve):
                for t in range(NT):
                    if t % T == 0:
                        dve.wait_ge(x_in[t // T], 16)
                    dve.wait_ge(gathered[t % RING], 16 * TOP * (t // RING + 1))
                    for j in range(TOP):
                        if j:
                            dve.wait_ge(combined, TOP * t + j)
                        nc.vector.scalar_tensor_tensor(x_all[:, t, :], yg[:, t % RING, j, :], share[:, t, j:j + 1],
                                                       x_all[:, t, :], ALU.mult, ALU.add).then_inc(combined, 1)

            @block.sync
            def _(sp):
                for b in range(B):
                    sp.dma_start(x_all[:, b * T:(b + 1) * T, :], out_v[:, b * T:(b + 1) * T, :]).then_inc(x_in[b], 16)
                for b in range(B):
                    sp.wait_ge(combined, TOP * T * (b + 1))
                    sp.dma_start(out_v[:, b * T:(b + 1) * T, :], x_all[:, b * T:(b + 1) * T, :]).then_inc(out_done, 16)
                sp.wait_ge(out_done, 16 * B)


def kernel(x, ctx_1024, fside_Bx1xSxS2_0, L0_attn_Wq, L0_attn_Wk, L0_attn_Wv, L0_attn_q_gamma, L0_attn_q_beta,
           L0_attn_k_gamma, L0_attn_k_beta, L0_attn_Wo, L0_attn_bo, L0_xattn_Wq, L0_xattn_Wk, L0_xattn_Wv, L0_xattn_Wo,
           L0_ffn_gate_w, L0_ffn_gate_up_w, L0_ffn_down_w):
    import numpy as np
    import concourse.bacc as bacc
    from concourse.bass_utils import run_bass_kernel_spmd

    x = np.asarray(x)
    B, S, D = x.shape
    HD = D // 16
    as_np = lambda a: np.ascontiguousarray(np.asarray(a))
    theta = np.arange(S)[:, None] * np.exp(-np.arange(0, HD, 2) / HD * math.log(10000.0))[None, :]
    cos, sin = np.repeat(np.cos(theta), 2, axis=1), np.repeat(np.sin(theta), 2, axis=1)
    sin[:, :HD // 2] *= -1.0
    rope = np.stack([cos, sin]).astype(np.float32)
    wo1 = np.repeat(as_np(L0_attn_Wo).T.reshape(16, 1, HD, D), 2, axis=1)
    wq, wk = (as_np(w).T.reshape(D, 4, D // 4) for w in (L0_attn_Wq, L0_attn_Wk))
    wqk = np.stack([wq, wk], axis=2).reshape(D, 2 * D)
    arrays = {
        "x": x, "ctx_in": as_np(ctx_1024), "fside": as_np(fside_Bx1xSxS2_0),
        "wqkv": np.concatenate([wqk, as_np(L0_attn_Wv).T], axis=1),
        "head_affine": np.stack([as_np(a) for a in (L0_attn_q_gamma, L0_attn_k_gamma, L0_attn_q_beta, L0_attn_k_beta)]),
        "rope": rope, "wo1": wo1.reshape(-1, D), "bo": as_np(L0_attn_bo),
        "wq2": as_np(L0_xattn_Wq).T, "wk2": as_np(L0_xattn_Wk).T, "wv2": as_np(L0_xattn_Wv).T, "wo2": as_np(L0_xattn_Wo).T,
        "gate_w": as_np(L0_ffn_gate_w), "gate_up_w": as_np(L0_ffn_gate_up_w), "down_w": as_np(L0_ffn_down_w),
    }
    arrays = {f"in_{k}": np.ascontiguousarray(a) for k, a in arrays.items()}
    nc = bacc.Bacc("TRN2", target_bir_lowering=False, num_devices=1)
    args = [nc.dram_tensor(k, a.shape, mybir.dt.from_np(a.dtype), kind="ExternalInput").ap() for k, a in arrays.items()]
    args.append(nc.dram_tensor("out_dram", x.shape, F32, kind="ExternalOutput").ap())
    build(nc, *args)
    return run_bass_kernel_spmd(nc, [arrays], core_ids=[0]).results[0]["out_dram"]
```
